# Optimizing a Trainium2 kernel written in Bass

```python
import numpy as np
import jax
import jax.numpy as jnp

def _softmax(x, axis=-1):
    return jax.nn.softmax(x, axis=axis)

def _gelu(x):
    return jax.nn.gelu(x, approximate=True)

def _silu(x):
    return jax.nn.silu(x)

def _sigmoid(x):
    return jax.nn.sigmoid(x)

def _layernorm(x, axis=-1, eps=1e-05):
    m = jnp.mean(x, axis=axis, keepdims=True)
    v = jnp.var(x, axis=axis, keepdims=True)
    return (x - m) / jnp.sqrt(v + eps)

def _scatter_add(tgt, idx, src, axis=0):
    return tgt.at[idx].add(src)

def _segment_sum(src, seg, n):
    return jax.ops.segment_sum(src, seg, n)
kernel_name = 'mk_metaformer_d2_conv_nhwc256_r2_dd046b'

def setup_inputs(seed: int=0):
    np.random.seed(seed)
    _w = jnp.asarray

    def _rec_inputs():
        import jax
        import jax.numpy as jnp
        _gk = jax.random.key(seed)
        x = -0.0003929 + 0.9999 * jax.random.normal(jax.random.fold_in(_gk, 1), (4, 64, 64, 128), jnp.float32)
        return x
    x = _rec_inputs()

    def _L0_conv_setup():
        import jax, jax.numpy as jnp
        import numpy as np
        NUM_HEADS = 8
        BLOCK = 8
        HALO = 2

        def _rel_to_abs(rel):
            B, G, qh, qw, dim = rel.shape
            p = (dim + 1) // 2
            gap = p - qw
            flat = rel.reshape(B, G, qh, qw * dim)[:, :, :, qw - 1:-1]
            return flat.reshape(B, G, qh, qw, 2 * (p - 1))[:, :, :, :, gap:p + gap]

        def _relative_logits(pos_q, pos_emb_h, pos_emb_w):
            rel_w = _rel_to_abs(jnp.einsum('bghwd,dr->bghwr', pos_q, pos_emb_w))
            q_t = pos_q.transpose(0, 1, 3, 2, 4)
            rel_h = _rel_to_abs(jnp.einsum('bgwhd,dr->bgwhr', q_t, pos_emb_h))
            rel_h = rel_h.transpose(0, 1, 3, 2, 4)
            return rel_h[..., :, None] + rel_w[..., None, :]
        key = jax.random.key(seed)
        ks = jax.random.split(key, 6)
        B, H, W, C = (4, 64, 64, 128)
        out_ch = 128
        kd = C // NUM_HEADS
        kvk = BLOCK + 2 * HALO
        std = kd ** (-0.5)
        return {'x': jax.random.normal(ks[0], (B, H, W, C), jnp.float32), 'w_q': jax.random.normal(ks[1], (C, C), jnp.float32) * 0.02, 'w_kv': jax.random.normal(ks[2], (C, C + out_ch), jnp.float32) * 0.02, 'w_out': jax.random.normal(ks[3], (C, out_ch), jnp.float32) * 0.02, 'pos_emb_h': jax.random.normal(ks[4], (kd, 2 * kvk - 1), jnp.float32) * std, 'pos_emb_w': jax.random.normal(ks[5], (kd, 2 * kvk - 1), jnp.float32) * std}
    _L0_conv_all = _L0_conv_setup()
    _L0_conv_in = {k: v for k, v in _L0_conv_all.items() if k in ('w_q', 'w_kv', 'w_out', 'pos_emb_h', 'pos_emb_w')}
    del _L0_conv_all

    def _L0_ffn_setup():
        import jax, jax.numpy as jnp
        import numpy as np
        B, S, D = (8, 2048, 128)
        H = 4 * D
        CAPACITY = 0.5
        key = jax.random.key(seed)
        ks = jax.random.split(key, 6)
        x = jax.random.normal(ks[0], (B, S, D), dtype=jnp.float32)
        attention_mask = jnp.zeros((B, 1, 1, S), dtype=jnp.float32)
        wr = jax.random.normal(ks[1], (D, 1), dtype=jnp.float32) * 0.02
        br = jnp.zeros((1,), dtype=jnp.float32)
        w1 = jax.random.normal(ks[2], (D, H), dtype=jnp.float32) * 0.02
        b1 = jnp.zeros((H,), dtype=jnp.float32)
        w2 = jax.random.normal(ks[3], (H, D), dtype=jnp.float32) * 0.02
        b2 = jnp.zeros((D,), dtype=jnp.float32)
        return {'x': x, 'attention_mask': attention_mask, 'wr': wr, 'br': br, 'w1': w1, 'b1': b1, 'w2': w2, 'b2': b2}
    _L0_ffn_all = _L0_ffn_setup()
    _L0_ffn_in = {k: v for k, v in _L0_ffn_all.items() if k in ('attention_mask', 'wr', 'br', 'w1', 'b1', 'w2', 'b2')}
    del _L0_ffn_all

    def _L1_conv_setup():
        import jax, jax.numpy as jnp
        import numpy as np
        KERNEL = 3
        DILATIONS = (2, 3)
        NUM_HEADS = 8

        def _unfold_windows(t, k, dil):
            B, C, H, W = t.shape
            pad = dil * (k - 1) // 2
            tp = jnp.pad(t, ((0, 0), (0, 0), (pad, pad), (pad, pad)))
            ws = [tp[:, :, i * dil:i * dil + H, j * dil:j * dil + W] for i in range(k) for j in range(k)]
            return jnp.stack(ws, axis=2)

        def _dilate_attention(q, k_, v, kernel, dil, head_dim):
            B, d, H, W = q.shape
            nh = d // head_dim
            scale = head_dim ** (-0.5)
            qh = q.reshape(B, nh, head_dim, H, W)
            kw = _unfold_windows(k_, kernel, dil).reshape(B, nh, head_dim, kernel * kernel, H, W)
            vw = _unfold_windows(v, kernel, dil).reshape(B, nh, head_dim, kernel * kernel, H, W)
            attn = jax.nn.softmax(jnp.einsum('bndhw,bndkhw->bnkhw', qh, kw) * scale, axis=2)
            out = jnp.einsum('bnkhw,bndkhw->bndhw', attn, vw)
            return out.transpose(0, 3, 4, 1, 2).reshape(B, H, W, d)
        key = jax.random.key(seed)
        k1, k2, k3, k4 = jax.random.split(key, 4)
        B, H, W, C = (4, 64, 64, 128)
        x = jax.random.normal(k1, (B, H, W, C), dtype=jnp.float32)
        Wqkv = jax.random.normal(k2, (3 * C, C), dtype=jnp.float32) * C ** (-0.5)
        Wproj = jax.random.normal(k3, (C, C), dtype=jnp.float32) * C ** (-0.5)
        bproj = jnp.zeros((C,), dtype=jnp.float32)
        return {'x': x, 'Wqkv': Wqkv, 'Wproj': Wproj, 'bproj': bproj}
    _L1_conv_all = _L1_conv_setup()
    _L1_conv_in = {k: v for k, v in _L1_conv_all.items() if k in ('Wqkv', 'Wproj', 'bproj')}
    del _L1_conv_all

    def _L1_ffn_setup():
        import jax, jax.numpy as jnp
        import numpy as np
        B, N, D = (16, 2048, 128)
        NUM_EXPERTS, TOP_K, HEADS = (4, 2, 4)
        N_EDGES = 524288
        LN_EPS = 1e-05

        def _layernorm(x, g, b):
            mu = x.mean(-1, keepdims=True)
            var = ((x - mu) ** 2).mean(-1, keepdims=True)
            return (x - mu) * jax.lax.rsqrt(var + LN_EPS) * g + b

        def _forward(x, edge_index, W_gat, att_src, att_dst, b_gat, ln_gamma, ln_beta, W1, b1, W2, b2):
            Bc, Nc, Dc = x.shape
            M = Bc * Nc
            x_flat = x.reshape(M, Dc)
            h = (x_flat @ W_gat).reshape(M, HEADS, NUM_EXPERTS)
            loops = jnp.arange(M, dtype=edge_index.dtype)
            src = jnp.concatenate([edge_index[0], loops])
            dst = jnp.concatenate([edge_index[1], loops])
            a_src = (h * att_src).sum(-1)
            a_dst = (h * att_dst).sum(-1)
            e = jax.nn.leaky_relu(a_src[src] + a_dst[dst], negative_slope=0.2)
            e_max = jax.ops.segment_max(e, dst, num_segments=M)
            ee = jnp.exp(e - e_max[dst])
            denom = jax.ops.segment_sum(ee, dst, num_segments=M)
            alpha = ee / (denom[dst] + 1e-16)
            msg = h[src] * alpha[:, :, None]
            agg = jax.ops.segment_sum(msg, dst, num_segments=M).reshape(M, HEADS * NUM_EXPERTS) + b_gat
            scores = _layernorm(agg, ln_gamma, ln_beta).reshape(M, HEADS, NUM_EXPERTS).mean(1)
            scores = scores.reshape(Bc, Nc, NUM_EXPERTS)
            topk_s, topk_i = jax.lax.top_k(scores, TOP_K)
            w = jax.nn.softmax(topk_s, axis=-1)
            out = jnp.zeros_like(x)
            for ei in range(NUM_EXPERTS):
                g = jnp.where(topk_i == ei, w, 0.0).sum(-1)
                hh = jax.nn.gelu(x @ W1[ei] + b1[ei], approximate=False)
                out = out + g[..., None] * (hh @ W2[ei] + b2[ei])
            return out
        key = jax.random.key(seed)
        ks = jax.random.split(key, 8)
        s = 0.05
        return {'x': jax.random.normal(ks[0], (B, N, D), jnp.float32), 'W_gat': jax.random.normal(ks[1], (D, HEADS * NUM_EXPERTS), jnp.float32) * s, 'att_src': jax.random.normal(ks[2], (HEADS, NUM_EXPERTS), jnp.float32) * s, 'att_dst': jax.random.normal(ks[3], (HEADS, NUM_EXPERTS), jnp.float32) * s, 'b_gat': jnp.zeros((HEADS * NUM_EXPERTS,), jnp.float32), 'ln_gamma': jnp.ones((HEADS * NUM_EXPERTS,), jnp.float32), 'ln_beta': jnp.zeros((HEADS * NUM_EXPERTS,), jnp.float32), 'W1': jax.random.normal(ks[4], (NUM_EXPERTS, D, 2 * D), jnp.float32) * s, 'b1': jnp.zeros((NUM_EXPERTS, 2 * D), jnp.float32), 'W2': jax.random.normal(ks[5], (NUM_EXPERTS, 2 * D, D), jnp.float32) * s, 'b2': jnp.zeros((NUM_EXPERTS, D), jnp.float32), 'edge_index': jax.random.randint(ks[6], (2, N_EDGES), 0, B * N, jnp.int32)}
    _L1_ffn_all = _L1_ffn_setup()
    _L1_ffn_in = {k: v for k, v in _L1_ffn_all.items() if k in ('W_gat', 'att_src', 'att_dst', 'b_gat', 'ln_gamma', 'ln_beta', 'W1', 'b1', 'W2', 'b2', 'edge_index')}
    del _L1_ffn_all
    return {'x': x, 'L0_conv_w_q': _L0_conv_in['w_q'], 'L0_conv_w_kv': _L0_conv_in['w_kv'], 'L0_conv_w_out': _L0_conv_in['w_out'], 'L0_conv_pos_emb_h': _L0_conv_in['pos_emb_h'], 'L0_conv_pos_emb_w': _L0_conv_in['pos_emb_w'], 'L0_ffn_attention_mask': _L0_ffn_in['attention_mask'], 'L0_ffn_wr': _L0_ffn_in['wr'], 'L0_ffn_br': _L0_ffn_in['br'], 'L0_ffn_w1': _L0_ffn_in['w1'], 'L0_ffn_b1': _L0_ffn_in['b1'], 'L0_ffn_w2': _L0_ffn_in['w2'], 'L0_ffn_b2': _L0_ffn_in['b2'], 'L1_conv_Wqkv': _L1_conv_in['Wqkv'], 'L1_conv_Wproj': _L1_conv_in['Wproj'], 'L1_conv_bproj': _L1_conv_in['bproj'], 'L1_ffn_W_gat': _L1_ffn_in['W_gat'], 'L1_ffn_att_src': _L1_ffn_in['att_src'], 'L1_ffn_att_dst': _L1_ffn_in['att_dst'], 'L1_ffn_b_gat': _L1_ffn_in['b_gat'], 'L1_ffn_ln_gamma': _L1_ffn_in['ln_gamma'], 'L1_ffn_ln_beta': _L1_ffn_in['ln_beta'], 'L1_ffn_W1': _L1_ffn_in['W1'], 'L1_ffn_b1': _L1_ffn_in['b1'], 'L1_ffn_W2': _L1_ffn_in['W2'], 'L1_ffn_b2': _L1_ffn_in['b2'], 'L1_ffn_edge_index': _L1_ffn_in['edge_index']}

def reference(x, L0_conv_w_q, L0_conv_w_kv, L0_conv_w_out, L0_conv_pos_emb_h, L0_conv_pos_emb_w, L0_ffn_attention_mask, L0_ffn_wr, L0_ffn_br, L0_ffn_w1, L0_ffn_b1, L0_ffn_w2, L0_ffn_b2, L1_conv_Wqkv, L1_conv_Wproj, L1_conv_bproj, L1_ffn_W_gat, L1_ffn_att_src, L1_ffn_att_dst, L1_ffn_b_gat, L1_ffn_ln_gamma, L1_ffn_ln_beta, L1_ffn_W1, L1_ffn_b1, L1_ffn_W2, L1_ffn_b2, L1_ffn_edge_index):
    import jax
    import jax.numpy as jnp

    def _L0_conv_ref(x, w_q, w_kv, w_out, pos_emb_h, pos_emb_w):
        import jax, jax.numpy as jnp
        import numpy as np
        NUM_HEADS = 8
        BLOCK = 8
        HALO = 2

        def _rel_to_abs(rel):
            B, G, qh, qw, dim = rel.shape
            p = (dim + 1) // 2
            gap = p - qw
            flat = rel.reshape(B, G, qh, qw * dim)[:, :, :, qw - 1:-1]
            return flat.reshape(B, G, qh, qw, 2 * (p - 1))[:, :, :, :, gap:p + gap]

        def _relative_logits(pos_q, pos_emb_h, pos_emb_w):
            rel_w = _rel_to_abs(jnp.einsum('bghwd,dr->bghwr', pos_q, pos_emb_w))
            q_t = pos_q.transpose(0, 1, 3, 2, 4)
            rel_h = _rel_to_abs(jnp.einsum('bgwhd,dr->bgwhr', q_t, pos_emb_h))
            rel_h = rel_h.transpose(0, 1, 3, 2, 4)
            return rel_h[..., :, None] + rel_w[..., None, :]
        B, H, W, C = x.shape
        kd = C // NUM_HEADS
        kvk = BLOCK + 2 * HALO
        out_ch = w_out.shape[1]
        v_dim = out_ch // NUM_HEADS
        kv_per_head = (C + out_ch) // NUM_HEADS
        hh, ww = (H // BLOCK, W // BLOCK)
        scale = float(1.0 / np.sqrt(kd))
        q = (x @ w_q).reshape(B, hh, BLOCK, ww, BLOCK, NUM_HEADS, kd)
        q = q.transpose(0, 5, 1, 3, 2, 4, 6)
        attn_q = q.reshape(B, NUM_HEADS, hh, ww, BLOCK * BLOCK, kd) * scale
        pos_q = q.reshape(B, NUM_HEADS * hh * ww, BLOCK, BLOCK, kd)
        kv = jnp.pad(x @ w_kv, ((0, 0), (HALO, HALO), (HALO, HALO), (0, 0)))
        idx = np.arange(hh)[:, None] * BLOCK + np.arange(kvk)[None, :]
        idy = np.arange(ww)[:, None] * BLOCK + np.arange(kvk)[None, :]
        patches = kv[:, idx][:, :, :, idy]
        patches = patches.transpose(0, 1, 3, 2, 4, 5)
        kvh = patches.reshape(B, hh, ww, kvk, kvk, NUM_HEADS, kv_per_head)
        kvh = kvh.transpose(0, 5, 1, 2, 3, 4, 6).reshape(B, NUM_HEADS, hh, ww, kvk * kvk, kv_per_head)
        key, value = (kvh[..., :kd], kvh[..., kd:])
        scores = jnp.einsum('bnhwqd,bnhwkd->bnhwqk', attn_q, key)
        pos = _relative_logits(pos_q, pos_emb_h, pos_emb_w)
        pos = pos.reshape(B, NUM_HEADS, hh, ww, BLOCK * BLOCK, kvk * kvk)
        attn = jax.nn.softmax(scores + pos, axis=-1)
        out = jnp.einsum('bnhwqk,bnhwkv->bnhwqv', attn, value)
        out = out.reshape(B, NUM_HEADS, hh, ww, BLOCK, BLOCK, v_dim)
        out = out.transpose(0, 2, 4, 3, 5, 1, 6).reshape(B, H, W, NUM_HEADS * v_dim)
        return out @ w_out

    def _L0_ffn_ref(x, attention_mask, wr, br, w1, b1, w2, b2):
        import jax, jax.numpy as jnp
        import numpy as np
        B, S, D = (8, 2048, 128)
        H = 4 * D
        CAPACITY = 0.5
        b, s, d = x.shape
        weights = (jnp.einsum('bsd,do->bso', x, wr) + br)[..., 0]
        k = max(1, int(CAPACITY * s))
        kk = k - 1 if k > 1 else 1
        _, idx = jax.lax.top_k(weights, k)
        sel_idx = idx[:, :kk]
        sel = jnp.take_along_axis(x, sel_idx[:, :, None], axis=1)
        h = jax.nn.gelu(jnp.einsum('bkd,dh->bkh', sel, w1) + b1)
        y = jnp.einsum('bkh,hd->bkd', h, w2) + b2
        w_sel = jnp.take_along_axis(weights, sel_idx, axis=1)
        y = y * w_sel[..., None]
        batch_idx = jnp.arange(b)[:, None]
        processed = jnp.zeros_like(x).at[batch_idx, sel_idx].set(y)
        return processed + x

    def _L1_conv_ref(x, Wqkv, Wproj, bproj):
        import jax, jax.numpy as jnp
        import numpy as np
        KERNEL = 3
        DILATIONS = (2, 3)
        NUM_HEADS = 8

        def _unfold_windows(t, k, dil):
            B, C, H, W = t.shape
            pad = dil * (k - 1) // 2
            tp = jnp.pad(t, ((0, 0), (0, 0), (pad, pad), (pad, pad)))
            ws = [tp[:, :, i * dil:i * dil + H, j * dil:j * dil + W] for i in range(k) for j in range(k)]
            return jnp.stack(ws, axis=2)

        def _dilate_attention(q, k_, v, kernel, dil, head_dim):
            B, d, H, W = q.shape
            nh = d // head_dim
            scale = head_dim ** (-0.5)
            qh = q.reshape(B, nh, head_dim, H, W)
            kw = _unfold_windows(k_, kernel, dil).reshape(B, nh, head_dim, kernel * kernel, H, W)
            vw = _unfold_windows(v, kernel, dil).reshape(B, nh, head_dim, kernel * kernel, H, W)
            attn = jax.nn.softmax(jnp.einsum('bndhw,bndkhw->bnkhw', qh, kw) * scale, axis=2)
            out = jnp.einsum('bnkhw,bndkhw->bndhw', attn, vw)
            return out.transpose(0, 3, 4, 1, 2).reshape(B, H, W, d)
        B, H, W, C = x.shape
        nd = len(DILATIONS)
        head_dim = C // NUM_HEADS
        qkv = jnp.einsum('bhwc,oc->bohw', x, Wqkv).reshape(B, 3, nd, C // nd, H, W)
        outs = []
        for i, dil in enumerate(DILATIONS):
            q, k_, v = (qkv[:, 0, i], qkv[:, 1, i], qkv[:, 2, i])
            outs.append(_dilate_attention(q, k_, v, KERNEL, dil, head_dim))
        xo = jnp.concatenate(outs, axis=-1)
        return jnp.einsum('bhwc,oc->bhwo', xo, Wproj) + bproj

    def _L1_ffn_ref(x, W_gat, att_src, att_dst, b_gat, ln_gamma, ln_beta, W1, b1, W2, b2, edge_index):
        import jax, jax.numpy as jnp
        import numpy as np
        B, N, D = (16, 2048, 128)
        NUM_EXPERTS, TOP_K, HEADS = (4, 2, 4)
        N_EDGES = 524288
        LN_EPS = 1e-05

        def _layernorm(x, g, b):
            mu = x.mean(-1, keepdims=True)
            var = ((x - mu) ** 2).mean(-1, keepdims=True)
            return (x - mu) * jax.lax.rsqrt(var + LN_EPS) * g + b

        def _forward(x, edge_index, W_gat, att_src, att_dst, b_gat, ln_gamma, ln_beta, W1, b1, W2, b2):
            Bc, Nc, Dc = x.shape
            M = Bc * Nc
            x_flat = x.reshape(M, Dc)
            h = (x_flat @ W_gat).reshape(M, HEADS, NUM_EXPERTS)
            loops = jnp.arange(M, dtype=edge_index.dtype)
            src = jnp.concatenate([edge_index[0], loops])
            dst = jnp.concatenate([edge_index[1], loops])
            a_src = (h * att_src).sum(-1)
            a_dst = (h * att_dst).sum(-1)
            e = jax.nn.leaky_relu(a_src[src] + a_dst[dst], negative_slope=0.2)
            e_max = jax.ops.segment_max(e, dst, num_segments=M)
            ee = jnp.exp(e - e_max[dst])
            denom = jax.ops.segment_sum(ee, dst, num_segments=M)
            alpha = ee / (denom[dst] + 1e-16)
            msg = h[src] * alpha[:, :, None]
            agg = jax.ops.segment_sum(msg, dst, num_segments=M).reshape(M, HEADS * NUM_EXPERTS) + b_gat
            scores = _layernorm(agg, ln_gamma, ln_beta).reshape(M, HEADS, NUM_EXPERTS).mean(1)
            scores = scores.reshape(Bc, Nc, NUM_EXPERTS)
            topk_s, topk_i = jax.lax.top_k(scores, TOP_K)
            w = jax.nn.softmax(topk_s, axis=-1)
            out = jnp.zeros_like(x)
            for ei in range(NUM_EXPERTS):
                g = jnp.where(topk_i == ei, w, 0.0).sum(-1)
                hh = jax.nn.gelu(x @ W1[ei] + b1[ei], approximate=False)
                out = out + g[..., None] * (hh @ W2[ei] + b2[ei])
            return out
        return _forward(x, edge_index, W_gat, att_src, att_dst, b_gat, ln_gamma, ln_beta, W1, b1, W2, b2)

    def _gn(v, G=32, eps=1e-05):
        B_, H_, W_, C_ = v.shape
        g = v.reshape(B_, H_, W_, G, C_ // G)
        m = jnp.mean(g, axis=(1, 2, 4), keepdims=True)
        s = jnp.var(g, axis=(1, 2, 4), keepdims=True)
        return ((g - m) / jnp.sqrt(s + eps)).reshape(v.shape)

    def _ln_c(v, eps=1e-06):
        m = jnp.mean(v, axis=-1, keepdims=True)
        s = jnp.var(v, axis=-1, keepdims=True)
        return (v - m) / jnp.sqrt(s + eps)

    def _ln_t(v, eps=1e-05):
        m = jnp.mean(v, axis=-1, keepdims=True)
        s = jnp.var(v, axis=-1, keepdims=True)
        return (v - m) / jnp.sqrt(s + eps)

    def _to_tokens(v):
        B_, H_, W_, C_ = v.shape
        return v.reshape(B_, H_ * W_, C_)

    def _from_tokens(t, like):
        return t.reshape(like.shape)
    x = x + _L0_conv_ref(_ln_c(x), L0_conv_w_q, L0_conv_w_kv, L0_conv_w_out, L0_conv_pos_emb_h, L0_conv_pos_emb_w)
    t = _to_tokens(x)
    t = t + _L0_ffn_ref(_ln_t(t), L0_ffn_attention_mask, L0_ffn_wr, L0_ffn_br, L0_ffn_w1, L0_ffn_b1, L0_ffn_w2, L0_ffn_b2)
    x = _from_tokens(t, x)
    x = x + _L1_conv_ref(_ln_c(x), L1_conv_Wqkv, L1_conv_Wproj, L1_conv_bproj)
    t = _to_tokens(x)
    t = t + _L1_ffn_ref(_ln_t(t), L1_ffn_W_gat, L1_ffn_att_src, L1_ffn_att_dst, L1_ffn_b_gat, L1_ffn_ln_gamma, L1_ffn_ln_beta, L1_ffn_W1, L1_ffn_b1, L1_ffn_W2, L1_ffn_b2, L1_ffn_edge_index)
    x = _from_tokens(t, x)
    return x

_drawn_inputs = setup_inputs


def setup_inputs(seed=0):
    import zlib

    import numpy as np

    out = dict(_drawn_inputs(seed))
    spreads = {'L0_ffn_b1': (0.0, 0.8),
     'L0_ffn_b2': (0.0, 0.8),
     'L1_conv_bproj': (0.0, 0.512),
     'L1_ffn_b_gat': (0.0, 1.342),
     'L1_ffn_ln_gamma': (1.0, 0.6),
     'L1_ffn_ln_beta': (0.0, 2.0),
     'L1_ffn_b1': (0.0, 1.592),
     'L1_ffn_b2': (0.0, 0.733)}
    factors = {'L0_conv_w_q': 8.0,
     'L0_conv_w_kv': 8.0,
     'L0_conv_w_out': 8.0,
     'L0_conv_pos_emb_h': 8.0,
     'L0_conv_pos_emb_w': 8.0,
     'L0_ffn_wr': 6.708,
     'L0_ffn_w1': 8.0,
     'L0_ffn_w2': 8.0,
     'L1_ffn_att_src': 47.62,
     'L1_ffn_att_dst': 200.0,
     'L1_ffn_W_gat': 2.986}
    for name, (base, spread) in spreads.items():
        noise = np.random.default_rng([zlib.crc32(name.encode()), seed]).standard_normal(out[name].shape)
        drawn = base * np.exp(spread * noise) if base else spread * noise
        out[name] = jnp.asarray(drawn.astype(out[name].dtype))
    for name, factor in factors.items():
        out[name] = (out[name] * factor).astype(out[name].dtype)
    return out
```

```python
import concourse.bass as bass
from concourse import mybir
from contextlib import ExitStack

f32=mybir.dt.float32; i32=mybir.dt.int32; bf16=mybir.dt.bfloat16
ACT=mybir.ActivationFunctionType; ALU=mybir.AluOpType; AX=mybir.AxisListType
P=128; IMGS=4; IMGTOK=4096; TILES=32; C=128

def declare_dense(nc, ctx, SA, SB):
    class N: pass
    n=N()
    def sb(name,shape,dt=f32):
        t=ctx.enter_context(nc.sbuf_tensor(name,shape,dt)); return t
    def sem(name):
        s=ctx.enter_context(nc.semaphore(name)); return s
    n.X=SA[:,8192:12288].rearrange("p (t c) -> p t c",c=C)
    n.HTL=SA[:,12288:16384].rearrange("p (a m c) -> p a m c",a=2,m=4)
    n.XN=SA[:,16384:17408].rearrange("p (a t c) -> p a t c",a=2,t=4)
    n.ZQ,n.ZH,n.ZW=(SA[:,17408+1024*i:18432+1024*i].rearrange("p (w s q) -> p w s q",w=8,s=2) for i in range(3))
    n.KPAD=SB[:,0:4900]
    n.XPAD=sb("XPAD",[P,68*68]); n.VPAD=sb("VPAD",[P,70*70])
    V=n.VPAD
    n.XW=V[:,0:816]; n.KW=V[:,816:1632]; n.XV=V[:,1632:2784].rearrange("p (w k) -> p w k",w=8)
    n.PTS=V[0:72,2784:3808].rearrange("p (a q) -> p a q",a=8); n.VS=V[0:72,3808:4320].rearrange("p (s a q) -> p s a q",s=2,a=2); n.AOT=V[:,4320:4832]
    n.TB=V[:,0:640].rearrange("p (t k) -> p t k",k=20); n.ADB=V[:,640:768].rearrange("p (t k) -> p t k",k=4); n.HM=V[:,768:1280].rearrange("p (t k) -> p t k",k=16)
    n.ST=sb("ST",[P,TILES,6]); n.MV=sb("MV",[P,TILES,2]); n.RSTD=sb("RSTD",[P,TILES]); n.NMR=sb("NMR",[P,TILES]); n.RS1=sb("RS1",[P,TILES])
    n.QT=sb("QT",[P,512]); n.PRX=sb("PRX",[P,1152]); n.AOM=sb("AOM",[P,2,64])
    n.PR_=n.PRX[:,:].rearrange("p (s j k) -> p s j k",s=2,j=4)
    n.LG=n.PRX[:,0:288].rearrange("p (t k) -> p t k",t=4); n.AT=n.PRX[0:72,288:800]
    n.MX=sb("MX",[P,2,4]); n.SM=sb("SM",[P,2,4]); n.RSM=sb("RSM",[P,2,4])
    n.WQ=sb("WQ",[P,P]); n.WK=sb("WK",[P,P]); n.WV=sb("WV",[P,P]); n.WO=sb("WO",[P,P]); n.EH=sb("EH",[P,8,P]); n.EW=sb("EW",[P,8,P])
    n.W1=sb("W1",[P,512]); n.W2=sb("W2",[P,4,P]); n.B1=sb("B1",[P,4]); n.B2R=sb("B2R",[1,P]); n.WR=sb("WR",[P,1]); n.WRB=sb("WRB",[P,P]); n.BR=sb("BR",[P,1])
    n.WQKV=sb("WQKV",[P,384]); n.WP=sb("WP",[P,P]); n.BPR=sb("BPR",[1,4,P]); n.WG=sb("WG",[P,16]); n.AS=sb("AS",[P,16]); n.AD=sb("AD",[P,16])
    n.PAR=sb("PAR",[P,2]); n.PAR4=sb("PAR4",[P,2]); n.LM=sb("LM",[P,P]); n.INDH=sb("INDH",[P,144]); n.INDW=sb("INDW",[P,144]); n.EXPN=sb("EXPN",[72,9,P]); n.HONE=sb("HONE",[P,8])
    n.WCOL=sb("WCOL",[P,TILES]); n.RK=sb("RK",[P,4,TILES]); n.RANK=sb("RANK",[P,TILES]); n.GS=sb("GS",[P,TILES])
    n.PRD=n.HTL[:,0,:,:]
    n.PR2=n.HTL[:,1,:,:]
    n.LMX=sb("LMX",[P,4,8])
    n.tick_dve, n.tick_pe, n.s_xv, n.w_load, n.x_load, n.wprep = [sem(s) for s in ("tick_dve", "tick_pe", "s_xv", "w_load", "x_load", "wprep",)]
    n.bar_pe, n.bar_act, n.bar_dve, n.ln_st, n.ln_sd, n.ln_xn = [sem(s) for s in ("bar_pe", "bar_act", "bar_dve", "ln_st", "ln_sd", "ln_xn",)]
    n.ln_tr, n.ln_cp, n.s_xw, n.s_k, n.s_kc, n.s_q = [sem(s) for s in ("ln_tr", "ln_cp", "s_xw", "s_k", "s_kc", "s_q",)]
    n.s_qc, n.s_zq, n.s_ph, n.s_pw, n.s_zh, n.s_zw = [sem(s) for s in ("s_qc", "s_zq", "s_ph", "s_pw", "s_zh", "s_zw",)]
    n.s_qk, n.s_mx, n.s_exp, n.s_nrm, n.s_tr, n.s_pta = [sem(s) for s in ("s_qk", "s_mx", "s_exp", "s_nrm", "s_tr", "s_pta",)]
    n.s_ptd, n.s_v, n.s_vc, n.s_pv, n.s_ao, n.s_pj = [sem(s) for s in ("s_ptd", "s_v", "s_vc", "s_pv", "s_ao", "s_pj",)]
    n.s_xa, n.s_w, n.s_wc, n.s_h, n.s_ge, n.s_y = [sem(s) for s in ("s_xa", "s_w", "s_wc", "s_h", "s_ge", "s_y",)]
    n.s_ya, n.s_pz, n.s_kv, n.s_kvc, n.s_vvc, n.s_cq = [sem(s) for s in ("s_ya", "s_pz", "s_kv", "s_kvc", "s_vvc", "s_cq",)]
    n.s_cqc, n.s_pr, n.s_lg, n.s_sb, n.s_ex, n.s_nm = [sem(s) for s in ("s_cqc", "s_pr", "s_lg", "s_sb", "s_ex", "s_nm",)]
    n.s_at, n.s_atc, n.s_ep, n.s_p2, n.s_pp, n.s_cxa = [sem(s) for s in ("s_at", "s_atc", "s_ep", "s_p2", "s_pp", "s_cxa",)]
    n.s_gt, n.s_tb, n.x3_st, n.tn_st, n.t_st, n.wdone = [sem(s) for s in ("s_gt", "s_tb", "x3_st", "tn_st", "t_st", "wdone",)]
    n.bar=dict(pe=n.bar_pe,act=n.bar_act,dve=n.bar_dve)
    return n

def sync_weights(sp, n, d):
    k=0
    def ld(dst,src):
        nonlocal k
        sp.dma_start(dst,src).then_inc(n.w_load,16); k+=16
    ld(n.WQ[:,:],d["w_q"]); 
    kv=d["w_kv"].rearrange("c (n t e) -> c n t e",n=8,t=2)
    ld(n.WK[:,:].rearrange("c (n e) -> c n e",n=8),kv[:,:,0,:]); ld(n.WV[:,:].rearrange("c (n e) -> c n e",n=8),kv[:,:,1,:])
    ld(n.WO[:,:],d["w_out"])
    ld(n.W1[:,:],d["w1"]); ld(n.W2[:,:,:],d["w2"].rearrange("(m p) o -> p m o",p=P)); 
    ld(n.B1[:,:],d["b1T"]); ld(n.B2R[:,:],d["b2"].rearrange("(a n) -> a n",a=1))
    ld(n.WR[:,:],d["wr"]); ld(n.BR[:,:],d["br"].rearrange("(a n) -> a n",a=1).to_broadcast((P,1)))
    ld(n.WQKV[:,:],d["WqkvT"]); ld(n.WP[:,:],d["WprojT"])
    for i in range(4): ld(n.BPR[:,i,:],d["bproj"].rearrange("(a n) -> a n",a=1))
    ld(n.WG[:,:],d["W_gat"]); ld(n.AS[:,:],d["att_src"].rearrange("h e -> (h e)").rearrange("(a n) -> a n",a=1).to_broadcast((P,16))); ld(n.AD[:,:],d["att_dst"].rearrange("h e -> (h e)").rearrange("(a n) -> a n",a=1).to_broadcast((P,16)))
    for t,nm in ((n.PAR,"PAR"),(n.LM,"LM"),(n.INDH,"INDH"),(n.INDW,"INDW"),(n.HONE,"HONE")): ld(t[:,:],d[nm])
    ld(n.EXPN[:,:,:],d["EXPN"])
    sp.wait_ge(n.wprep,1)
    for h in range(8):
        for t,nm in ((n.EH,"pos_emb_h"),(n.EW,"pos_emb_w")):
            for q in range(8):
                ld(t[16*h:16*h+16,q,16*h:16*h+12],d[nm][:,11-q:23-q])
    n.NW=k

def dve_prep(dve,n):
    dve.memset(n.EH[:,:,:],0.0); dve.memset(n.EW[:,:,:],0.0).then_inc(n.wprep,1)
    dve.wait_ge(n.w_load,n.NW)
    dve.tensor_scalar(n.PAR4[:,:],n.PAR[:,:],0.25,None,ALU.mult)
    dve.tensor_copy(n.WRB[:,:],n.WR[:,:].to_broadcast((P,P))).then_inc(n.wprep,1)

SE=4
def barrier(eng, n, me, b, st):
    eng.drain().then_inc(n.bar[me],1)
    for o in ("pe","act","dve"):
        if o!=me: eng.wait_ge(n.bar[o],b*SE+(st+1))

class Ln:
    @staticmethod
    def dve(dve,n,L,eps):
        for t in range(TILES): dve.bn_stats(n.ST[:,t,:],n.X[:,t,:])
        dve.drain()
        for t in range(TILES): dve.bn_aggr(n.MV[:,t,:],n.ST[:,t,:])
        dve.drain()
        dve.tensor_scalar(n.RSTD[:,:],n.MV[:,:,1],eps,None,ALU.add).then_inc(n.ln_st,1)
        dve.wait_ge(n.ln_sd,L+1)
        dve.reciprocal(n.RSTD[:,:],n.RSTD[:,:])
        dve.drain()
        dve.tensor_tensor(n.NMR[:,:],n.MV[:,:,0],n.RSTD[:,:],ALU.mult)
        dve.drain()
        dve.tensor_scalar(n.NMR[:,:],n.NMR[:,:],-1.0,None,ALU.mult)
        dve.drain()
        for g in range(8):
            if g>=2: dve.wait_ge(n.ln_tr,L*8+(g-1))
            for i in range(4):
                t=4*g+i
                last=dve.tensor_scalar(n.XN[:,g%2,i,:],n.X[:,t,:],n.RSTD[:,t:t+1],n.NMR[:,t:t+1],ALU.mult,ALU.add)
            last.then_inc(n.ln_xn,1)
    @staticmethod
    def pe(pe,n,PSB,ident,L):
        for g in range(8):
            pe.wait_ge(n.ln_xn,L*8+(g+1))
            if g>=2: pe.wait_ge(n.ln_cp,L*8+(g-1))
            for i in range(4):
                last=pe.transpose(PSB[:,(6+g%2)*512+i*P:(6+g%2)*512+(i+1)*P],n.XN[:,g%2,i,:],ident)
            last.then_inc(n.ln_tr,1)
    @staticmethod
    def act(act,n,PSB,L,padded):
        act.wait_ge(n.ln_st,L+1)
        act.activation(n.RSTD[:,:],n.RSTD[:,:],ACT.Sqrt).then_inc(n.ln_sd,1)
        for g in range(8):
            act.wait_ge(n.ln_tr,L*8+(g+1))
            src=PSB[:,(6+g%2)*512:(7+g%2)*512]
            if padded:
                dst=n.XPAD[:,:].rearrange("c (y x) -> c y x",y=68)[:,2+8*g:10+8*g,2:66]
                src=src.rearrange("c (y x) -> c y x",y=8)
            else: dst=n.XPAD[:,g*512:(g+1)*512]
            act.activation(dst,src,ACT.Copy).then_inc(n.ln_cp,1)

def l0conv_dve(dve,n,PSB,b):
    dve.wait_ge(n.x_load,b*64+64)
    xp=n.XPAD[:,:].rearrange("c (y x) -> c y x",y=68)
    dve.memset(xp[:,0:2,:],0.0); dve.memset(xp[:,66:68,:],0.0); dve.memset(xp[:,2:66,0:2],0.0); dve.memset(xp[:,2:66,66:68],0.0).then_inc(n.s_pz,1)
    Ln.dve(dve,n,b*4,1e-6)
    with dve.Fori(0,8) as hh:
        st=b*8+hh
        def norm(w):
            dve.wait_ge(n.s_exp,st*8+(w+1))
            dve.reciprocal(n.RSM[:,w%2,:],n.SM[:,w%2,:])
            dve.drain()
            dve.tensor_tensor(n.PR_[:,w%2,:,:],n.PR_[:,w%2,:,:],n.RSM[:,w%2,:].unsqueeze(2).to_broadcast((P,4,144)),ALU.mult).then_inc(n.s_nrm,1)
        def mx(w):
            dve.wait_ge(n.s_qk,st*8+(w+1))
            dve.tensor_reduce(n.MX[:,w%2,:],PSB[:,0:2048].rearrange("p (j x) -> p j x",j=4)[:,:,0:144],AX.X,ALU.max,negate=True).then_inc(n.s_mx,1)
        dve.wait_ge(n.s_qc,st+1)
        q=n.QT[:,:].rearrange("p (y w x) -> p w y x",y=8,w=8)
        for s in range(2):
            for w in range(8):
                last=dve.tensor_scalar(n.ZQ[:,w,s,:].rearrange("p (y x) -> p y x",y=8),q[:,w],n.PAR4[:,s:s+1],None,ALU.mult)
        last.then_inc(n.s_zq,1)
        dve.wait_ge(n.s_ph,st+1)
        q=PSB[:,5*512:6*512].rearrange("p (y w x) -> p w y x",y=8,w=8)
        for s in range(2):
            for w in range(8):
                last=dve.tensor_scalar(n.ZH[:,w,s,:].rearrange("p (y x) -> p y x",y=8),q[:,w],n.PAR[:,s:s+1],None,ALU.mult)
        last.then_inc(n.s_zh,1)
        mx(0)
        for w in range(8):
            norm(w)
            if w<7: mx(w+1)
            dve.wait_ge(n.s_tr,st*8+(w+1))
            dve.tensor_copy(n.PTS[:,4:8,:],PSB[0:72,5*512:6*512].rearrange("p (a q) -> p a q",a=4)).then_inc(n.s_ptd,1)
            dve.wait_ge(n.s_pv,st*8+(w+1))
            dve.tensor_scalar(n.AOM[:,w%2,:],PSB[:,7*512:7*512+64],n.PAR[:,0:1],None,ALU.mult)
            dve.drain()
            dve.scalar_tensor_tensor(out=n.AOT[:,:].rearrange("p (y x) -> p y x",y=8)[:,:,8*w:8*w+8],in0=PSB[:,7*512+64:7*512+128].rearrange("p (y x) -> p y x",y=8),scalar=n.PAR[:,1:2],in1=n.AOM[:,w%2,:].rearrange("p (y x) -> p y x",y=8),op0=ALU.mult,op1=ALU.add).then_inc(n.s_ao,1)
        dve.wait_ge(n.s_pj,st+1)
        xs=n.X[:,bass.ds(hh*4,4),:]
        dve.tensor_tensor(xs,xs,PSB[:,6*512:7*512].rearrange("p (t c) -> p t c",t=4),ALU.add).then_inc(n.s_xa,1)
    barrier(dve,n,"dve",b,0)

def l0conv_act(act,n,PSB,b,d):
    for q in range(4):
        act.dma_start(n.X[:,8*q:8*q+8,:],d["x"].rearrange("(t p) c -> p t c",p=P)[:,bass.ds(b*TILES+8*q,8),:]).then_inc(n.x_load,16)
    act.wait_ge(n.s_pz,b+1)
    Ln.act(act,n,PSB,b*4,True)
    act.drain()
    with act.Fori(0,8) as hh:
        st=b*8+hh
        act.wait_ge(n.s_pj,st)
        act.activation(n.XW[:,:],n.XPAD[:,bass.ds(hh*(8*68),12*68)],ACT.Copy).then_inc(n.s_xw,1)
        act.drain()
        for w in range(8):
            last=act.activation(n.XV[:,w,:].rearrange("p (y x) -> p y x",y=12),n.XW[:,:].rearrange("p (y x) -> p y x",y=12)[:,:,8*w:8*w+12],ACT.Copy)
        last.then_inc(n.s_xv,1)
        act.wait_ge(n.s_k,st+1)
        for i in range(2):
            last=act.activation(n.KW[:,408*i:408*(i+1)],PSB[:,(6+i)*512:(6+i)*512+408],ACT.Copy)
        last.then_inc(n.s_kc,1)
        act.wait_ge(n.s_q,st+1)
        act.activation(n.QT[:,:],PSB[:,4*512:5*512],ACT.Copy).then_inc(n.s_qc,1)
        act.wait_ge(n.s_pw,st+1)
        q=PSB[:,4*512:5*512].rearrange("p (x y w) -> p w y x",x=8,y=8)
        for s in range(2):
            for w in range(8):
                last=act.activation(n.ZW[:,w,s,:].rearrange("p (y x) -> p y x",y=8),q[:,w],ACT.Copy,scale=n.PAR[:,s:s+1])
        last.then_inc(n.s_zw,1)
        def ex(w):
            act.wait_ge(n.s_mx,st*8+(w+1))
            if w>=2: act.wait_ge(n.s_tr,st*8+(w-1))
            for j in range(4):
                last=act.activation(n.PR_[:,w%2,j,:],PSB[:,j*512:j*512+144],ACT.Exp,bias=n.MX[:,w%2,j:j+1],accum_out=n.SM[:,w%2,j:j+1])
            last.then_inc(n.s_exp,1)
        def vc(w):
            act.wait_ge(n.s_v,st*8+(w+1))
            act.activation(n.VS[:,w%2,:,:],PSB[0:72,6*512:6*512+256].rearrange("p (a q) -> p a q",a=2),ACT.Copy).then_inc(n.s_vc,1)
        ex(0); vc(0)
        for w in range(8):
            if w<7: ex(w+1); vc(w+1)
            act.wait_ge(n.s_tr,st*8+(w+1))
            act.activation(n.PTS[:,0:4,:],PSB[0:72,4*512:5*512].rearrange("p (a q) -> p a q",a=4),ACT.Copy).then_inc(n.s_pta,1)
    barrier(act,n,"act",b,0)

def l0conv_pe(pe,n,PSB,ident,b):
    Ln.pe(pe,n,PSB,ident,b*4)
    with pe.Fori(0,8) as hh:
        st=b*8+hh
        xw=n.XW[:,:].rearrange("c (y x) -> c y x",y=12); kw=n.KW[:,:].rearrange("c (y x) -> c y x",y=12)
        pe.wait_ge(n.s_xw,st+1); pe.wait_ge(n.s_xa,st); pe.wait_ge(n.s_pta,st*8)
        for i in range(2):
            last=pe.matmul(PSB[:,(6+i)*512:(6+i)*512+408],n.WK[:,:],n.XW[:,408*i:408*(i+1)],start=True,stop=True)
        last.then_inc(n.s_k,1)
        pe.matmul(PSB[:,4*512:5*512],n.WQ[:,:],xw[:,2:10,2:66],start=True,stop=True).then_inc(n.s_q,1)
        pe.wait_ge(n.s_qc,st+1); pe.wait_ge(n.s_zq,st+1)
        qt=n.QT[:,:].rearrange("c (y w x) -> c y w x",y=8,w=8)
        for y in range(8):
            last=pe.matmul(PSB[:,5*512+64*y:5*512+64*(y+1)],n.EH[:,y,:],n.QT[:,64*y:64*(y+1)],start=True,stop=True)
        last.then_inc(n.s_ph,1)
        for x in range(8):
            last=pe.matmul(PSB[:,4*512+64*x:4*512+64*(x+1)],n.EW[:,x,:],qt[:,:,:,x],start=True,stop=True)
        last.then_inc(n.s_pw,1)
        pe.wait_ge(n.s_xv,st+1); pe.wait_ge(n.s_kc,st+1); pe.wait_ge(n.s_zh,st+1); pe.wait_ge(n.s_zw,st+1)
        def S(w):
            if w>=1: pe.wait_ge(n.s_exp,st*8+w)
            for j in range(4):
                r=slice(32*j,32*j+32)
                z=lambda t: t[r,w,:,:].rearrange("p s q -> p (s q)")
                o=PSB[:,j*512:j*512+144]
                pe.matmul(o,z(n.ZQ),kw[r,:,8*w:8*w+12],start=True,stop=False)
                pe.matmul(o,z(n.ZH),n.INDH[r,:],start=False,stop=False)
                last=pe.matmul(o,z(n.ZW),n.INDW[r,:],start=False,stop=True)
            last.then_inc(n.s_qk,1)
        def V(w):
            if w>=1: pe.wait_ge(n.s_vc,st*8+w)
            for g in range(2):
                last=pe.matmul(PSB[0:72,6*512+g*P:6*512+(g+1)*P],n.XV[:,w,72*g:72*g+72],n.WV[:,:],start=True,stop=True)
            last.then_inc(n.s_v,1)
        S(0); V(0)
        for w in range(8):
            if w<7: S(w+1); V(w+1)
            pe.wait_ge(n.s_nrm,st*8+(w+1)); 
            if w>=1: pe.wait_ge(n.s_pta,st*8+w); pe.wait_ge(n.s_ptd,st*8+w)
            for j in range(4):
                for g in range(2):
                    o=(4+j//2)*512+((j%2)*2+g)*P
                    last=pe.transpose(PSB[0:72,o:o+P],n.PR_[:,w%2,j,72*g:72*g+72],ident)
            last.then_inc(n.s_tr,1)
            pe.wait_ge(n.s_pta,st*8+(w+1)); pe.wait_ge(n.s_ptd,st*8+(w+1)); pe.wait_ge(n.s_vc,st*8+(w+1))
            if w>=1: pe.wait_ge(n.s_ao,st*8+w)
            for j in range(4):
                for g in range(2):
                    last=pe.matmul(PSB[32*j:32*j+32,7*512:7*512+P],n.VS[:,w%2,g,32*j:32*j+32],n.PTS[:,2*j+g,:],start=(g==0),stop=(g==1))
            last.then_inc(n.s_pv,1)
        pe.wait_ge(n.s_ao,st*8+8)
        for i in range(4):
            last=pe.matmul(PSB[:,6*512+P*i:6*512+P*(i+1)],n.AOT[:,P*i:P*(i+1)],n.WO[:,:],start=True,stop=True)
        last.then_inc(n.s_pj,1)
    barrier(pe,n,"pe",b,0)

KEEP=2047
def l0ffn_dve(dve,n,PSB,b,ident):
    Ln.dve(dve,n,b*4+1,1e-5)
    dve.tensor_scalar(n.RS1[:,:],n.RSTD[:,:],1.0,None,ALU.add)
    dve.memset(n.RK[:,:,:],0.0)
    dve.drain()
    for t in range(TILES):
        dve.tensor_scalar(n.X[:,t,:],n.X[:,t,:],n.RS1[:,t:t+1],n.NMR[:,t:t+1],ALU.mult,ALU.add)
    wrow=n.VPAD[:,0:IMGTOK]; junk=n.KPAD[:,0:IMGTOK]
    dve.wait_ge(n.s_wc,b*8+8)
    dve.tensor_tensor(junk.rearrange("p (t j) -> p t j",j=P),wrow.rearrange("p (t j) -> p t j",j=P),ident.unsqueeze(1).to_broadcast((P,TILES,P)),ALU.mult)
    dve.drain()
    dve.tensor_reduce(n.WCOL[:,:],junk.rearrange("p (t j) -> p t j",j=P),AX.X,ALU.add)
    dve.drain()
    for t in range(TILES):
        w=n.WCOL[:,t:t+1]
        if t: dve.tensor_scalar(junk[:,0:t*P],wrow[:,0:t*P],w,0.0,ALU.is_ge,ALU.add,accum_out=n.RK[:,0,t:t+1])
        if t<TILES-1: dve.tensor_scalar(junk[:,(t+1)*P:],wrow[:,(t+1)*P:],w,0.0,ALU.is_gt,ALU.add,accum_out=n.RK[:,1,t:t+1])
        blk=wrow[:,t*P:(t+1)*P]
        dve.scalar_tensor_tensor(out=junk[:,t*P:(t+1)*P],in0=blk,scalar=w,in1=n.LM[:,:],op0=ALU.is_ge,op1=ALU.mult,accum_out=n.RK[:,2,t:t+1])
        dve.drain()
        dve.scalar_tensor_tensor(out=junk[:,t*P:(t+1)*P],in0=blk,scalar=w,in1=n.UM,op0=ALU.is_gt,op1=ALU.mult,accum_out=n.RK[:,3,t:t+1])
        dve.drain()
    dve.tensor_reduce(n.RANK[:,:],n.RK[:,:,:].rearrange("p a t -> p t a"),AX.X,ALU.add)
    dve.drain()
    dve.scalar_tensor_tensor(out=n.GS[:,:],in0=n.RANK[:,:],scalar=float(KEEP),in1=n.WCOL[:,:],op0=ALU.is_lt,op1=ALU.mult)
    dve.drain()
    for g in range(8):
        dve.wait_ge(n.s_y,b*8+(g+1))
        for i in range(4):
            t=4*g+i
            last=dve.scalar_tensor_tensor(out=n.X[:,t,:],in0=PSB[:,(6+g%2)*512+i*P:(6+g%2)*512+(i+1)*P],scalar=n.GS[:,t:t+1],in1=n.X[:,t,:],op0=ALU.mult,op1=ALU.add)
        last.then_inc(n.s_ya,1)
    barrier(dve,n,"dve",b,1)

def l0ffn_act(act,n,PSB,b):
    Ln.act(act,n,PSB,b*4+1,False)
    for g in range(8):
        act.wait_ge(n.s_w,b*8+(g+1))
        act.activation(n.VPAD[:,512*g:512*(g+1)],PSB[:,(g%2)*512:(g%2+1)*512],ACT.Identity,bias=n.BR[:,:]).then_inc(n.s_wc,1)
    for g in range(8):
        for m in range(4):
            act.wait_ge(n.s_h,b*32+(4*g+m+1))
            if g>=2 and m==0: act.wait_ge(n.s_y,b*8+(g-1))
            act.activation(n.HTL[:,g%2,m,:],PSB[:,(2+m)*512:(3+m)*512],ACT.Gelu_apprx_tanh,bias=n.B1[:,m:m+1]).then_inc(n.s_ge,1)
    barrier(act,n,"act",b,1)

def l0ffn_pe(pe,n,PSB,ident,ones,b):
    Ln.pe(pe,n,PSB,ident,b*4+1)
    pe.wait_ge(n.ln_cp,b*32+16)
    for g in range(8):
        if g>=2: pe.wait_ge(n.s_wc,b*8+(g-1))
        pe.matmul(PSB[:,(g%2)*512:(g%2+1)*512],n.WRB[:,:],n.XPAD[:,512*g:512*(g+1)],start=True,stop=True).then_inc(n.s_w,1)
    def H(g):
        for m in range(4):
            if g: pe.wait_ge(n.s_ge,b*32+(4*(g-1)+m+1))
            pe.matmul(PSB[:,(2+m)*512:(3+m)*512],n.W1[:,P*m:P*(m+1)],n.XPAD[:,512*g:512*(g+1)],start=True,stop=True).then_inc(n.s_h,1)
    H(0)
    for g in range(8):
        if g<7: H(g+1)
        pe.wait_ge(n.s_ge,b*32+(4*g+4))
        if g>=2: pe.wait_ge(n.s_ya,b*8+(g-1))
        for i in range(4):
            o=PSB[:,(6+g%2)*512+i*P:(6+g%2)*512+(i+1)*P]
            pe.matmul(o,ones[0:1,:],n.B2R[:,:],start=True,stop=False)
            for m in range(4):
                last=pe.matmul(o,n.HTL[:,g%2,m,i*P:(i+1)*P],n.W2[:,m,:],start=False,stop=(m==3))
        last.then_inc(n.s_y,1)
    barrier(pe,n,"pe",b,1)

def halves(n_,buf,g8,a,bb):
    out=[]
    for lo,dil in ((0,2),(64,3)):
        v=buf[lo:lo+64,:].rearrange("p (y x) -> p y x",y=70)
        out.append((lo,v[:,bass.ds(g8+(3+(a-1)*dil),8),3+(bb-1)*dil:3+(bb-1)*dil+64]))
    return out
def l1conv_dve(dve,n,PSB,b):
    dve.memset(n.KPAD[:,:],0.0); dve.memset(n.VPAD[:,:],0.0).then_inc(n.s_pz,1)
    Ln.dve(dve,n,b*4+2,1e-6)
    for g in range(8):
        dve.wait_ge(n.s_kv,b*8+(g+1))
        dve.tensor_copy(n.VPAD[:,:].rearrange("p (y x) -> p y x",y=70)[:,3+8*g:11+8*g,3:67],PSB[:,(2+g%2)*512:(3+g%2)*512].rearrange("p (y x) -> p y x",y=8)).then_inc(n.s_vvc,1)
    dve.drain()
    dve.wait_ge(n.s_kvc,b*8+8); dve.sem_inc(n.tick_dve,1)
    with dve.Fori(0,8) as g:
        c=b*8+g
        dve.wait_ge(n.s_cqc,c+1)
        for k in range(9):
            if k>=3: dve.wait_ge(n.s_lg,c*9+(k-2))
            for lo,src in halves(n,n.KPAD,g*8,k//3,k%3):
                last=dve.tensor_tensor(n.PRD[lo:lo+64,k%3,:].rearrange("p (y x) -> p y x",y=8),n.QT[lo:lo+64,:].rearrange("p (y x) -> p y x",y=8),src,ALU.mult)
            last.then_inc(n.s_pr,1)
        dve.wait_ge(n.s_lg,c*9+9)
        lg=PSB[:,5*512:5*512+288]
        dve.tensor_reduce(n.LMX[:,:,:],lg.rearrange("p (t k h) -> p t h k",t=4,k=9),AX.X,ALU.max)
        dve.drain()
        for t in range(4):
            last=dve.tensor_tensor(n.LG[:,t,:].rearrange("p (k h) -> p k h",k=9),lg[:,72*t:72*(t+1)].rearrange("p (k h) -> p k h",k=9),n.LMX[:,t,:].unsqueeze(1).to_broadcast((P,9,8)),ALU.subtract)
        last.then_inc(n.s_sb,1)
        dve.wait_ge(n.s_ex,c+1)
        dve.tensor_reduce(n.LMX[:,:,:],n.LG[:,:,:].rearrange("p t (k h) -> p t h k",k=9),AX.X,ALU.add)
        dve.drain()
        dve.reciprocal(n.LMX[:,:,:],n.LMX[:,:,:])
        dve.drain()
        for t in range(4):
            v=n.LG[:,t,:].rearrange("p (k h) -> p k h",k=9)
            last=dve.tensor_tensor(v,v,n.LMX[:,t,:].unsqueeze(1).to_broadcast((P,9,8)),ALU.mult)
        last.then_inc(n.s_nm,1)
        for k in range(9):
            dve.wait_ge(n.s_ep,c*9+(k+1))
            if k>=3: dve.wait_ge(n.s_pp,c*9+(k-2))
            for lo,src in halves(n,n.VPAD,g*8,k//3,k%3):
                last=dve.tensor_tensor(n.PR2[lo:lo+64,k%3,:].rearrange("p (y x) -> p y x",y=8),PSB[lo:lo+64,(k%2)*512:(k%2+1)*512].rearrange("p (y x) -> p y x",y=8),src,ALU.mult)
            last.then_inc(n.s_p2,1)
        dve.wait_ge(n.s_pp,c*9+9)
        xs=n.X[:,bass.ds(g*4,4),:]
        dve.tensor_tensor(xs,xs,PSB[:,7*512:8*512].rearrange("p (t c) -> p t c",t=4),ALU.add).then_inc(n.s_cxa,1)
    barrier(dve,n,"dve",b,2)

def l1conv_act(act,n,PSB,b):
    Ln.act(act,n,PSB,b*4+2,False)
    for g in range(8):
        act.wait_ge(n.s_kv,b*8+(g+1))
        act.activation(n.KPAD[:,:].rearrange("p (y x) -> p y x",y=70)[:,3+8*g:11+8*g,3:67],PSB[:,(g%2)*512:(g%2+1)*512].rearrange("p (y x) -> p y x",y=8),ACT.Copy).then_inc(n.s_kvc,1)
    with act.Fori(0,8) as g:
        c=b*8+g
        act.wait_ge(n.s_cq,c+1)
        act.activation(n.QT[:,:],PSB[:,4*512:5*512],ACT.Copy).then_inc(n.s_cqc,1)
        act.wait_ge(n.s_sb,c+1)
        act.activation(n.LG[:,:,:],n.LG[:,:,:],ACT.Exp,scale=0.25).then_inc(n.s_ex,1)
        act.wait_ge(n.s_at,c+1)
        act.activation(n.AT[:,:],PSB[0:72,6*512:7*512],ACT.Copy).then_inc(n.s_atc,1)
    barrier(act,n,"act",b,2)

def l1conv_pe(pe,n,PSB,ident,ones,b):
    Ln.pe(pe,n,PSB,ident,b*4+2)
    pe.wait_ge(n.ln_cp,b*32+24)
    for g in range(8):
        if g>=2: pe.wait_ge(n.s_kvc,b*8+(g-1)); pe.wait_ge(n.s_vvc,b*8+(g-1))
        x=n.XPAD[:,512*g:512*(g+1)]
        pe.matmul(PSB[:,(g%2)*512:(g%2+1)*512],n.WQKV[:,P:2*P],x,start=True,stop=True)
        pe.matmul(PSB[:,(2+g%2)*512:(3+g%2)*512],n.WQKV[:,2*P:3*P],x,start=True,stop=True).then_inc(n.s_kv,1)
    pe.wait_ge(n.s_kvc,b*8+8); pe.wait_ge(n.s_vvc,b*8+8); pe.sem_inc(n.tick_pe,1)
    with pe.Fori(0,8) as g:
        c=b*8+g
        pe.wait_ge(n.s_cqc,c)
        pe.matmul(PSB[:,4*512:5*512],n.WQKV[:,0:P],n.XPAD[:,bass.ds(g*512,512)],start=True,stop=True).then_inc(n.s_cq,1)
        pe.wait_ge(n.s_sb,c)
        for k in range(9):
            pe.wait_ge(n.s_pr,c*9+(k+1))
            for t in range(4):
                o=5*512+72*t+8*k
                last=pe.matmul(PSB[:,o:o+8],n.PRD[:,k%3,P*t:P*(t+1)],n.HONE[:,:],start=True,stop=True)
            last.then_inc(n.s_lg,1)
        pe.wait_ge(n.s_cxa,c)
        pe.matmul(PSB[:,7*512:8*512],ones[0:1,:],n.BPR[:,:,:].rearrange("a t c -> a (t c)"),start=True,stop=False,skip_group_check=True)
        pe.wait_ge(n.s_nm,c+1); pe.wait_ge(n.s_atc,c)
        for t in range(4):
            last=pe.transpose(PSB[0:72,6*512+P*t:6*512+P*(t+1)],n.LG[:,t,:],ident)
        last.then_inc(n.s_at,1)
        pe.wait_ge(n.s_atc,c+1)
        def E(k):
            if k>=2: pe.wait_ge(n.s_p2,c*9+(k-1))
            pe.matmul(PSB[:,(k%2)*512:(k%2+1)*512],n.EXPN[:,k,:],n.AT[:,:],start=True,stop=True).then_inc(n.s_ep,1)
        E(0)
        for k in range(9):
            if k<8: E(k+1)
            pe.wait_ge(n.s_p2,c*9+(k+1))
            for t in range(4):
                last=pe.matmul(PSB[:,7*512+P*t:7*512+P*(t+1)],n.PR2[:,k%3,P*t:P*(t+1)],n.WP[:,:],start=False,stop=(k==8),skip_group_check=True)
            last.then_inc(n.s_pp,1)
    barrier(pe,n,"pe",b,2)

def gat_dve(dve,n,PSB,b):
    Ln.dve(dve,n,b*4+3,1e-5)
    dve.wait_ge(n.s_gt,b+1)
    h=PSB[:,0:512].rearrange("p (t c) -> p t c",c=16)
    dve.tensor_copy(n.TB[:,:,0:16],h)
    for a,(att,dst) in enumerate(((n.AS,n.TB[:,:,16:20]),(n.AD,n.ADB[:,:,:]))):
        dve.drain()
        dve.tensor_tensor(n.HM[:,:,:],h,att[:,:].unsqueeze(1).to_broadcast((P,TILES,16)),ALU.mult)
        dve.drain()
        last=dve.tensor_reduce(dst,n.HM[:,:,:].rearrange("p t (h e) -> p t h e",h=4),AX.X,ALU.add)
    last.then_inc(n.s_tb,1)
    dve.drain()
    dve.wait_ge(n.x3_st,b*16+16); dve.wait_ge(n.tn_st,b*16+16); dve.wait_ge(n.t_st,b*32+32); dve.sem_inc(n.tick_dve,1)
    barrier(dve,n,"dve",b,3)
def gat_act(act,n,PSB,b,d):
    act.dma_start(d["X3"].rearrange("(t p) c -> p t c",p=P)[:,bass.ds(b*TILES,TILES),:],n.X[:,:,:]).then_inc(n.x3_st,16)
    Ln.act(act,n,PSB,b*4+3,False)
    act.drain()
    act.wait_ge(n.ln_cp,b*32+32)
    act.dma_start(d["TNT"][:,bass.ds(b*IMGTOK,IMGTOK)],n.XPAD[:,0:IMGTOK]).then_inc(n.tn_st,16)
    act.wait_ge(n.s_tb,b+1)
    act.dma_start(d["T"].rearrange("(t p) c -> p t c",p=P)[:,bass.ds(b*TILES,TILES),:],n.TB[:,:,:]).then_inc(n.t_st,16)
    act.dma_start(d["ADT"].rearrange("(t p) c -> p t c",p=P)[:,bass.ds(b*TILES,TILES),:],n.ADB[:,:,:]).then_inc(n.t_st,16)
    barrier(act,n,"act",b,3)
def gat_pe(pe,n,PSB,ident,b):
    Ln.pe(pe,n,PSB,ident,b*4+3)
    pe.wait_ge(n.ln_cp,b*32+32)
    for t in range(TILES):
        last=pe.matmul(PSB[:,16*t:16*t+16],n.XPAD[:,P*t:P*(t+1)],n.WG[:,:],start=True,stop=True)
    last.then_inc(n.s_gt,1)
    barrier(pe,n,"pe",b,3)

P=128; NODES=16384; NT=NODES//P; COLS=4096; CH=64; NCH=COLS//CH; BIG=1e30; OUT_OF_RANGE=float(2**20)
IOA=bass.IndirectOffsetOnAxis

def declare_nodes(nc,ctx,n,SA):
    def sem(name):
        s=ctx.enter_context(nc.semaphore(name)); return s
    def sb(name,shape,dt=f32):
        t=ctx.enter_context(nc.sbuf_tensor(name,shape,dt)); return t
    n.np_mm, n.np_rdy, n.ad_ld, n.ad_sc, n.d0_rdy, n.d0_g = [sem(s) for s in ("np_mm", "np_rdy", "ad_ld", "ad_sc", "d0_rdy", "d0_g",)]
    n.d0_st, n.a2_ld, n.keep_rdy, n.fw_rdy, n.fw_exp, n.rb_rdy = [sem(s) for s in ("d0_st", "a2_ld", "keep_rdy", "fw_rdy", "fw_exp", "rb_rdy",)]
    n.lc_sh, n.lc_shd, n.lc_in, n.lc_tr, n.lc_e, n.lc_ee = [sem(s) for s in ("lc_sh", "lc_shd", "lc_in", "lc_tr", "lc_e", "lc_ee",)]
    n.lc_o, n.lc_t2, n.lc_tab, n.lc_st, n.tbn_ld, n.re_g = [sem(s) for s in ("lc_o", "lc_t2", "lc_tab", "lc_st", "tbn_ld", "re_g",)]
    n.ce_g, n.nd1, n.nd1e, n.nd2, n.nd2e, n.nd3 = [sem(s) for s in ("ce_g", "nd1", "nd1e", "nd2", "nd2e", "nd3",)]
    n.nd3e, n.g_rdy, n.moe_w, n.moe_h, n.moe_ge, n.moe_y = [sem(s) for s in ("nd3e", "g_rdy", "moe_w", "moe_h", "moe_ge", "moe_y",)]
    n.moe_dv, = [sem(s) for s in ("moe_dv",)]
    n.rbs=[sem(f"rbs{i}") for i in range(2)]; n.moe_ys=[sem(f"moe_ys{i}") for i in range(2)]
    n.gath=[sem(f"gath{i}") for i in range(2)]; n.gst=[sem(f"gst{i}") for i in range(2)]; n.adc=[sem(f"adc{i}") for i in range(2)]; n.rst=[sem(f"rst{i}") for i in range(2)]
    n.moe_in=[sem(f"moe_in{i}") for i in range(2)]; n.moe_out=[sem(f"moe_out{i}") for i in range(2)]
    n.SIX=sb("SIX",[P,NT],i32); n.EIX=sb("EIX",[P,NT],i32); n.PIX=sb("PIX",[P,NT],i32); n.VAL=sb("VAL",[P,NT]); n.MUL=sb("MUL",[P,NT]); n.NSF=sb("NSF",[P,NT]); n.NT1=sb("NT1",[P,NT]); n.NT2=sb("NT2",[P,NT],i32)
    n.D0=sb("D0",[P,1],i32); n.AD0=sb("AD0",[P,4]); n.GIX=[sb(f"GIX{i}",[P,CH],i32) for i in range(2)]
    n.IDW=sb("IDW",[P,P+1]); n.LCM=sb("LCM",[P,3,20]); n.LCD=sb("LCD",[P,4]); n.LCT=sb("LCT",[20,3,P]); n.MCX=sb("MCX",[20,P+1]); n.SCX=sb("SCX",[20,P+1]); n.LCE=sb("LCE",[20,2,P]); n.CTB=sb("CTB",[P,24])
    n.G4=sb("G4",[P,NT,4]); n.BG=sb("BG",[P,16]); n.GM=sb("GM",[P,16]); n.BT=sb("BT",[P,16])
    A=n.HTL[:,:,:,:].rearrange("p a b c -> p (a b c)")
    n.G=A[:,0:2560].rearrange("p (s c k) -> p s c k",s=2,k=20)
    n.ADC=A[:,2560:3072].rearrange("p (s c k) -> p s c k",s=2,k=4)
    n.ADX=A[:,3072:3584].rearrange("p (s c k) -> p s c k",s=2,k=4)
    X=n.XPAD[:,:]
    n.RB=X[:,0:3120].rearrange("p (s c k) -> p s c k",s=2,k=24)
    n.EE=X[:,3120:3632].rearrange("p (s c k) -> p s c k",s=2,k=4)
    n.PEN=X[:,3632:3760].rearrange("p (s c) -> p s c",s=2)
    n.FW=n.KPAD[:,2048:3072].rearrange("p (s f c k) -> p s f c k",s=2,f=2,k=4)
    n.V=n.KPAD[:,0:2048].rearrange("p (s c k) -> p s c k",s=2,k=16)
    n.RE=n.VPAD[:,0:3072].rearrange("p (t k) -> p t k",k=24)
    n.CE=n.KPAD[:,0:3072].rearrange("p (t k) -> p t k",k=24)
    n.TBN=SA[:,0:2560].rearrange("p (t k) -> p t k",k=20)
    n.ADN=n.VPAD[:,3072:3584].rearrange("p (t k) -> p t k",k=4)
    n.HM2=SA[:,0:8192].rearrange("p (s m c) -> p s m c",s=2,m=8)
    n.TNC=X[:,0:1024].rearrange("p (s c) -> p s c",s=2)
    n.X3C=X[:,1024:2048].rearrange("p (s t c) -> p s t c",s=2,t=4)
    n.WM1=A[:,1024:2048].rearrange("p (e c) -> p e c",e=4)
    n.WM2=A[:,2048:3072].rearrange("p (m c) -> p m c",m=8)
    n.B1M=A[:,3072:3080]; n.B2M=A[0:1,3584:4096]

def pos_pe(pe,n,PSB,ltri,ones,cnt):
    pe.matmul(PSB[:,0:P],ltri,cnt,start=True,stop=True)
    pe.matmul(PSB[:,P:2*P],ones,cnt,start=True,stop=True).then_inc(n.np_mm,1)
def pos_dve(dve,n,PSB,ones,cnt):
    dve.wait_ge(n.np_mm,1)
    dve.tensor_tensor_scan(n.NSF[:,:],ones,PSB[:,P:2*P],0.0,ALU.mult,ALU.add); dve.drain()
    dve.tensor_tensor(n.NSF[:,:],n.NSF[:,:],PSB[:,P:2*P],ALU.subtract); dve.drain()
    dve.tensor_tensor(n.NSF[:,:],n.NSF[:,:],PSB[:,0:P],ALU.add)
    dve.tensor_scalar(n.VAL[:,:],cnt,0.0,None,ALU.is_gt)
    dve.tensor_scalar(n.NT1[:,:],cnt,0.0,OUT_OF_RANGE,ALU.is_equal,ALU.mult); dve.drain()
    dve.tensor_tensor(n.SIX[:,:],n.NSF[:,:],n.NT1[:,:],ALU.add); dve.drain()
    dve.tensor_tensor(n.NT1[:,:],n.NSF[:,:],cnt,ALU.add); dve.drain()
    dve.tensor_scalar(n.EIX[:,:],n.NT1[:,:],-1.0,0.0,ALU.add,ALU.max)
    dve.tensor_copy(n.NT2[:,:],n.NSF[:,:]); dve.drain()
    dve.tensor_scalar(n.NT2[:,:],n.NT2[:,:],12,None,ALU.logical_shift_right)
    dve.tensor_scalar(n.PIX[:,:],n.EIX[:,:],12,None,ALU.logical_shift_right); dve.drain()
    dve.tensor_tensor(n.MUL[:,:],n.NT2[:,:],n.PIX[:,:],ALU.not_equal); dve.drain()
    dve.tensor_tensor(n.MUL[:,:],n.MUL[:,:],n.VAL[:,:],ALU.mult).then_inc(n.np_rdy,1)

def edges_prep_dve(dve,n,SA):
    I=SA.bitcast(i32)
    s=lambda t,i: t[:,i*4096:(i+1)*4096]
    dve.wait_ge(n.a2_ld,16)
    dve.tensor_scalar(s(I,4),s(I,0),32767,None,ALU.bitwise_and)
    dve.tensor_scalar(s(I,1),s(I,0),15,None,ALU.logical_shift_right); dve.drain()
    dve.tensor_copy(s(SA,2),s(I,4)); dve.drain()
    d=s(SA,2); k=s(SA,4)
    dve.tensor_scalar(n.D0[:,:],d[:,0:1],float(NODES-1),None,ALU.min).then_inc(n.d0_rdy,1)
    dve.tensor_tensor(k[:,1:],d[:,1:],d[:,0:COLS-1],ALU.is_equal)
    dve.memset(k[:,0:1],0.0); dve.drain()
    dve.memset(n.ADX[:,1,:,:],0.0)
    dve.memset(n.RB[:,1,CH,0:4],-BIG); dve.memset(n.RB[:,1,CH,4:24],0.0)
    dve.drain()
    dve.tensor_copy(n.LCD[:,0:1],d[:,0:1]); dve.tensor_copy(n.LCD[:,1:2],d[:,COLS-1:COLS]).then_inc(n.keep_rdy,1)
    dve.drain()
def edges_dve(dve,n,SA):
    k_=SA[:,4*4096:5*4096]
    with dve.Fori(0,NCH//2) as i:
        for s in range(2):
            j=i*2+s
            G=n.G[:,s]; K=k_[:,bass.ds(j*CH,CH)]; RB=n.RB[:,s]; E=n.EE[:,s]; PEN=n.PEN[:,s,:]; FW=n.FW[:,s]
            dve.wait_ge(n.rst[s],i*16)
            dve.tensor_copy(RB[:,0,:],n.RB[:,1-s,CH,:])
            dve.tensor_scalar(PEN,K,-1.0,BIG,ALU.add,ALU.mult)
            dve.wait_ge(n.adc[s],i*16+16)
            for h in range(4):
                dve.tensor_tensor_scan(n.ADX[:,s,:,h],K,n.ADC[:,s,:,h],n.ADX[:,1-s,CH-1,h:h+1],ALU.mult,ALU.add)
            dve.drain()
            dve.wait_ge(n.gath[s],i*(CH*16)+CH*16)
            dve.tensor_tensor(E,G[:,:,16:20],n.ADX[:,s],ALU.add); dve.drain()
            dve.scalar_tensor_tensor(out=E,in0=E,scalar=0.2,in1=E,op0=ALU.mult,op1=ALU.max); dve.drain()
            for h in range(4):
                dve.tensor_tensor_scan(RB[:,1:CH+1,h],PEN,E[:,:,h],RB[:,0,h:h+1],ALU.add,ALU.max)
            dve.drain()
            dve.tensor_tensor(FW[:,0],RB[:,0:CH,0:4],PEN.unsqueeze(2).to_broadcast((P,CH,4)),ALU.add)
            dve.tensor_tensor(FW[:,1],E,RB[:,1:CH+1,0:4],ALU.subtract); dve.drain()
            dve.tensor_tensor(FW[:,0],FW[:,0],RB[:,1:CH+1,0:4],ALU.subtract).then_inc(n.fw_rdy,1)
            dve.wait_ge(n.fw_exp,j+1)
            dve.tensor_tensor(n.V[:,s].rearrange("p c (h e) -> p c h e",h=4),G[:,:,0:16].rearrange("p c (h e) -> p c h e",h=4),FW[:,1].unsqueeze(3).to_broadcast((P,CH,4,4)),ALU.mult)
            for h in range(4):
                last=dve.tensor_tensor_scan(RB[:,1:CH+1,4+h],FW[:,0,:,h],FW[:,1,:,h],RB[:,0,4+h:5+h],ALU.mult,ALU.add)
            dve.drain()
            for c in range(16):
                last=dve.tensor_tensor_scan(RB[:,1:CH+1,8+c],FW[:,0,:,c//4],n.V[:,s,:,c],RB[:,0,8+c:9+c],ALU.mult,ALU.add)
            last.then_inc(n.rbs[s],1)
            dve.drain()
def edges_act(act,n,d):
    R=d["R"].rearrange("(p c) k -> p c k",p=P)
    with act.Fori(0,NCH//2) as i:
        for s in range(2):
            j=i*2+s
            act.wait_ge(n.fw_rdy,j+1)
            act.activation(n.FW[:,s],n.FW[:,s],ACT.Exp).then_inc(n.fw_exp,1)
            act.wait_ge(n.rbs[s],i+1)
            act.dma_start(R[:,bass.ds(j*CH,CH),:],n.RB[:,s,1:CH+1,:]).then_inc(n.rst[s],16)
def edges_pool(pool,n,d,tick,ADS):
    for t in range(NT):
        if t==0: pool.wait_ge(n.np_rdy,1); pool.wait_ge(n.ad_ld,16)
        pool.indirect_dma_start(out=d["AEXP"],out_offset=IOA(ap=n.SIX[:,t:t+1],axis=0),in_=n.ADN[:,t,:],in_offset=None,bounds_check=4096*128-1,oob_is_err=False).then_inc(n.ad_sc,16)
    pool.wait_ge(n.d0_rdy,1)
    pool.indirect_dma_start(out=n.AD0[:,:],out_offset=None,in_=d["ADT"],in_offset=IOA(ap=n.D0[:,:],axis=0)).then_inc(n.d0_g,16)
    with pool.Fori(0,NCH//2) as i:
        for s in range(2):
            pool.wait_ge(n.gst[s],i*16+16); pool.sem_inc(tick,1)
            pool.wait_ge(n.rbs[s],i); pool.sem_inc(tick,1)
            for c in range(CH):
                pool.indirect_dma_start(out=n.G[:,s,c,:],out_offset=None,in_=d["T"],in_offset=IOA(ap=n.GIX[s][:,c:c+1],axis=0)).then_inc(n.gath[s],16)
    pool.wait_ge(n.rst[0],NCH//2*16); pool.wait_ge(n.rst[1],NCH//2*16)
    for t in range(NT):
        pool.indirect_dma_start(out=n.RE[:,t,:],out_offset=None,in_=d["R"],in_offset=IOA(ap=n.EIX[:,t:t+1],axis=0)).then_inc(n.re_g,16)
    pool.wait_ge(n.lc_st,16)
    for t in range(NT):
        pool.indirect_dma_start(out=n.CE[:,t,:],out_offset=None,in_=d["CT"],in_offset=IOA(ap=n.PIX[:,t:t+1],axis=0)).then_inc(n.ce_g,16)
def edges_sync(sp,n,d,SA,tick,A2):
    I=SA.bitcast(i32)
    sp.dma_start(n.ADN,d["ADT"].rearrange("(t p) c -> p t c",p=P)).then_inc(n.ad_ld,16)
    sp.dma_start(I[:,0:4096],A2.rearrange("(p c) o -> p (c o)",p=P)).then_inc(n.a2_ld,16)
    sp.wait_ge(n.keep_rdy,1)
    sp.dma_start(n.TBN,d["T"].rearrange("(t p) c -> p t c",p=P)).then_inc(n.tbn_ld,16)
    for t,k in ((n.BG,"b_gat"),(n.GM,"gamma"),(n.BT,"beta")):
        sp.dma_start(t[:,:],d[k].rearrange("(a n) -> a n",a=1).to_broadcast((P,16))).then_inc(n.tbn_ld,16)
    sp.wait_ge(n.ad_sc,16*NT); sp.wait_ge(n.d0_g,16)
    A=d["AEXP"].rearrange("(p c) k -> p c k",p=P)
    sp.dma_start(A[:,0,:],n.AD0[:,:]).then_inc(n.d0_st,16)
    sp.wait_ge(n.d0_st,16); sp.wait_ge(n.keep_rdy,1)
    with sp.Fori(0,NCH//2) as i:
        for s in range(2):
            j=i*2+s
            sp.wait_ge(n.gath[s],i*(CH*16)); sp.sem_inc(tick,1)
            sp.dma_start(n.GIX[s][:,:],I[:,bass.ds(j*CH+4096,CH)]).then_inc(n.gst[s],16)
            sp.wait_ge(n.rbs[s],i); sp.sem_inc(tick,1)
            sp.dma_start(n.ADC[:,s],A[:,bass.ds(j*CH,CH),:]).then_inc(n.adc[s],16)
def carry_dve(dve,n,PSB):
    L=n.RB[:,1,CH,:]
    dve.wait_ge(n.lc_sh,1)
    dve.tensor_tensor(n.LCD[:,2:3],n.LCD[:,0:1],n.LCD[:,1:2],ALU.is_equal)
    dve.tensor_tensor(n.LCD[:,3:4],n.LCD[:,0:1],PSB[:,0:1],ALU.is_equal); dve.drain()
    dve.tensor_tensor(n.LCD[:,2:3],n.LCD[:,2:3],n.LCD[:,3:4],ALU.mult); dve.drain()
    dve.tensor_scalar(n.LCD[:,3:4],n.LCD[:,2:3],-1.0,BIG,ALU.add,ALU.mult); dve.drain()
    dve.tensor_copy(n.LCM[:,2,:],n.LCD[:,3:4].to_broadcast((P,20)))
    dve.tensor_copy(n.LCM[:,0,0:4],L[:,0:4])
    dve.tensor_copy(n.LCM[:,0,4:20].rearrange("p (h e) -> p h e",h=4),L[:,0:4].unsqueeze(2).to_broadcast((P,4,4)))
    dve.tensor_copy(n.LCM[:,1,:],L[:,4:24]).then_inc(n.lc_in,1)
    dve.memset(n.MCX[:,0:1],-BIG); dve.memset(n.SCX[:,0:1],0.0)
    dve.wait_ge(n.lc_tr,1)
    dve.tensor_copy(n.LCT[:,:,:],PSB[0:20,0:384].rearrange("p (a c) -> p a c",a=3)); dve.drain()
    lm,ls,pc=(n.LCT[:,i,:] for i in range(3))
    dve.tensor_tensor_scan(n.MCX[:,1:],pc,lm,-BIG,ALU.add,ALU.max); dve.drain()
    dve.tensor_tensor(n.LCE[:,0,:],n.MCX[:,0:P],pc,ALU.add)
    dve.tensor_tensor(n.LCE[:,1,:],lm,n.MCX[:,1:],ALU.subtract); dve.drain()
    dve.tensor_tensor(n.LCE[:,0,:],n.LCE[:,0,:],n.MCX[:,1:],ALU.subtract).then_inc(n.lc_e,1)
    dve.wait_ge(n.lc_ee,1)
    dve.tensor_tensor(n.LCE[:,1,:],n.LCE[:,1,:],ls,ALU.mult); dve.drain()
    dve.tensor_tensor_scan(n.SCX[:,1:],n.LCE[:,0,:],n.LCE[:,1,:],0.0,ALU.mult,ALU.add).then_inc(n.lc_o,1)
    dve.wait_ge(n.lc_t2,1)
    dve.tensor_copy(n.CTB[:,0:4],PSB[:,0:4]); dve.tensor_copy(n.CTB[:,4:24],PSB[:,20:40]).then_inc(n.lc_tab,1)
def carry_pe(pe,n,PSB,ident):
    pe.wait_ge(n.rbs[0],NCH//2); pe.wait_ge(n.rbs[1],NCH//2)
    pe.matmul(PSB[:,0:1],n.IDW[:,0:P],n.LCD[:,1:2],start=True,stop=True).then_inc(n.lc_sh,1)
    pe.wait_ge(n.lc_in,1)
    for i in range(3): last=pe.transpose(PSB[0:20,i*P:(i+1)*P],n.LCM[:,i,:],ident)
    last.then_inc(n.lc_tr,1)
    pe.wait_ge(n.lc_o,1)
    pe.transpose(PSB[:,0:20],n.MCX[:,0:P],ident[0:20,0:20])
    pe.transpose(PSB[:,20:40],n.SCX[:,0:P],ident[0:20,0:20]).then_inc(n.lc_t2,1)
def carry_act(act,n,d):
    act.wait_ge(n.lc_e,1)
    act.activation(n.LCE[:,:,:],n.LCE[:,:,:],ACT.Exp).then_inc(n.lc_ee,1)
    act.wait_ge(n.lc_tab,1)
    act.dma_start(d["CT"],n.CTB[:,:]).then_inc(n.lc_st,16)
def node_dve(dve,n,SA):
    o=[4096]
    def tmp(k):
        a=SA[:,o[0]:o[0]+NT*k]; o[0]+=NT*k
        return a.rearrange("p (t k) -> p t k",k=k)
    mE,mC,mS,M=tmp(4),tmp(4),tmp(4),tmp(4); DEN=tmp(4); MSG=tmp(16); T16=tmp(16); SC=tmp(4); MN=tmp(1); VR=tmp(1); I1=tmp(4); I2=tmp(4); M1=tmp(1); M2=tmp(1); FR=tmp(1); T1=tmp(1)
    dr=dve.drain
    b1=lambda a,k: a.to_broadcast((P,NT,k))
    h4=lambda a: a.rearrange("p t (h e) -> p t h e",h=4)
    be=lambda a: a.unsqueeze(3).to_broadcast((P,NT,4,4))
    dve.wait_ge(n.tbn_ld,16*4); dve.wait_ge(n.ad_ld,16)
    dve.tensor_tensor(mS,n.TBN[:,:,16:20],n.ADN[:,:,:],ALU.add)
    dve.tensor_scalar(n.VAL[:,:],n.VAL[:,:],-1.0,BIG,ALU.add,ALU.mult); dve.tensor_scalar(n.MUL[:,:],n.MUL[:,:],-1.0,BIG,ALU.add,ALU.mult); dr()
    dve.scalar_tensor_tensor(out=mS,in0=mS,scalar=0.2,in1=mS,op0=ALU.mult,op1=ALU.max)
    dve.wait_ge(n.re_g,16*NT)
    dve.tensor_tensor(mE,n.RE[:,:,0:4],n.VAL[:,:].unsqueeze(2).to_broadcast((P,NT,4)),ALU.add)
    dve.wait_ge(n.ce_g,16*NT)
    dve.tensor_tensor(mC,n.CE[:,:,0:4],n.MUL[:,:].unsqueeze(2).to_broadcast((P,NT,4)),ALU.add); dr()
    dve.tensor_tensor(M,mE,mC,ALU.max); dr()
    dve.tensor_tensor(M,M,mS,ALU.max); dr()
    for a in (mE,mC): dve.tensor_tensor(a,a,M,ALU.subtract)
    dve.tensor_tensor(mS,mS,M,ALU.subtract).then_inc(n.nd1,1)
    dve.wait_ge(n.nd1e,1)
    dve.tensor_tensor(DEN,n.RE[:,:,4:8],mE,ALU.mult)
    dve.tensor_tensor(M,n.CE[:,:,4:8],mC,ALU.mult)
    dve.tensor_tensor(h4(MSG),h4(n.RE[:,:,8:24]),be(mE),ALU.mult)
    dve.tensor_tensor(h4(T16),h4(n.CE[:,:,8:24]),be(mC),ALU.mult); dr()
    dve.tensor_tensor(DEN,DEN,M,ALU.add); dve.tensor_tensor(MSG,MSG,T16,ALU.add); dr()
    dve.tensor_tensor(DEN,DEN,mS,ALU.add); dve.tensor_tensor(h4(T16),h4(n.TBN[:,:,0:16]),be(mS),ALU.mult); dr()
    dve.tensor_tensor(MSG,MSG,T16,ALU.add); dve.tensor_scalar(DEN,DEN,1e-16,None,ALU.add); dr()
    dve.reciprocal(DEN,DEN); dr()
    dve.tensor_tensor(h4(MSG),h4(MSG),be(DEN),ALU.mult); dr()
    bc=lambda a: a[:,:].unsqueeze(1).to_broadcast((P,NT,16))
    dve.tensor_tensor(MSG,MSG,bc(n.BG),ALU.add); dr()
    dve.tensor_reduce(MN,MSG,AX.X,ALU.add); dr()
    dve.tensor_scalar(MN,MN,1.0/16,None,ALU.mult); dr()
    dve.tensor_tensor(MSG,MSG,b1(MN,16),ALU.subtract); dr()
    dve.tensor_tensor(T16,MSG,MSG,ALU.mult); dr()
    dve.tensor_reduce(VR,T16,AX.X,ALU.add); dr()
    dve.tensor_scalar(VR,VR,1.0/16,1e-5,ALU.mult,ALU.add).then_inc(n.nd2,1)
    dve.wait_ge(n.nd2e,1)
    dve.reciprocal(VR,VR); dr()
    dve.tensor_tensor(MSG,MSG,b1(VR,16),ALU.mult); dr()
    dve.tensor_tensor(MSG,MSG,bc(n.GM),ALU.mult); dr()
    dve.tensor_tensor(MSG,MSG,bc(n.BT),ALU.add); dr()
    dve.tensor_reduce(SC,MSG.rearrange("p t (h e) -> p t e h",h=4),AX.X,ALU.add); dr()
    dve.tensor_scalar(SC,SC,0.25,None,ALU.mult); dr()
    def first(mx,ind):
        dve.tensor_reduce(mx,SC,AX.X,ALU.max); dr()
        dve.tensor_tensor(ind,SC,b1(mx,4),ALU.is_equal)
        dve.memset(FR,1.0); dr()
        for e in range(4):
            dve.tensor_tensor(ind[:,:,e:e+1],ind[:,:,e:e+1],FR,ALU.mult); dr()
            dve.tensor_tensor(FR,FR,ind[:,:,e:e+1],ALU.subtract); dr()
    first(M1,I1)
    dve.tensor_scalar(T16[:,:,0:4],I1,-3e38,None,ALU.mult); dr()
    dve.tensor_tensor(SC,SC,T16[:,:,0:4],ALU.add); dr()
    first(M2,I2)
    dve.tensor_tensor(T1,M2,M1,ALU.subtract).then_inc(n.nd3,1)
    dve.wait_ge(n.nd3e,1)
    dve.tensor_scalar(M1,T1,1.0,None,ALU.add); dr()
    dve.reciprocal(M1,M1); dr()
    dve.tensor_tensor(M2,T1,M1,ALU.mult); dr()
    dve.tensor_tensor(I1,I1,b1(M1,4),ALU.mult); dve.tensor_tensor(I2,I2,b1(M2,4),ALU.mult); dr()
    dve.tensor_tensor(n.G4[:,:,:],I1,I2,ALU.add).then_inc(n.g_rdy,1)
    dr()
def node_act(act,n,SA):
    o=4096
    act.wait_ge(n.nd1,1)
    act.activation(SA[:,o:o+NT*12],SA[:,o:o+NT*12],ACT.Exp).then_inc(n.nd1e,1)
    act.wait_ge(n.nd2,1)
    vr=o+NT*(4*5+32+4+1)
    act.activation(SA[:,vr:vr+NT],SA[:,vr:vr+NT],ACT.Sqrt).then_inc(n.nd2e,1)
    t1=vr+NT*(1+8+3)
    act.wait_ge(n.nd3,1)
    act.activation(SA[:,t1:t1+NT],SA[:,t1:t1+NT],ACT.Exp).then_inc(n.nd3e,1)
NCK=NODES//512
def moe_sync(sp,n,d,tick):
    sp.wait_ge(n.rbs[0],NCH//2); sp.wait_ge(n.rbs[1],NCH//2)
    for dst,k in ((n.WM1,"W1"),(n.WM2,"W2"),(n.B1M,"b1mT"),(n.B2M,"b2m")):
        src=d[k]
        if k=="W1": src=src.rearrange("e c h -> c e h")
        if k=="W2": src=src.rearrange("e (f p) o -> p (e f) o",p=P)
        if k=="b2m": src=src.rearrange("e c -> (e c)").rearrange("(a n) -> a n",a=1)
        sp.dma_start(dst,src).then_inc(n.moe_w,16)
    x3=d["X3"].rearrange("(t p) c -> p t c",p=P)
    sp.wait_ge(n.g_rdy,1)
    with sp.Fori(0,NCK//2) as i:
        for s in range(2):
            j=i*2+s
            sp.wait_ge(n.moe_out[s],i*16); sp.sem_inc(tick,1)
            sp.dma_start(n.TNC[:,s,:],d["TNT"][:,bass.ds(j*512,512)]).then_inc(n.moe_in[s],16)
            sp.dma_start(n.X3C[:,s],x3[:,bass.ds(j*4,4),:]).then_inc(n.moe_in[s],16)
def moe_pe(pe,n,PSB,ones):
    pe.wait_ge(n.moe_w,64)
    with pe.Fori(0,NCK//2) as i:
        for s in range(2):
            j=i*2+s
            pe.wait_ge(n.moe_in[s],i*32+32)
            for m in range(8):
                (pe.wait_ge(n.moe_ge,j*8+(m-3)) if m>=4 else None)
                pe.matmul(PSB[:,(m%4)*512:(m%4+1)*512],n.WM1[:,m//2,(m%2)*P:(m%2+1)*P],n.TNC[:,s,:],start=True,stop=True).then_inc(n.moe_h,1)
            for t in range(4):
                if t==0: pe.wait_ge(n.moe_ge,j*8+8); pe.wait_ge(n.moe_dv,j*4)
                o=PSB[:,(4+t)*512:(5+t)*512]
                pe.matmul(o,ones[0:1,:],n.B2M,start=True,stop=False,skip_group_check=True)
                for m in range(8):
                    last=pe.matmul(PSB[:,(4+t)*512+(m//2)*P:(4+t)*512+(m//2+1)*P],n.HM2[:,s,m,P*t:P*(t+1)],n.WM2[:,m,:],start=False,stop=(m==7),skip_group_check=True)
                last.then_inc(n.moe_ys[s],1)
def moe_act(act,n,PSB):
    act.wait_ge(n.moe_w,64)
    with act.Fori(0,NCK//2) as i:
        for s in range(2):
            j=i*2+s
            for m in range(8):
                act.wait_ge(n.moe_h,j*8+(m+1))
                if m==0: act.wait_ge(n.moe_ys[s],i*4)
                act.activation(n.HM2[:,s,m,:],PSB[:,(m%4)*512:(m%4+1)*512],ACT.Gelu,bias=n.B1M[:,m:m+1]).then_inc(n.moe_ge,1)
def moe_pool(pool,n,out,tick):
    o=out.rearrange("(t p) c -> p t c",p=P)
    with pool.Fori(0,NCK//2) as i:
        for s in range(2):
            j=i*2+s
            pool.wait_ge(n.moe_dv,j*4+4); pool.sem_inc(tick,1)
            pool.dma_start(o[:,bass.ds(j*4,4),:],n.X3C[:,s]).then_inc(n.moe_out[s],16)
    for s in range(2): pool.wait_ge(n.moe_out[s],NCK//2*16)
def moe_dve(dve,n,PSB):
    with dve.Fori(0,NCK//2) as i:
        for s in range(2):
            j=i*2+s
            for t in range(4):
                dve.wait_ge(n.moe_ys[s],i*4+(t+1))
                for e in range(4):
                    x=n.X3C[:,s,t,:]
                    last=dve.scalar_tensor_tensor(out=x,in0=PSB[:,(4+t)*512+e*P:(4+t)*512+(e+1)*P],scalar=n.G4[:,bass.ds(j*4+t,1),e],in1=x,op0=ALU.mult,op1=ALU.add)
                    if e<3: dve.drain()
                last.then_inc(n.moe_dv,1)

EDGES=524288; SEGS=8; STEPS=COLS//SEGS; INVALID=NODES; DIG=128
NI=STEPS//4; ROUNDS=NI//2

def declare_sort(nc,ctx):
    class N: pass
    m=N()
    def sb(name,shape,dt=f32):
        t=ctx.enter_context(nc.sbuf_tensor(name,shape,dt)); return t
    def sem(name):
        s=ctx.enter_context(nc.semaphore(name)); return s
    m.SA=sb("SA_",[P,5*COLS])[:,:]; m.SI=m.SA.bitcast(i32)
    m.S=[m.SA[:,i*COLS:(i+1)*COLS] for i in range(5)]; m.SJ=[m.SI[:,i*COLS:(i+1)*COLS] for i in range(5)]
    m.SB=sb("SB_",[P,5120])[:,:]
    SBb=m.SB.bitcast(bf16)
    oh=lambda i: SBb[:,i*2048:(i+1)*2048].rearrange("p (u s v) -> p u s v",u=2,s=SEGS)
    m.OHL,m.OHH,m.junk=oh(0),oh(1),oh(2)
    m.Tc=m.SB[:,3072:4096].rearrange("p (s v) -> p s v",s=SEGS); m.INI=m.SB[:,4096:5120].rearrange("p (s v) -> p s v",s=SEGS)
    m.ident,m.ltri,m.ones,m.iotaf,m.tot,m.TT,m.cnt=[sb(t,[P,P]) for t in ("ident","ltri","ones","iotaf","tot","TT","cnt")]
    m.identb=sb("identb",[P,P],bf16); m.iotab=sb("iotab",[P,P],bf16); m.zb=sb("zb",[P,512],bf16); m.big=sb("big",[P,SEGS,4]); m.fill=sb("fill",[P,512],i32); m.zero=sb("zero",[P,512])
    m.IX=[sb(f"IX{i}",[P,32],i32) for i in range(2)]; m.PY=[sb(f"PY{i}",[P,32],i32) for i in range(2)]
    m.c_load, m.e_load, m.fill_rdy, m.fill_done, m.const_rdy, m.oh_rdy = [sem(s) for s in ("c_load", "e_load", "fill_rdy", "fill_done", "const_rdy", "oh_rdy",)]
    m.oh_free, m.hist_done, m.tt_rdy, m.lt_done, m.ini_rdy, m.accA = [sem(s) for s in ("oh_free", "hist_done", "tt_rdy", "lt_done", "ini_rdy", "accA",)]
    m.accB, m.exA, m.exB, m.pos_rdy, m.re_load, m.tick_sp = [sem(s) for s in ("accB", "exA", "exB", "pos_rdy", "re_load", "tick_sp",)]
    m.tick_pool, m.o_sem = [sem(s) for s in ("tick_pool", "o_sem",)]
    m.staged=[sem(f"staged{i}") for i in range(2)]; m.scat=[[sem(f"scat{r}{i}") for i in range(2)] for r in range(2)]
    return m

def sort_sync_loads(sp,m,d):
    for t,src in ((m.ident,"ident"),(m.ltri,"ltri"),(m.iotaf,"iota")):
        sp.dma_start(t[:,:],d[src]).then_inc(m.c_load,16)
    sp.dma_start(m.SJ[4],d["edges"][0].rearrange("(p c) -> p c",p=P)).then_inc(m.e_load,16)
    sp.dma_start(m.SJ[1],d["edges"][1].rearrange("(p c) -> p c",p=P)).then_inc(m.e_load,16)
def sort_sync_fill(sp,m,d):
    sp.wait_ge(m.fill_rdy,2)
    for A in ("A1","A2"):
        a=d[A].rearrange("(q p c) o -> q p (c o)",p=P,c=512)
        for q in range(EDGES//(P*512)): sp.dma_start(a[q],m.fill[:,:]).then_inc(m.fill_done,16)
    a=d["AEXP"].rearrange("(p c) k -> p (c k)",p=P)
    for q in range(32): sp.dma_start(a[:,512*q:512*(q+1)],m.zero[:,:]).then_inc(m.fill_done,16)
FILLS=16*(2*EDGES//(P*512)+32)
def sort_sync(sp,m,d,r):
    if r==1:
        for s in range(2): sp.wait_ge(m.scat[0][s],512*ROUNDS)
        sp.dma_start(m.SJ[0],d["A1"].rearrange("(p c) o -> p (c o)",p=P)).then_inc(m.re_load,16)
    pk=m.SJ[0].rearrange("p (s k) -> p s k",s=SEGS); ps=m.SJ[1].rearrange("p (s k) -> p s k",s=SEGS)
    with sp.Fori(0,ROUNDS) as i:
        for s in range(2):
            g=i*2+s
            sp.wait_ge(m.pos_rdy,g+(r*NI+1)); sp.sem_inc(m.tick_sp,1)
            sp.wait_ge(m.scat[r][s],i*512); sp.sem_inc(m.tick_sp,1)
            sp.dma_start(m.IX[s][:,:],ps[:,:,bass.ds(g*4,4)]).then_inc(m.staged[s],16)
            sp.dma_start(m.PY[s][:,:],pk[:,:,bass.ds(g*4,4)]).then_inc(m.staged[s],16)
def sort_pool(pool,m,d,r):
    if r==0: pool.wait_ge(m.fill_done,FILLS)
    A=d[("A1","A2")[r]]
    with pool.Fori(0,ROUNDS) as i:
        for s in range(2):
            pool.wait_ge(m.staged[s],i*32+(r*ROUNDS*32+32)); pool.sem_inc(m.tick_pool,1)
            for c in range(32):
                pool.indirect_dma_start(out=A,out_offset=IOA(ap=m.IX[s][:,c:c+1],axis=0),in_=m.PY[s][:,c:c+1],in_offset=None,bounds_check=EDGES-1,oob_is_err=False).then_inc(m.scat[r][s],16)
def sort_dve_prep(dve,m):
    S,SJ=m.S,m.SJ
    dve.memset(m.ones[:,:],1.0); dve.memset(m.zb[:,:],0.0)
    dve.wait_ge(m.c_load,48)
    dve.tensor_copy(m.identb[:,:],m.ident[:,:])
    dve.tensor_copy(m.iotab[:,:],m.iotaf[:,:]).then_inc(m.const_rdy,1)
    dve.wait_ge(m.e_load,32)
    dve.tensor_scalar(S[3],SJ[1],float(INVALID),None,ALU.min)
    dve.tensor_scalar(SJ[2],SJ[4],float(NODES-1),None,ALU.min); dve.drain()
    dve.tensor_copy(SJ[1],S[3])
    dve.tensor_scalar(SJ[0],SJ[2],15,None,ALU.logical_shift_left); dve.drain()
    dve.tensor_tensor(SJ[0],SJ[0],SJ[1],ALU.bitwise_or)
    dve.tensor_scalar(SJ[4],SJ[1],127,None,ALU.bitwise_and); dve.drain()
    dve.tensor_copy(S[2],SJ[4]); dve.drain()
    dve.tensor_scalar(S[4],S[3],float(INVALID),1000.0,ALU.is_ge,ALU.mult); dve.drain()
    dve.tensor_tensor(S[2],S[2],S[4],ALU.add); dve.drain()
    dve.tensor_scalar(SJ[4],SJ[1],7,None,ALU.logical_shift_right); dve.drain()
    dve.tensor_copy(S[3],SJ[4]); dve.drain()
def sort_dve(dve,m,PS,r):
    S,SJ=m.S,m.SJ
    if r==1:
        dve.wait_ge(m.re_load,16); dve.wait_ge(m.accA,STEPS+1); dve.wait_ge(m.accB,STEPS+1)
        for s in range(2): dve.wait_ge(m.staged[s],32*ROUNDS)
        dve.tensor_scalar(SJ[4],SJ[0],32767,7,ALU.bitwise_and,ALU.logical_shift_right); dve.drain()
        dve.tensor_copy(S[2],SJ[4]); dve.drain()
    with dve.Fori(0,STEPS//2) as i:
        for u in range(2):
            k=i*2+u
            dve.wait_ge(m.oh_free,k+(1+r*STEPS))
            for s in range(SEGS):
                last=dve.tensor_scalar(m.OHL[:,u,s,:],m.iotab[:,:],S[2][:,bass.ds(k+s*STEPS,1)],None,ALU.is_equal)
                if r==0: last=dve.tensor_scalar(m.OHH[:,u,s,:],m.iotab[:,:],S[3][:,bass.ds(k+s*STEPS,1)],None,ALU.is_equal)
            last.then_inc(m.oh_rdy,1)
    dve.wait_ge(m.hist_done,r+1)
    for b in range(2): dve.tensor_copy(m.Tc[:,4*b:4*b+4,:],PS[b].rearrange("p (s v) -> p s v",s=4))
    if r==0: dve.tensor_copy(m.cnt[:,:],PS[2][:,0:P])
    dve.drain()
    dve.tensor_reduce(m.TT[:,:],m.Tc.rearrange("p s v -> p v s"),AX.X,ALU.add).then_inc(m.tt_rdy,1)
    dve.wait_ge(m.lt_done,r+1)
    dve.tensor_tensor_scan(m.tot[:,:],m.ones[:,:],PS[3][:,P:2*P],0.0,ALU.mult,ALU.add); dve.drain()
    dve.tensor_tensor(m.tot[:,:],m.tot[:,:],PS[3][:,P:2*P],ALU.subtract); dve.drain()
    dve.tensor_tensor(m.INI[:,0,:],m.tot[:,:],PS[3][:,0:P],ALU.add)
    for s in range(1,SEGS):
        dve.drain()
        last=dve.tensor_tensor(m.INI[:,s,:],m.INI[:,s-1,:],m.Tc[:,s-1,:],ALU.add)
    last.then_inc(m.ini_rdy,1)
    with dve.Fori(0,NI) as i:
        for u in range(4):
            k=i*4+u
            dve.wait_ge(m.accA,k+(r*(STEPS+1))); dve.wait_ge(m.accB,k+(r*(STEPS+1)))
            for s in range(SEGS):
                last=dve.tensor_scalar(m.OHL[:,u%2,s,:],m.iotab[:,:],S[2][:,bass.ds(k+s*STEPS,1)],None,ALU.is_equal)
            last.then_inc(m.oh_rdy,1)
            for b in range(2):
                dve.wait_ge((m.accA,m.accB)[b],k+(1+r*(STEPS+1)))
                for s in range(4*b,4*b+4):
                    last=dve.scalar_tensor_tensor(out=m.junk[:,u%2,s,:],in0=m.iotab[:,:],scalar=S[2][:,bass.ds(k+s*STEPS,1)],in1=PS[b][:,(s%4)*DIG:(s%4+1)*DIG],op0=ALU.is_equal,op1=ALU.mult,accum_out=S[4][:,bass.ds(k+s*STEPS,1)])
                last.then_inc((m.exA,m.exB)[b],1)
        v=lambda t: t.rearrange("p (s k) -> p s k",s=SEGS)[:,:,bass.ds(i*4,4)]
        dve.tensor_scalar(m.big[:,:,:],v(S[2]),float(DIG),OUT_OF_RANGE,ALU.is_ge,ALU.mult)
        dve.drain()
        dve.tensor_tensor(v(SJ[1]),v(S[4]),m.big[:,:,:],ALU.add).then_inc(m.pos_rdy,1)
def sort_pe(pe,m,PS,r):
    if r==0: pe.wait_ge(m.const_rdy,1); pe.sem_inc(m.oh_free,2)
    if r==1: pe.wait_ge(m.pos_rdy,NI)
    for b in range(3): pe.matmul(PS[b],m.zb[:,0:P],m.zb[:,:],start=True,stop=True)
    with pe.Fori(0,STEPS//2) as i:
        for u in range(2):
            k=i*2+u
            pe.wait_ge(m.oh_rdy,k+(1+r*2*STEPS))
            if r==0:
                for s in range(SEGS): pe.matmul(PS[2][:,0:P],m.OHL[:,u,s,:],m.OHH[:,u,s,:],start=False,stop=True,skip_group_check=True)
            for b in range(2): last=pe.matmul(PS[b],m.identb[:,:],m.OHL[:,u,4*b:4*b+4,:],start=False,stop=True,skip_group_check=True)
            last.then_inc(m.oh_free,1)
    for b in range(3): last=pe.matmul(PS[b],m.zb[:,0:P],m.zb[:,:],start=False,stop=True,skip_group_check=True)
    last.then_inc(m.hist_done,1)
    pe.wait_ge(m.tt_rdy,r+1)
    pe.matmul(PS[3][:,0:P],m.ltri[:,:],m.TT[:,:],start=True,stop=True)
    pe.matmul(PS[3][:,P:2*P],m.ones[:,:],m.TT[:,:],start=True,stop=True).then_inc(m.lt_done,1)
    pe.wait_ge(m.ini_rdy,r+1)
    for b in range(2): pe.matmul(PS[b],m.ident[:,:],m.INI[:,4*b:4*b+4,:],start=True,stop=True).then_inc((m.accA,m.accB)[b],1)
    with pe.Fori(0,STEPS//2) as i:
        for u in range(2):
            k=i*2+u
            pe.wait_ge(m.oh_rdy,k+(1+STEPS+r*2*STEPS))
            for b in range(2):
                pe.wait_ge((m.exA,m.exB)[b],k+(1+r*STEPS))
                pe.matmul(PS[b],m.identb[:,:],m.OHL[:,u,4*b:4*b+4,:],start=False,stop=True,skip_group_check=True).then_inc((m.accA,m.accB)[b],1)

def build(nc,d,out):
    ctx=ExitStack()
    with ctx:
        m=declare_sort(nc,ctx)
        n=declare_dense(nc,ctx,m.SA,m.SB); n.UM=m.ltri[:,:]
        declare_nodes(nc,ctx,n,m.SA)
        for k,sh,dt in (("A1",(EDGES,1),i32),("A2",(EDGES,1),i32),("AEXP",(EDGES,4),f32),("R",(EDGES,24),f32),("CT",(P,24),f32),
                        ("T",(NODES,20),f32),("ADT",(NODES,4),f32),("TNT",(P,NODES),f32),("X3",(NODES,P),f32)):
            d[k]=nc.dram_tensor("s_"+k,sh,dt).ap()
        PSB=ctx.enter_context(nc.psum_tensor("PSB",[P,4096],f32))[:,:]
        PS=[PSB[:,512*i:512*(i+1)] for i in range(8)]
        ident=m.ident[:,:]; ones=m.ones
        block=ctx.enter_context(nc.Block())

        @block.sync
        def _(sp):
            sort_sync_loads(sp,m,d)
            sync_weights(sp,n,d)
            sort_sync_fill(sp,m,d)
            sort_sync(sp,m,d,0)
            sort_sync(sp,m,d,1)
            for s in range(2): sp.wait_ge(m.scat[1][s],512*ROUNDS)
            sp.wait_ge(n.bar_dve,16)
            edges_sync(sp,n,d,m.SA,m.tick_sp,d["A2"])
            moe_sync(sp,n,d,m.tick_sp)

        @block.gpsimd
        def _(pool):
            pool.memset(m.fill[:,:],INVALID).then_inc(m.fill_rdy,1)
            pool.memset(m.zero[:,:],0.0).then_inc(m.fill_rdy,1)
            sort_pool(pool,m,d,0)
            sort_pool(pool,m,d,1)
            edges_pool(pool,n,d,m.tick_pool,None)
            moe_pool(pool,n,out,m.tick_pool)

        @block.vector
        def _(dve):
            sort_dve_prep(dve,m)
            dve_prep(dve,n)
            dve.memset(n.IDW[:,0:1],0.0); dve.tensor_copy(n.IDW[:,1:P+1],ident)
            sort_dve(dve,m,PS,0)
            dve.wait_ge(m.accA,STEPS+1); dve.wait_ge(m.accB,STEPS+1)
            dve.drain().then_inc(n.wdone,1)
            with dve.Fori(0,IMGS) as b:
                l0conv_dve(dve,n,PSB,b)
                l0ffn_dve(dve,n,PSB,b,ident)
                l1conv_dve(dve,n,PSB,b)
                gat_dve(dve,n,PSB,b)
            pos_dve(dve,n,PSB,ones[:,:],m.cnt[:,:])
            sort_dve(dve,m,PS,1)
            dve.wait_ge(m.accA,2*(STEPS+1)); dve.wait_ge(m.accB,2*(STEPS+1))
            edges_prep_dve(dve,n,m.SA)
            edges_dve(dve,n,m.SA)
            carry_dve(dve,n,PSB)
            node_dve(dve,n,m.SA)
            moe_dve(dve,n,PSB)

        @block.scalar
        def _(act):
            act.wait_ge(n.wdone,1)
            with act.Fori(0,IMGS) as b:
                l0conv_act(act,n,PSB,b,d)
                l0ffn_act(act,n,PSB,b)
                l1conv_act(act,n,PSB,b)
                gat_act(act,n,PSB,b,d)
            edges_act(act,n,d)
            carry_act(act,n,d)
            node_act(act,n,m.SA)
            moe_act(act,n,PSB)

        @block.tensor
        def _(pe):
            sort_pe(pe,m,PS,0)
            pe.wait_ge(n.wdone,1)
            with pe.Fori(0,IMGS) as b:
                l0conv_pe(pe,n,PSB,ident,b)
                l0ffn_pe(pe,n,PSB,ident,ones,b)
                l1conv_pe(pe,n,PSB,ident,ones,b)
                gat_pe(pe,n,PSB,ident,b)
            pos_pe(pe,n,PSB,m.ltri[:,:],ones[:,:],m.cnt[:,:])
            pe.wait_ge(n.np_rdy,1)
            sort_pe(pe,m,PS,1)
            carry_pe(pe,n,PSB,ident)
            moe_pe(pe,n,PSB,ones)


def shape_constants(np):
    p=np.arange(P); f=np.float32; k=np.arange(144)
    expand=np.zeros((72,9,P),f)
    for t in range(9):
        for h in range(8): expand[t*8+h,t,16*h:16*h+16]=1
    return dict(ident=np.eye(P,dtype=f), ltri=(p[:,None]<p[None,:]).astype(f), iota=np.tile(p.astype(f),(P,1)),
      PAR=((p[:,None]//16)%2==np.arange(2)[None,:]).astype(f), LM=(p[None,:]<p[:,None]).astype(f),
      INDH=((k[None,:]//12)==(p[:,None]%16)).astype(f), INDW=((k[None,:]%12)==(p[:,None]%16)).astype(f),
      HONE=((p[:,None]//16)==np.arange(8)[None,:]).astype(f), EXPN=expand)

def kernel(**inputs):
    import numpy as np
    import concourse.bacc as bacc
    from concourse.bass_utils import run_bass_kernel_spmd as run

    a=lambda k: np.asarray(inputs[k])
    arrays=dict(x=a("x").reshape(NODES,P),w_q=a("L0_conv_w_q"),w_kv=a("L0_conv_w_kv"),w_out=a("L0_conv_w_out"),
        pos_emb_h=a("L0_conv_pos_emb_h"),pos_emb_w=a("L0_conv_pos_emb_w"),wr=a("L0_ffn_wr"),br=a("L0_ffn_br"),
        w1=a("L0_ffn_w1"),w2=a("L0_ffn_w2"),b2=a("L0_ffn_b2"),b1T=a("L0_ffn_b1").reshape(4,P).T,
        WqkvT=a("L1_conv_Wqkv").T,WprojT=a("L1_conv_Wproj").T,bproj=a("L1_conv_bproj"),
        W_gat=a("L1_ffn_W_gat"),att_src=a("L1_ffn_att_src"),att_dst=a("L1_ffn_att_dst"),b_gat=a("L1_ffn_b_gat"),
        gamma=a("L1_ffn_ln_gamma"),beta=a("L1_ffn_ln_beta"),W1=a("L1_ffn_W1"),W2=a("L1_ffn_W2"),
        b1mT=a("L1_ffn_b1").reshape(8,P).T,b2m=a("L1_ffn_b2"),edges=a("L1_ffn_edge_index"))
    arrays.update(shape_constants(np))
    nc=bacc.Bacc("TRN2",target_bir_lowering=False,num_devices=1)
    feed,d={},{}
    for k,v in arrays.items():
        v=np.ascontiguousarray(v)
        feed["in_"+k]=v
        d[k]=nc.dram_tensor("in_"+k,v.shape,mybir.dt.from_np(v.dtype),kind="ExternalInput").ap()
    out=nc.dram_tensor("out_0",(NODES,P),f32,kind="ExternalOutput").ap()
    build(nc,d,out)
    r=run(nc,[feed],core_ids=[0])
    return np.asarray(r.results[0]["out_0"]).reshape(4,64,64,P)
```

```python
import concourse.bass as bass
from concourse import mybir
from contextlib import ExitStack

f32=mybir.dt.float32; i32=mybir.dt.int32; bf16=mybir.dt.bfloat16
ACT=mybir.ActivationFunctionType; ALU=mybir.AluOpType; AX=mybir.AxisListType
P=128; IMGS=4; IMGTOK=4096; TILES=32; C=128

def declare_dense(nc, ctx, SA, SB):
    class N: pass
    n=N()
    def sb(name,shape,dt=f32):
        t=ctx.enter_context(nc.sbuf_tensor(name,shape,dt)); return t
    def sem(name):
        s=ctx.enter_context(nc.semaphore(name)); return s
    n.X=SA[:,8192:12288].rearrange("p (t c) -> p t c",c=C)
    n.HTL=SA[:,12288:16384].rearrange("p (a m c) -> p a m c",a=2,m=4)
    n.XN=SA[:,16384:17408].rearrange("p (a t c) -> p a t c",a=2,t=4)
    n.ZQ,n.ZH,n.ZW=(SA[:,17408+1024*i:18432+1024*i].rearrange("p (w s q) -> p w s q",w=8,s=2) for i in range(3))
    n.KPAD=SB[:,0:4900]
    n.XPAD=sb("XPAD",[P,68*68]); n.VPAD=sb("VPAD",[P,70*70])
    V=n.VPAD
    n.XW=V[:,0:816]; n.KW=V[:,816:1632]; n.XV=V[:,1632:2784].rearrange("p (w k) -> p w k",w=8)
    n.PTS=V[0:72,2784:3808].rearrange("p (a q) -> p a q",a=8); n.VS=V[0:72,3808:4320].rearrange("p (s a q) -> p s a q",s=2,a=2); n.AOT=V[:,4320:4832]
    n.TB=V[:,0:640].rearrange("p (t k) -> p t k",k=20); n.ADB=V[:,640:768].rearrange("p (t k) -> p t k",k=4); n.HM=V[:,768:1280].rearrange("p (t k) -> p t k",k=16)
    n.ST=sb("ST",[P,TILES,6]); n.MV=sb("MV",[P,TILES,2]); n.RSTD=sb("RSTD",[P,TILES]); n.NMR=sb("NMR",[P,TILES]); n.RS1=sb("RS1",[P,TILES])
    n.QT=sb("QT",[P,512]); n.PRX=sb("PRX",[P,1152]); n.AOM=sb("AOM",[P,2,64])
    n.PR_=n.PRX[:,:].rearrange("p (s j k) -> p s j k",s=2,j=4)
    n.LG=n.PRX[:,0:288].rearrange("p (t k) -> p t k",t=4); n.AT=n.PRX[0:72,288:800]
    n.MX=sb("MX",[P,2,4]); n.SM=sb("SM",[P,2,4]); n.RSM=sb("RSM",[P,2,4])
    n.WQ=sb("WQ",[P,P]); n.WK=sb("WK",[P,P]); n.WV=sb("WV",[P,P]); n.WO=sb("WO",[P,P]); n.EH=sb("EH",[P,8,P]); n.EW=sb("EW",[P,8,P])
    n.W1=sb("W1",[P,512]); n.W2=sb("W2",[P,4,P]); n.B1=sb("B1",[P,4]); n.B2R=sb("B2R",[1,P]); n.WR=sb("WR",[P,1]); n.WRB=sb("WRB",[P,P]); n.BR=sb("BR",[P,1])
    n.WQKV=sb("WQKV",[P,384]); n.WP=sb("WP",[P,P]); n.BPR=sb("BPR",[1,4,P]); n.WG=sb("WG",[P,16]); n.AS=sb("AS",[P,16]); n.AD=sb("AD",[P,16])
    n.PAR=sb("PAR",[P,2]); n.PAR4=sb("PAR4",[P,2]); n.LM=sb("LM",[P,P]); n.INDH=sb("INDH",[P,144]); n.INDW=sb("INDW",[P,144]); n.EXPN=sb("EXPN",[72,9,P]); n.HONE=sb("HONE",[P,8])
    n.WCOL=sb("WCOL",[P,TILES]); n.RK=sb("RK",[P,4,TILES]); n.RANK=sb("RANK",[P,TILES]); n.GS=sb("GS",[P,TILES])
    n.PRD=n.HTL[:,0,:,:]
    n.PR2=n.HTL[:,1,:,:]
    n.LMX=sb("LMX",[P,4,8])
    n.tick_dve, n.tick_pe, n.s_xv, n.w_load, n.x_load, n.wprep = [sem(s) for s in ("tick_dve", "tick_pe", "s_xv", "w_load", "x_load", "wprep",)]
    n.bar_pe, n.bar_act, n.bar_dve, n.ln_st, n.ln_sd, n.ln_xn = [sem(s) for s in ("bar_pe", "bar_act", "bar_dve", "ln_st", "ln_sd", "ln_xn",)]
    n.ln_tr, n.ln_cp, n.s_xw, n.s_k, n.s_kc, n.s_q = [sem(s) for s in ("ln_tr", "ln_cp", "s_xw", "s_k", "s_kc", "s_q",)]
    n.s_qc, n.s_zq, n.s_ph, n.s_pw, n.s_zh, n.s_zw = [sem(s) for s in ("s_qc", "s_zq", "s_ph", "s_pw", "s_zh", "s_zw",)]
    n.s_qk, n.s_mx, n.s_exp, n.s_nrm, n.s_tr, n.s_pta = [sem(s) for s in ("s_qk", "s_mx", "s_exp", "s_nrm", "s_tr", "s_pta",)]
    n.s_ptd, n.s_v, n.s_vc, n.s_pv, n.s_ao, n.s_pj = [sem(s) for s in ("s_ptd", "s_v", "s_vc", "s_pv", "s_ao", "s_pj",)]
    n.s_xa, n.s_w, n.s_wc, n.s_h, n.s_ge, n.s_y = [sem(s) for s in ("s_xa", "s_w", "s_wc", "s_h", "s_ge", "s_y",)]
    n.s_ya, n.s_pz, n.s_kv, n.s_kvc, n.s_vvc, n.s_cq = [sem(s) for s in ("s_ya", "s_pz", "s_kv", "s_kvc", "s_vvc", "s_cq",)]
    n.s_cqc, n.s_pr, n.s_lg, n.s_sb, n.s_ex, n.s_nm = [sem(s) for s in ("s_cqc", "s_pr", "s_lg", "s_sb", "s_ex", "s_nm",)]
    n.s_at, n.s_atc, n.s_ep, n.s_p2, n.s_pp, n.s_cxa = [sem(s) for s in ("s_at", "s_atc", "s_ep", "s_p2", "s_pp", "s_cxa",)]
    n.s_gt, n.s_tb, n.x3_st, n.tn_st, n.t_st, n.sorted_ = [sem(s) for s in ("s_gt", "s_tb", "x3_st", "tn_st", "t_st", "sorted_",)]
    n.bar=dict(pe=n.bar_pe,act=n.bar_act,dve=n.bar_dve)
    return n

def sync_weights(sp, n, d):
    k=0
    def ld(dst,src):
        nonlocal k
        sp.dma_start(dst,src).then_inc(n.w_load,16); k+=16
    ld(n.WQ[:,:],d["w_q"]); 
    kv=d["w_kv"].rearrange("c (n t e) -> c n t e",n=8,t=2)
    ld(n.WK[:,:].rearrange("c (n e) -> c n e",n=8),kv[:,:,0,:]); ld(n.WV[:,:].rearrange("c (n e) -> c n e",n=8),kv[:,:,1,:])
    ld(n.WO[:,:],d["w_out"])
    ld(n.W1[:,:],d["w1"]); ld(n.W2[:,:,:],d["w2"].rearrange("(m p) o -> p m o",p=P)); 
    ld(n.B1[:,:],d["b1T"]); ld(n.B2R[:,:],d["b2"].rearrange("(a n) -> a n",a=1))
    ld(n.WR[:,:],d["wr"]); ld(n.BR[:,:],d["br"].rearrange("(a n) -> a n",a=1).to_broadcast((P,1)))
    ld(n.WQKV[:,:],d["WqkvT"]); ld(n.WP[:,:],d["WprojT"])
    for i in range(4): ld(n.BPR[:,i,:],d["bproj"].rearrange("(a n) -> a n",a=1))
    ld(n.WG[:,:],d["W_gat"]); ld(n.AS[:,:],d["att_src"].rearrange("h e -> (h e)").rearrange("(a n) -> a n",a=1).to_broadcast((P,16))); ld(n.AD[:,:],d["att_dst"].rearrange("h e -> (h e)").rearrange("(a n) -> a n",a=1).to_broadcast((P,16)))
    for t,nm in ((n.PAR,"PAR"),(n.LM,"LM"),(n.INDH,"INDH"),(n.INDW,"INDW"),(n.HONE,"HONE")): ld(t[:,:],d[nm])
    ld(n.EXPN[:,:,:],d["EXPN"])
    sp.wait_ge(n.wprep,1)
    for h in range(8):
        for t,nm in ((n.EH,"pos_emb_h"),(n.EW,"pos_emb_w")):
            for q in range(8):
                ld(t[16*h:16*h+16,q,16*h:16*h+12],d[nm][:,11-q:23-q])
    n.NW=k

def dve_prep(dve,n):
    dve.memset(n.EH[:,:,:],0.0); dve.memset(n.EW[:,:,:],0.0).then_inc(n.wprep,1)
    dve.wait_ge(n.w_load,n.NW)
    dve.tensor_scalar(n.PAR4[:,:],n.PAR[:,:],0.25,None,ALU.mult)
    dve.tensor_copy(n.WRB[:,:],n.WR[:,:].to_broadcast((P,P))).then_inc(n.wprep,1)

SE=4
def barrier(eng, n, me, b, st):
    eng.drain().then_inc(n.bar[me],1)
    for o in ("pe","act","dve"):
        if o!=me: eng.wait_ge(n.bar[o],b*SE+(st+1))

class Ln:
    @staticmethod
    def dve(dve,n,L,eps):
        for t in range(TILES): dve.bn_stats(n.ST[:,t,:],n.X[:,t,:])
        dve.drain()
        for t in range(TILES): dve.bn_aggr(n.MV[:,t,:],n.ST[:,t,:])
        dve.drain()
        dve.tensor_scalar(n.RSTD[:,:],n.MV[:,:,1],eps,None,ALU.add).then_inc(n.ln_st,1)
        dve.wait_ge(n.ln_sd,L+1)
        dve.reciprocal(n.RSTD[:,:],n.RSTD[:,:])
        dve.drain()
        dve.tensor_tensor(n.NMR[:,:],n.MV[:,:,0],n.RSTD[:,:],ALU.mult)
        dve.drain()
        dve.tensor_scalar(n.NMR[:,:],n.NMR[:,:],-1.0,None,ALU.mult)
        dve.drain()
        for g in range(8):
            if g>=2: dve.wait_ge(n.ln_tr,L*8+(g-1))
            for i in range(4):
                t=4*g+i
                last=dve.tensor_scalar(n.XN[:,g%2,i,:],n.X[:,t,:],n.RSTD[:,t:t+1],n.NMR[:,t:t+1],ALU.mult,ALU.add)
            last.then_inc(n.ln_xn,1)
    @staticmethod
    def pe(pe,n,PSB,ident,L):
        for g in range(8):
            pe.wait_ge(n.ln_xn,L*8+(g+1))
            if g>=2: pe.wait_ge(n.ln_cp,L*8+(g-1))
            for i in range(4):
                last=pe.transpose(PSB[:,(6+g%2)*512+i*P:(6+g%2)*512+(i+1)*P],n.XN[:,g%2,i,:],ident)
            last.then_inc(n.ln_tr,1)
    @staticmethod
    def act(act,n,PSB,L,padded):
        act.wait_ge(n.ln_st,L+1)
        act.activation(n.RSTD[:,:],n.RSTD[:,:],ACT.Sqrt).then_inc(n.ln_sd,1)
        for g in range(8):
            act.wait_ge(n.ln_tr,L*8+(g+1))
            src=PSB[:,(6+g%2)*512:(7+g%2)*512]
            if padded:
                dst=n.XPAD[:,:].rearrange("c (y x) -> c y x",y=68)[:,2+8*g:10+8*g,2:66]
                src=src.rearrange("c (y x) -> c y x",y=8)
            else: dst=n.XPAD[:,g*512:(g+1)*512]
            act.activation(dst,src,ACT.Copy).then_inc(n.ln_cp,1)

def l0conv_dve(dve,n,PSB,b):
    dve.wait_ge(n.x_load,b*64+64)
    xp=n.XPAD[:,:].rearrange("c (y x) -> c y x",y=68)
    dve.memset(xp[:,0:2,:],0.0); dve.memset(xp[:,66:68,:],0.0); dve.memset(xp[:,2:66,0:2],0.0); dve.memset(xp[:,2:66,66:68],0.0).then_inc(n.s_pz,1)
    Ln.dve(dve,n,b*4,1e-6)
    with dve.Fori(0,8) as hh:
        st=b*8+hh
        def norm(w):
            dve.wait_ge(n.s_exp,st*8+(w+1))
            dve.reciprocal(n.RSM[:,w%2,:],n.SM[:,w%2,:])
            dve.drain()
            dve.tensor_tensor(n.PR_[:,w%2,:,:],n.PR_[:,w%2,:,:],n.RSM[:,w%2,:].unsqueeze(2).to_broadcast((P,4,144)),ALU.mult).then_inc(n.s_nrm,1)
        def mx(w):
            dve.wait_ge(n.s_qk,st*8+(w+1))
            dve.tensor_reduce(n.MX[:,w%2,:],PSB[:,0:2048].rearrange("p (j x) -> p j x",j=4)[:,:,0:144],AX.X,ALU.max,negate=True).then_inc(n.s_mx,1)
        dve.wait_ge(n.s_qc,st+1)
        q=n.QT[:,:].rearrange("p (y w x) -> p w y x",y=8,w=8)
        for s in range(2):
            for w in range(8):
                last=dve.tensor_scalar(n.ZQ[:,w,s,:].rearrange("p (y x) -> p y x",y=8),q[:,w],n.PAR4[:,s:s+1],None,ALU.mult)
        last.then_inc(n.s_zq,1)
        dve.wait_ge(n.s_ph,st+1)
        q=PSB[:,5*512:6*512].rearrange("p (y w x) -> p w y x",y=8,w=8)
        for s in range(2):
            for w in range(8):
                last=dve.tensor_scalar(n.ZH[:,w,s,:].rearrange("p (y x) -> p y x",y=8),q[:,w],n.PAR[:,s:s+1],None,ALU.mult)
        last.then_inc(n.s_zh,1)
        mx(0)
        for w in range(8):
            norm(w)
            if w<7: mx(w+1)
            dve.wait_ge(n.s_tr,st*8+(w+1))
            dve.tensor_copy(n.PTS[:,4:8,:],PSB[0:72,5*512:6*512].rearrange("p (a q) -> p a q",a=4)).then_inc(n.s_ptd,1)
            dve.wait_ge(n.s_pv,st*8+(w+1))
            dve.tensor_scalar(n.AOM[:,w%2,:],PSB[:,7*512:7*512+64],n.PAR[:,0:1],None,ALU.mult)
            dve.drain()
            dve.scalar_tensor_tensor(out=n.AOT[:,:].rearrange("p (y x) -> p y x",y=8)[:,:,8*w:8*w+8],in0=PSB[:,7*512+64:7*512+128].rearrange("p (y x) -> p y x",y=8),scalar=n.PAR[:,1:2],in1=n.AOM[:,w%2,:].rearrange("p (y x) -> p y x",y=8),op0=ALU.mult,op1=ALU.add).then_inc(n.s_ao,1)
        dve.wait_ge(n.s_pj,st+2)
        xs=n.X[:,bass.ds(hh*4,4),:]
        dve.tensor_tensor(xs,xs,PSB[:,6*512:7*512].rearrange("p (t c) -> p t c",t=4),ALU.add).then_inc(n.s_xa,1)
    barrier(dve,n,"dve",b,0)

def l0conv_act(act,n,PSB,b,d):
    for q in range(4):
        act.dma_start(n.X[:,8*q:8*q+8,:],d["x"].rearrange("(t p) c -> p t c",p=P)[:,bass.ds(b*TILES+8*q,8),:]).then_inc(n.x_load,16)
    act.wait_ge(n.s_pz,b+1)
    Ln.act(act,n,PSB,b*4,True)
    act.drain()
    with act.Fori(0,8) as hh:
        st=b*8+hh
        act.wait_ge(n.s_pj,st+1)
        act.activation(n.XW[:,:],n.XPAD[:,bass.ds(hh*(8*68),12*68)],ACT.Copy).then_inc(n.s_xw,1)
        act.drain()
        for w in range(8):
            last=act.activation(n.XV[:,w,:].rearrange("p (y x) -> p y x",y=12),n.XW[:,:].rearrange("p (y x) -> p y x",y=12)[:,:,8*w:8*w+12],ACT.Copy)
        last.then_inc(n.s_xv,1)
        act.wait_ge(n.s_k,st+1)
        for i in range(2):
            last=act.activation(n.KW[:,408*i:408*(i+1)],PSB[:,(6+i)*512:(6+i)*512+408],ACT.Copy)
        last.then_inc(n.s_kc,1)
        act.wait_ge(n.s_q,st+1)
        act.activation(n.QT[:,:],PSB[:,4*512:5*512],ACT.Copy).then_inc(n.s_qc,1)
        act.wait_ge(n.s_pw,st+1)
        q=PSB[:,4*512:5*512].rearrange("p (x y w) -> p w y x",x=8,y=8)
        for s in range(2):
            for w in range(8):
                last=act.activation(n.ZW[:,w,s,:].rearrange("p (y x) -> p y x",y=8),q[:,w],ACT.Copy,scale=n.PAR[:,s:s+1])
        last.then_inc(n.s_zw,1)
        def ex(w):
            act.wait_ge(n.s_mx,st*8+(w+1))
            if w>=2: act.wait_ge(n.s_tr,st*8+(w-1))
            for j in range(4):
                last=act.activation(n.PR_[:,w%2,j,:],PSB[:,j*512:j*512+144],ACT.Exp,bias=n.MX[:,w%2,j:j+1],accum_out=n.SM[:,w%2,j:j+1])
            last.then_inc(n.s_exp,1)
        def vc(w):
            act.wait_ge(n.s_v,st*8+(w+1))
            act.activation(n.VS[:,w%2,:,:],PSB[0:72,6*512:6*512+256].rearrange("p (a q) -> p a q",a=2),ACT.Copy).then_inc(n.s_vc,1)
        ex(0); vc(0)
        for w in range(8):
            if w<7: ex(w+1); vc(w+1)
            act.wait_ge(n.s_tr,st*8+(w+1))
            act.activation(n.PTS[:,0:4,:],PSB[0:72,4*512:5*512].rearrange("p (a q) -> p a q",a=4),ACT.Copy).then_inc(n.s_pta,1)
    barrier(act,n,"act",b,0)

def l0conv_pe(pe,n,PSB,ident,b):
    Ln.pe(pe,n,PSB,ident,b*4)
    with pe.Fori(0,8) as hh:
        st=b*8+hh
        xw=n.XW[:,:].rearrange("c (y x) -> c y x",y=12); kw=n.KW[:,:].rearrange("c (y x) -> c y x",y=12)
        pe.wait_ge(n.s_xw,st+1); pe.wait_ge(n.s_xa,st+1); pe.wait_ge(n.s_pta,st*8+1)
        for i in range(2):
            last=pe.matmul(PSB[:,(6+i)*512:(6+i)*512+408],n.WK[:,:],n.XW[:,408*i:408*(i+1)],start=True,stop=True)
        last.then_inc(n.s_k,1)
        pe.matmul(PSB[:,4*512:5*512],n.WQ[:,:],xw[:,2:10,2:66],start=True,stop=True).then_inc(n.s_q,1)
        pe.wait_ge(n.s_qc,st+1); pe.wait_ge(n.s_zq,st+1)
        qt=n.QT[:,:].rearrange("c (y w x) -> c y w x",y=8,w=8)
        for y in range(8):
            last=pe.matmul(PSB[:,5*512+64*y:5*512+64*(y+1)],n.EH[:,y,:],n.QT[:,64*y:64*(y+1)],start=True,stop=True)
        last.then_inc(n.s_ph,1)
        for x in range(8):
            last=pe.matmul(PSB[:,4*512+64*x:4*512+64*(x+1)],n.EW[:,x,:],qt[:,:,:,x],start=True,stop=True)
        last.then_inc(n.s_pw,1)
        pe.wait_ge(n.s_xv,st+1); pe.wait_ge(n.s_kc,st+1); pe.wait_ge(n.s_zh,st+1); pe.wait_ge(n.s_zw,st+1)
        def S(w):
            if w>=1: pe.wait_ge(n.s_exp,st*8+w)
            for j in range(4):
                r=slice(32*j,32*j+32)
                z=lambda t: t[r,w,:,:].rearrange("p s q -> p (s q)")
                o=PSB[:,j*512:j*512+144]
                pe.matmul(o,z(n.ZQ),kw[r,:,8*w:8*w+12],start=True,stop=False)
                pe.matmul(o,z(n.ZH),n.INDH[r,:],start=False,stop=False)
                last=pe.matmul(o,z(n.ZW),n.INDW[r,:],start=False,stop=True)
            last.then_inc(n.s_qk,1)
        def V(w):
            if w>=1: pe.wait_ge(n.s_vc,st*8+w)
            for g in range(2):
                last=pe.matmul(PSB[0:72,6*512+g*P:6*512+(g+1)*P],n.XV[:,w,72*g:72*g+72],n.WV[:,:],start=True,stop=True)
            last.then_inc(n.s_v,1)
        S(0); V(0)
        for w in range(8):
            if w<7: S(w+1); V(w+1)
            pe.wait_ge(n.s_nrm,st*8+(w+1)); 
            if w>=1: pe.wait_ge(n.s_pta,st*8+(w+1)); pe.wait_ge(n.s_ptd,st*8+w)
            for j in range(4):
                for g in range(2):
                    o=(4+j//2)*512+((j%2)*2+g)*P
                    last=pe.transpose(PSB[0:72,o:o+P],n.PR_[:,w%2,j,72*g:72*g+72],ident)
            last.then_inc(n.s_tr,1)
            pe.wait_ge(n.s_pta,st*8+(w+2)); pe.wait_ge(n.s_ptd,st*8+(w+1)); pe.wait_ge(n.s_vc,st*8+(w+1))
            if w>=1: pe.wait_ge(n.s_ao,st*8+w)
            for j in range(4):
                for g in range(2):
                    last=pe.matmul(PSB[32*j:32*j+32,7*512:7*512+P],n.VS[:,w%2,g,32*j:32*j+32],n.PTS[:,2*j+g,:],start=(g==0),stop=(g==1))
            last.then_inc(n.s_pv,1)
        pe.wait_ge(n.s_ao,st*8+8)
        for i in range(4):
            last=pe.matmul(PSB[:,6*512+P*i:6*512+P*(i+1)],n.AOT[:,P*i:P*(i+1)],n.WO[:,:],start=True,stop=True)
        last.then_inc(n.s_pj,1)
    barrier(pe,n,"pe",b,0)

KEEP=2047
def l0ffn_dve(dve,n,PSB,b,ident):
    Ln.dve(dve,n,b*4+1,1e-5)
    dve.tensor_scalar(n.RS1[:,:],n.RSTD[:,:],1.0,None,ALU.add)
    dve.memset(n.RK[:,:,:],0.0)
    dve.drain()
    for t in range(TILES):
        dve.tensor_scalar(n.X[:,t,:],n.X[:,t,:],n.RS1[:,t:t+1],n.NMR[:,t:t+1],ALU.mult,ALU.add)
    wrow=n.VPAD[:,0:IMGTOK]; junk=n.KPAD[:,0:IMGTOK]
    dve.wait_ge(n.s_wc,b*8+8)
    dve.tensor_tensor(junk.rearrange("p (t j) -> p t j",j=P),wrow.rearrange("p (t j) -> p t j",j=P),ident.unsqueeze(1).to_broadcast((P,TILES,P)),ALU.mult)
    dve.drain()
    dve.tensor_reduce(n.WCOL[:,:],junk.rearrange("p (t j) -> p t j",j=P),AX.X,ALU.add)
    dve.drain()
    for t in range(TILES):
        w=n.WCOL[:,t:t+1]
        if t: dve.tensor_scalar(junk[:,0:t*P],wrow[:,0:t*P],w,0.0,ALU.is_ge,ALU.add,accum_out=n.RK[:,0,t:t+1])
        if t<TILES-1: dve.tensor_scalar(junk[:,(t+1)*P:],wrow[:,(t+1)*P:],w,0.0,ALU.is_gt,ALU.add,accum_out=n.RK[:,1,t:t+1])
        blk=wrow[:,t*P:(t+1)*P]
        dve.scalar_tensor_tensor(out=junk[:,t*P:(t+1)*P],in0=blk,scalar=w,in1=n.LM[:,:],op0=ALU.is_ge,op1=ALU.mult,accum_out=n.RK[:,2,t:t+1])
        dve.drain()
        dve.scalar_tensor_tensor(out=junk[:,t*P:(t+1)*P],in0=blk,scalar=w,in1=n.UM,op0=ALU.is_gt,op1=ALU.mult,accum_out=n.RK[:,3,t:t+1])
        dve.drain()
    dve.tensor_reduce(n.RANK[:,:],n.RK[:,:,:].rearrange("p a t -> p t a"),AX.X,ALU.add)
    dve.drain()
    dve.scalar_tensor_tensor(out=n.GS[:,:],in0=n.RANK[:,:],scalar=float(KEEP),in1=n.WCOL[:,:],op0=ALU.is_lt,op1=ALU.mult)
    dve.drain()
    for g in range(8):
        dve.wait_ge(n.s_y,b*8+(g+1))
        for i in range(4):
            t=4*g+i
            last=dve.scalar_tensor_tensor(out=n.X[:,t,:],in0=PSB[:,(6+g%2)*512+i*P:(6+g%2)*512+(i+1)*P],scalar=n.GS[:,t:t+1],in1=n.X[:,t,:],op0=ALU.mult,op1=ALU.add)
        last.then_inc(n.s_ya,1)
    barrier(dve,n,"dve",b,1)

def l0ffn_act(act,n,PSB,b):
    Ln.act(act,n,PSB,b*4+1,False)
    for g in range(8):
        act.wait_ge(n.s_w,b*8+(g+1))
        act.activation(n.VPAD[:,512*g:512*(g+1)],PSB[:,(g%2)*512:(g%2+1)*512],ACT.Identity,bias=n.BR[:,:]).then_inc(n.s_wc,1)
    for g in range(8):
        for m in range(4):
            act.wait_ge(n.s_h,b*32+(4*g+m+1))
            if g>=2 and m==0: act.wait_ge(n.s_y,b*8+(g-1))
            act.activation(n.HTL[:,g%2,m,:],PSB[:,(2+m)*512:(3+m)*512],ACT.Gelu_apprx_tanh,bias=n.B1[:,m:m+1]).then_inc(n.s_ge,1)
    barrier(act,n,"act",b,1)

def l0ffn_pe(pe,n,PSB,ident,ones,b):
    Ln.pe(pe,n,PSB,ident,b*4+1)
    pe.wait_ge(n.ln_cp,b*32+16)
    for g in range(8):
        if g>=2: pe.wait_ge(n.s_wc,b*8+(g-1))
        pe.matmul(PSB[:,(g%2)*512:(g%2+1)*512],n.WRB[:,:],n.XPAD[:,512*g:512*(g+1)],start=True,stop=True).then_inc(n.s_w,1)
    def H(g):
        for m in range(4):
            if g: pe.wait_ge(n.s_ge,b*32+(4*(g-1)+m+1))
            pe.matmul(PSB[:,(2+m)*512:(3+m)*512],n.W1[:,P*m:P*(m+1)],n.XPAD[:,512*g:512*(g+1)],start=True,stop=True).then_inc(n.s_h,1)
    H(0)
    for g in range(8):
        if g<7: H(g+1)
        pe.wait_ge(n.s_ge,b*32+(4*g+4))
        if g>=2: pe.wait_ge(n.s_ya,b*8+(g-1))
        for i in range(4):
            o=PSB[:,(6+g%2)*512+i*P:(6+g%2)*512+(i+1)*P]
            pe.matmul(o,ones[0:1,:],n.B2R[:,:],start=True,stop=False)
            for m in range(4):
                last=pe.matmul(o,n.HTL[:,g%2,m,i*P:(i+1)*P],n.W2[:,m,:],start=False,stop=(m==3))
        last.then_inc(n.s_y,1)
    barrier(pe,n,"pe",b,1)

def halves(n_,buf,g8,a,bb):
    out=[]
    for lo,dil in ((0,2),(64,3)):
        v=buf[lo:lo+64,:].rearrange("p (y x) -> p y x",y=70)
        out.append((lo,v[:,bass.ds(g8+(3+(a-1)*dil),8),3+(bb-1)*dil:3+(bb-1)*dil+64]))
    return out
def l1conv_dve(dve,n,PSB,b):
    dve.memset(n.KPAD[:,:],0.0); dve.memset(n.VPAD[:,:],0.0).then_inc(n.s_pz,1)
    Ln.dve(dve,n,b*4+2,1e-6)
    for g in range(8):
        dve.wait_ge(n.s_kv,b*8+(g+1))
        dve.tensor_copy(n.VPAD[:,:].rearrange("p (y x) -> p y x",y=70)[:,3+8*g:11+8*g,3:67],PSB[:,(2+g%2)*512:(3+g%2)*512].rearrange("p (y x) -> p y x",y=8)).then_inc(n.s_vvc,1)
    dve.drain()
    dve.wait_ge(n.s_kvc,b*8+8); dve.sem_inc(n.tick_dve,1)
    with dve.Fori(0,8) as g:
        c=b*8+g
        dve.wait_ge(n.s_cqc,c+2)
        for k in range(9):
            if k>=3: dve.wait_ge(n.s_lg,c*9+(k-2))
            for lo,src in halves(n,n.KPAD,g*8,k//3,k%3):
                last=dve.tensor_tensor(n.PRD[lo:lo+64,k%3,:].rearrange("p (y x) -> p y x",y=8),n.QT[lo:lo+64,:].rearrange("p (y x) -> p y x",y=8),src,ALU.mult)
            last.then_inc(n.s_pr,1)
        dve.wait_ge(n.s_lg,c*9+9)
        lg=PSB[:,5*512:5*512+288]
        dve.tensor_reduce(n.LMX[:,:,:],lg.rearrange("p (t k h) -> p t h k",t=4,k=9),AX.X,ALU.max)
        dve.drain()
        for t in range(4):
            last=dve.tensor_tensor(n.LG[:,t,:].rearrange("p (k h) -> p k h",k=9),lg[:,72*t:72*(t+1)].rearrange("p (k h) -> p k h",k=9),n.LMX[:,t,:].unsqueeze(1).to_broadcast((P,9,8)),ALU.subtract)
        last.then_inc(n.s_sb,1)
        dve.wait_ge(n.s_ex,c+1)
        dve.tensor_reduce(n.LMX[:,:,:],n.LG[:,:,:].rearrange("p t (k h) -> p t h k",k=9),AX.X,ALU.add)
        dve.drain()
        dve.reciprocal(n.LMX[:,:,:],n.LMX[:,:,:])
        dve.drain()
        for t in range(4):
            v=n.LG[:,t,:].rearrange("p (k h) -> p k h",k=9)
            last=dve.tensor_tensor(v,v,n.LMX[:,t,:].unsqueeze(1).to_broadcast((P,9,8)),ALU.mult)
        last.then_inc(n.s_nm,1)
        for k in range(9):
            dve.wait_ge(n.s_ep,c*9+(k+1))
            if k>=3: dve.wait_ge(n.s_pp,c*9+(k-2))
            for lo,src in halves(n,n.VPAD,g*8,k//3,k%3):
                last=dve.tensor_tensor(n.PR2[lo:lo+64,k%3,:].rearrange("p (y x) -> p y x",y=8),PSB[lo:lo+64,(k%2)*512:(k%2+1)*512].rearrange("p (y x) -> p y x",y=8),src,ALU.mult)
            last.then_inc(n.s_p2,1)
        dve.wait_ge(n.s_pp,c*9+9)
        xs=n.X[:,bass.ds(g*4,4),:]
        dve.tensor_tensor(xs,xs,PSB[:,7*512:8*512].rearrange("p (t c) -> p t c",t=4),ALU.add).then_inc(n.s_cxa,1)
    barrier(dve,n,"dve",b,2)

def l1conv_act(act,n,PSB,b):
    Ln.act(act,n,PSB,b*4+2,False)
    for g in range(8):
        act.wait_ge(n.s_kv,b*8+(g+1))
        act.activation(n.KPAD[:,:].rearrange("p (y x) -> p y x",y=70)[:,3+8*g:11+8*g,3:67],PSB[:,(g%2)*512:(g%2+1)*512].rearrange("p (y x) -> p y x",y=8),ACT.Copy).then_inc(n.s_kvc,1)
    with act.Fori(0,8) as g:
        c=b*8+g
        act.wait_ge(n.s_cq,c+1)
        act.activation(n.QT[:,:],PSB[:,4*512:5*512],ACT.Copy).then_inc(n.s_cqc,1)
        act.wait_ge(n.s_sb,c+2)
        act.activation(n.LG[:,:,:],n.LG[:,:,:],ACT.Exp,scale=0.25).then_inc(n.s_ex,1)
        act.wait_ge(n.s_at,c+1)
        act.activation(n.AT[:,:],PSB[0:72,6*512:7*512],ACT.Copy).then_inc(n.s_atc,1)
    barrier(act,n,"act",b,2)

def l1conv_pe(pe,n,PSB,ident,ones,b):
    Ln.pe(pe,n,PSB,ident,b*4+2)
    pe.wait_ge(n.ln_cp,b*32+24)
    for g in range(8):
        if g>=2: pe.wait_ge(n.s_kvc,b*8+(g-1)); pe.wait_ge(n.s_vvc,b*8+(g-1))
        x=n.XPAD[:,512*g:512*(g+1)]
        pe.matmul(PSB[:,(g%2)*512:(g%2+1)*512],n.WQKV[:,P:2*P],x,start=True,stop=True)
        pe.matmul(PSB[:,(2+g%2)*512:(3+g%2)*512],n.WQKV[:,2*P:3*P],x,start=True,stop=True).then_inc(n.s_kv,1)
    pe.wait_ge(n.s_kvc,b*8+8); pe.wait_ge(n.s_vvc,b*8+8); pe.sem_inc(n.tick_pe,1)
    with pe.Fori(0,8) as g:
        c=b*8+g
        pe.wait_ge(n.s_cqc,c+1)
        pe.matmul(PSB[:,4*512:5*512],n.WQKV[:,0:P],n.XPAD[:,bass.ds(g*512,512)],start=True,stop=True).then_inc(n.s_cq,1)
        pe.wait_ge(n.s_sb,c+1)
        for k in range(9):
            pe.wait_ge(n.s_pr,c*9+(k+1))
            for t in range(4):
                o=5*512+72*t+8*k
                last=pe.matmul(PSB[:,o:o+8],n.PRD[:,k%3,P*t:P*(t+1)],n.HONE[:,:],start=True,stop=True)
            last.then_inc(n.s_lg,1)
        pe.wait_ge(n.s_cxa,c+1)
        pe.matmul(PSB[:,7*512:8*512],ones[0:1,:],n.BPR[:,:,:].rearrange("a t c -> a (t c)"),start=True,stop=False,skip_group_check=True)
        pe.wait_ge(n.s_nm,c+1); pe.wait_ge(n.s_atc,c+1)
        for t in range(4):
            last=pe.transpose(PSB[0:72,6*512+P*t:6*512+P*(t+1)],n.LG[:,t,:],ident)
        last.then_inc(n.s_at,1)
        pe.wait_ge(n.s_atc,c+2)
        def E(k):
            if k>=2: pe.wait_ge(n.s_p2,c*9+(k-1))
            pe.matmul(PSB[:,(k%2)*512:(k%2+1)*512],n.EXPN[:,k,:],n.AT[:,:],start=True,stop=True).then_inc(n.s_ep,1)
        E(0)
        for k in range(9):
            if k<8: E(k+1)
            pe.wait_ge(n.s_p2,c*9+(k+1))
            for t in range(4):
                last=pe.matmul(PSB[:,7*512+P*t:7*512+P*(t+1)],n.PR2[:,k%3,P*t:P*(t+1)],n.WP[:,:],start=False,stop=(k==8),skip_group_check=True)
            last.then_inc(n.s_pp,1)
    barrier(pe,n,"pe",b,2)

def gat_dve(dve,n,PSB,b):
    Ln.dve(dve,n,b*4+3,1e-5)
    dve.wait_ge(n.s_gt,b+1)
    h=PSB[:,0:512].rearrange("p (t c) -> p t c",c=16)
    dve.tensor_copy(n.TB[:,:,0:16],h)
    for a,(att,dst) in enumerate(((n.AS,n.TB[:,:,16:20]),(n.AD,n.ADB[:,:,:]))):
        dve.drain()
        dve.tensor_tensor(n.HM[:,:,:],h,att[:,:].unsqueeze(1).to_broadcast((P,TILES,16)),ALU.mult)
        dve.drain()
        last=dve.tensor_reduce(dst,n.HM[:,:,:].rearrange("p t (h e) -> p t h e",h=4),AX.X,ALU.add)
    last.then_inc(n.s_tb,1)
    dve.drain()
    dve.wait_ge(n.x3_st,b*16+16); dve.wait_ge(n.tn_st,b*16+16); dve.wait_ge(n.t_st,b*32+32); dve.sem_inc(n.tick_dve,1)
    barrier(dve,n,"dve",b,3)
def gat_act(act,n,PSB,b,d):
    act.dma_start(d["X3"].rearrange("(t p) c -> p t c",p=P)[:,bass.ds(b*TILES,TILES),:],n.X[:,:,:]).then_inc(n.x3_st,16)
    Ln.act(act,n,PSB,b*4+3,False)
    act.drain()
    act.wait_ge(n.ln_cp,b*32+32)
    act.dma_start(d["TNT"][:,bass.ds(b*IMGTOK,IMGTOK)],n.XPAD[:,0:IMGTOK]).then_inc(n.tn_st,16)
    act.wait_ge(n.s_tb,b+1)
    act.dma_start(d["T"].rearrange("(t p) c -> p t c",p=P)[:,bass.ds(b*TILES,TILES),:],n.TB[:,:,:]).then_inc(n.t_st,16)
    act.dma_start(d["ADT"].rearrange("(t p) c -> p t c",p=P)[:,bass.ds(b*TILES,TILES),:],n.ADB[:,:,:]).then_inc(n.t_st,16)
    barrier(act,n,"act",b,3)
def gat_pe(pe,n,PSB,ident,b):
    Ln.pe(pe,n,PSB,ident,b*4+3)
    pe.wait_ge(n.ln_cp,b*32+32)
    for t in range(TILES):
        last=pe.matmul(PSB[:,16*t:16*t+16],n.XPAD[:,P*t:P*(t+1)],n.WG[:,:],start=True,stop=True)
    last.then_inc(n.s_gt,1)
    barrier(pe,n,"pe",b,3)

P=128; NODES=16384; NT=NODES//P; COLS=4096; CH=64; NCH=COLS//CH; BIG=1e30; OUT_OF_RANGE=float(2**20)
IOA=bass.IndirectOffsetOnAxis

def declare_nodes(nc,ctx,n,SA):
    def sem(name):
        s=ctx.enter_context(nc.semaphore(name)); return s
    def sb(name,shape,dt=f32):
        t=ctx.enter_context(nc.sbuf_tensor(name,shape,dt)); return t
    n.np_mm, n.np_rdy, n.ad_ld, n.ad_sc, n.d0_rdy, n.d0_g = [sem(s) for s in ("np_mm", "np_rdy", "ad_ld", "ad_sc", "d0_rdy", "d0_g",)]
    n.d0_st, n.a2_ld, n.keep_rdy, n.fw_rdy, n.fw_exp, n.rb_rdy = [sem(s) for s in ("d0_st", "a2_ld", "keep_rdy", "fw_rdy", "fw_exp", "rb_rdy",)]
    n.lc_sh, n.lc_shd, n.lc_in, n.lc_tr, n.lc_e, n.lc_ee = [sem(s) for s in ("lc_sh", "lc_shd", "lc_in", "lc_tr", "lc_e", "lc_ee",)]
    n.lc_o, n.lc_t2, n.lc_tab, n.lc_st, n.tbn_ld, n.re_g = [sem(s) for s in ("lc_o", "lc_t2", "lc_tab", "lc_st", "tbn_ld", "re_g",)]
    n.ce_g, n.nd1, n.nd1e, n.nd2, n.nd2e, n.nd3 = [sem(s) for s in ("ce_g", "nd1", "nd1e", "nd2", "nd2e", "nd3",)]
    n.nd3e, n.g_rdy, n.moe_w, n.moe_h, n.moe_ge, n.moe_y = [sem(s) for s in ("nd3e", "g_rdy", "moe_w", "moe_h", "moe_ge", "moe_y",)]
    n.moe_dv, n.edges_done, n.r_fill = [sem(s) for s in ("moe_dv","edges_done","r_fill",)]
    n.rbs=[sem(f"rbs{i}") for i in range(2)]; n.moe_ys=[sem(f"moe_ys{i}") for i in range(2)]
    n.gath=[sem(f"gath{i}") for i in range(2)]; n.gst=[sem(f"gst{i}") for i in range(2)]; n.adc=[sem(f"adc{i}") for i in range(2)]; n.rst=[sem(f"rst{i}") for i in range(2)]
    n.moe_in=[sem(f"moe_in{i}") for i in range(2)]; n.moe_out=[sem(f"moe_out{i}") for i in range(2)]
    n.SIX=sb("SIX",[P,NT],i32); n.EIX=sb("EIX",[P,NT],i32); n.PIX=sb("PIX",[P,NT],i32); n.VAL=sb("VAL",[P,NT]); n.MUL=sb("MUL",[P,NT]); n.NSF=sb("NSF",[P,NT]); n.NT1=sb("NT1",[P,NT]); n.NT2=sb("NT2",[P,NT],i32)
    n.END=sb("END",[P,NT]); n.QS=sb("QS",[P,NT]); n.QE=sb("QE",[P,NT])
    n.D0=sb("D0",[P,1],i32); n.AD0=sb("AD0",[P,4]); n.GIX=[sb(f"GIX{i}",[P,CH],i32) for i in range(2)]
    n.IDW=sb("IDW",[P,P+1]); n.LCM=sb("LCM",[P,3,20]); n.LCD=sb("LCD",[P,4]); n.LCT=sb("LCT",[20,3,P]); n.MCX=sb("MCX",[20,P+1]); n.SCX=sb("SCX",[20,P+1]); n.LCE=sb("LCE",[20,2,P]); n.CTB=sb("CTB",[P,24])
    n.G4=sb("G4",[P,NT,4]); n.BG=sb("BG",[P,16]); n.GM=sb("GM",[P,16]); n.BT=sb("BT",[P,16])
    A=n.HTL[:,:,:,:].rearrange("p a b c -> p (a b c)")
    n.G=A[:,0:2560].rearrange("p (s c k) -> p s c k",s=2,k=20)
    n.ADC=A[:,2560:3072].rearrange("p (s c k) -> p s c k",s=2,k=4)
    n.ADX=A[:,3072:3584].rearrange("p (s c k) -> p s c k",s=2,k=4)
    X=n.XPAD[:,:]
    n.RB=X[:,0:3120].rearrange("p (s c k) -> p s c k",s=2,k=24)
    n.EE=X[:,3120:3632].rearrange("p (s c k) -> p s c k",s=2,k=4)
    n.PEN=X[:,3632:3760].rearrange("p (s c) -> p s c",s=2)
    n.FW=n.KPAD[:,2048:3072].rearrange("p (s f c k) -> p s f c k",s=2,f=2,k=4)
    n.V=n.KPAD[:,0:2048].rearrange("p (s c k) -> p s c k",s=2,k=16)
    n.RE=n.VPAD[:,0:3072].rearrange("p (t k) -> p t k",k=24)
    n.CE=n.KPAD[:,0:3072].rearrange("p (t k) -> p t k",k=24)
    n.TBN=SA[:,0:2560].rearrange("p (t k) -> p t k",k=20)
    n.ADN=n.VPAD[:,3072:3584].rearrange("p (t k) -> p t k",k=4)
    n.HM2=SA[:,0:8192].rearrange("p (s m c) -> p s m c",s=2,m=8)
    n.TNC=X[:,0:1024].rearrange("p (s c) -> p s c",s=2)
    n.X3C=X[:,1024:2048].rearrange("p (s t c) -> p s t c",s=2,t=4)
    n.WM1=A[:,1024:2048].rearrange("p (e c) -> p e c",e=4)
    n.WM2=A[:,2048:3072].rearrange("p (m c) -> p m c",m=8)
    n.B1M=A[:,3072:3080]; n.B2M=A[0:1,3584:4096]

def pos_pe(pe,n,PSB,ltri,ones,cnt):
    pe.matmul(PSB[:,0:P],ltri,cnt,start=True,stop=True)
    pe.matmul(PSB[:,P:2*P],ones,cnt,start=True,stop=True).then_inc(n.np_mm,1)
def pos_dve(dve,n,PSB,ones,cnt,m):
    dve.wait_ge(n.np_mm,1)
    dve.tensor_tensor_scan(n.NSF[:,:],ones,PSB[:,P:2*P],0.0,ALU.mult,ALU.add); dve.drain()
    dve.tensor_tensor(n.NSF[:,:],n.NSF[:,:],PSB[:,P:2*P],ALU.subtract); dve.drain()
    dve.tensor_tensor(n.NSF[:,:],n.NSF[:,:],PSB[:,0:P],ALU.add)
    dve.tensor_scalar(n.VAL[:,:],cnt,0.0,None,ALU.is_gt); dve.drain()
    K=m.KV[:,1,:]
    dve.tensor_tensor(n.END[:,:],n.NSF[:,:],cnt,ALU.add); dve.drain()
    dve.tensor_scalar(n.END[:,:],n.END[:,:],-1.0,0.0,ALU.add,ALU.max); dve.drain()
    divide(dve,n.NSF[:,:],K,n.NT2[:,:],n.QS[:,:],n.NT1[:,:])
    divide(dve,n.END[:,:],K,n.NT2[:,:],n.QE[:,:],n.NT1[:,:])
    dve.tensor_copy(n.PIX[:,:],n.QE[:,:])
    dve.tensor_tensor(n.MUL[:,:],n.QS[:,:],n.QE[:,:],ALU.not_equal)
    dve.scalar_tensor_tensor(out=n.NSF[:,:],in0=n.QS[:,:],scalar=K[:,3:4],in1=n.NSF[:,:],op0=ALU.mult,op1=ALU.add)
    dve.scalar_tensor_tensor(out=n.EIX[:,:],in0=n.QE[:,:],scalar=K[:,3:4],in1=n.END[:,:],op0=ALU.mult,op1=ALU.add)
    dve.tensor_scalar(n.NT1[:,:],cnt,0.0,OUT_OF_RANGE,ALU.is_equal,ALU.mult); dve.drain()
    dve.tensor_tensor(n.SIX[:,:],n.NSF[:,:],n.NT1[:,:],ALU.add)
    dve.tensor_tensor(n.MUL[:,:],n.MUL[:,:],n.VAL[:,:],ALU.mult).then_inc(n.np_rdy,1)
    dve.drain()

def edges_prep_dve(dve,n,SA,V):
    I=SA.bitcast(i32)
    s=lambda t,i: t[:,i*4096:(i+1)*4096]
    dve.wait_ge(n.a2_ld,16)
    dve.tensor_scalar(s(I,4),s(I,0),32767,None,ALU.bitwise_and)
    dve.tensor_scalar(s(I,1),s(I,0),15,None,ALU.logical_shift_right); dve.drain()
    dve.tensor_copy(s(SA,2),s(I,4)); dve.drain()
    d=s(SA,2); k=s(SA,4)
    dve.tensor_scalar(n.D0[:,:],d[:,0:1],float(NODES-1),None,ALU.min).then_inc(n.d0_rdy,1)
    dve.tensor_tensor(k[:,1:],d[:,1:],d[:,0:COLS-1],ALU.is_equal)
    dve.memset(k[:,0:1],0.0); dve.drain()
    dve.memset(n.ADX[:,1,:,:],0.0)
    dve.memset(n.RB[:,1,CH,0:4],-BIG); dve.memset(n.RB[:,1,CH,4:24],0.0)
    dve.drain()
    dve.tensor_copy(n.LCD[:,0:1],d[:,0:1]); dve.tensor_copy(n.LCD[:,1:2],SA[:,bass.ds(V*128+(2*4096-1),1)]).then_inc(n.keep_rdy,1)
    dve.drain()
def edges_dve(dve,n,SA,V):
    k_=SA[:,4*4096:5*4096]
    def chunks(i):
        for s in range(2):
            j=i*2+s
            G=n.G[:,s]; K=k_[:,bass.ds(j*CH,CH)]; RB=n.RB[:,s]; E=n.EE[:,s]; PEN=n.PEN[:,s,:]; FW=n.FW[:,s]
            dve.wait_ge(n.rst[s],i*16+1)
            dve.tensor_copy(RB[:,0,:],n.RB[:,1-s,CH,:])
            dve.tensor_scalar(PEN,K,-1.0,BIG,ALU.add,ALU.mult)
            dve.wait_ge(n.adc[s],i*16+16)
            for h in range(4):
                dve.tensor_tensor_scan(n.ADX[:,s,:,h],K,n.ADC[:,s,:,h],n.ADX[:,1-s,CH-1,h:h+1],ALU.mult,ALU.add)
            dve.drain()
            dve.wait_ge(n.gath[s],i*(CH*16)+CH*16)
            dve.tensor_tensor(E,G[:,:,16:20],n.ADX[:,s],ALU.add); dve.drain()
            dve.scalar_tensor_tensor(out=E,in0=E,scalar=0.2,in1=E,op0=ALU.mult,op1=ALU.max); dve.drain()
            for h in range(4):
                dve.tensor_tensor_scan(RB[:,1:CH+1,h],PEN,E[:,:,h],RB[:,0,h:h+1],ALU.add,ALU.max)
            dve.drain()
            dve.tensor_tensor(FW[:,0],RB[:,0:CH,0:4],PEN.unsqueeze(2).to_broadcast((P,CH,4)),ALU.add)
            dve.tensor_tensor(FW[:,1],E,RB[:,1:CH+1,0:4],ALU.subtract); dve.drain()
            dve.tensor_tensor(FW[:,0],FW[:,0],RB[:,1:CH+1,0:4],ALU.subtract).then_inc(n.fw_rdy,1)
            dve.wait_ge(n.fw_exp,j+1)
            dve.tensor_tensor(n.V[:,s].rearrange("p c (h e) -> p c h e",h=4),G[:,:,0:16].rearrange("p c (h e) -> p c h e",h=4),FW[:,1].unsqueeze(3).to_broadcast((P,CH,4,4)),ALU.mult)
            for h in range(4):
                last=dve.tensor_tensor_scan(RB[:,1:CH+1,4+h],FW[:,0,:,h],FW[:,1,:,h],RB[:,0,4+h:5+h],ALU.mult,ALU.add)
            dve.drain()
            for c in range(16):
                last=dve.tensor_tensor_scan(RB[:,1:CH+1,8+c],FW[:,0,:,c//4],n.V[:,s,:,c],RB[:,0,8+c:9+c],ALU.mult,ALU.add)
            last.then_inc(n.rbs[s],1)
            dve.drain()
    with dve.Fori(0,NCH//2) as i:
        with dve.If(i<V): chunks(i)
    dve.drain().then_inc(n.edges_done,1)
def edges_act(act,n,d,V):
    R=d["R"].rearrange("(p c) k -> p c k",p=P)
    def chunks(i):
        for s in range(2):
            j=i*2+s
            act.wait_ge(n.fw_rdy,j+1)
            act.activation(n.FW[:,s],n.FW[:,s],ACT.Exp).then_inc(n.fw_exp,1)
            act.wait_ge(n.rbs[s],i+2)
            act.dma_start(R[:,bass.ds(j*CH,CH),:],n.RB[:,s,1:CH+1,:]).then_inc(n.rst[s],16)
    with act.Fori(0,NCH//2) as i:
        with act.If(i<V): chunks(i)
def edges_pool(pool,n,d,tick,V):
    for t in range(NT):
        if t==0: pool.wait_ge(n.np_rdy,1); pool.wait_ge(n.ad_ld,16)
        pool.indirect_dma_start(out=d["AEXP"],out_offset=IOA(ap=n.SIX[:,t:t+1],axis=0),in_=n.ADN[:,t,:],in_offset=None,bounds_check=4096*128-1,oob_is_err=False).then_inc(n.ad_sc,16)
    pool.wait_ge(n.d0_rdy,1)
    pool.indirect_dma_start(out=n.AD0[:,:],out_offset=None,in_=d["ADT"],in_offset=IOA(ap=n.D0[:,:],axis=0)).then_inc(n.d0_g,16)
    def gather(i):
        for s in range(2):
            pool.wait_ge(n.gst[s],i*16+16); pool.sem_inc(tick,1)
            pool.wait_ge(n.rbs[s],i+1); pool.sem_inc(tick,1)
            for c in range(CH):
                pool.indirect_dma_start(out=n.G[:,s,c,:],out_offset=None,in_=d["T"],in_offset=IOA(ap=n.GIX[s][:,c:c+1],axis=0)).then_inc(n.gath[s],16)
    with pool.Fori(0,NCH//2) as i:
        with pool.If(i<V): gather(i)
    for s in range(2): pool.wait_ge(n.rst[s],V*16+1); pool.sem_inc(tick,1)
    pool.wait_ge(n.r_fill,BLOCKS*96)
    for t in range(NT):
        pool.indirect_dma_start(out=n.RE[:,t,:],out_offset=None,in_=d["R"],in_offset=IOA(ap=n.EIX[:,t:t+1],axis=0)).then_inc(n.re_g,16)
    pool.wait_ge(n.lc_st,16)
    for t in range(NT):
        pool.indirect_dma_start(out=n.CE[:,t,:],out_offset=None,in_=d["CT"],in_offset=IOA(ap=n.PIX[:,t:t+1],axis=0)).then_inc(n.ce_g,16)
def edges_sync_fill(sp,m,n,d,V):
    R=d["R"].rearrange("(p c) k -> p (c k)",p=P)
    with sp.Fori(0,BLOCKS) as i:
        with sp.If(V<=i):
            for q in range(6): sp.dma_start(R[:,bass.ds(i*3072+q*512,512)],m.zero[:,:]).then_inc(n.r_fill,16)
        with sp.If(i<V): sp.sem_inc(n.r_fill,96)
def edges_sync(sp,n,d,SA,tick,A2,V):
    I=SA.bitcast(i32)
    sp.dma_start(n.ADN,d["ADT"].rearrange("(t p) c -> p t c",p=P)).then_inc(n.ad_ld,16)
    sp.dma_start(I[:,0:4096],A2.rearrange("(p c) o -> p (c o)",p=P)).then_inc(n.a2_ld,16)
    sp.wait_ge(n.keep_rdy,1)
    sp.dma_start(n.TBN,d["T"].rearrange("(t p) c -> p t c",p=P)).then_inc(n.tbn_ld,16)
    for t,k in ((n.BG,"b_gat"),(n.GM,"gamma"),(n.BT,"beta")):
        sp.dma_start(t[:,:],d[k].rearrange("(a n) -> a n",a=1).to_broadcast((P,16))).then_inc(n.tbn_ld,16)
    sp.wait_ge(n.ad_sc,16*NT); sp.wait_ge(n.d0_g,16)
    A=d["AEXP"].rearrange("(p c) k -> p c k",p=P)
    sp.dma_start(A[:,0,:],n.AD0[:,:]).then_inc(n.d0_st,16)
    sp.wait_ge(n.d0_st,16); sp.wait_ge(n.keep_rdy,1)
    def stage(i):
        for s in range(2):
            j=i*2+s
            if not (isinstance(i,int) and i==0): sp.wait_ge(n.gath[s],i*(CH*16)); sp.sem_inc(tick,1)
            sp.dma_start(n.GIX[s][:,:],I[:,bass.ds(j*CH+4096,CH)]).then_inc(n.gst[s],16)
            sp.wait_ge(n.rbs[s],i+1); sp.sem_inc(tick,1)
            sp.dma_start(n.ADC[:,s],A[:,bass.ds(j*CH,CH),:]).then_inc(n.adc[s],16)
    stage(0)
    with sp.Fori(1,NCH//2) as i:
        with sp.If(i<V): stage(i)
def carry_dve(dve,n,PSB):
    L=n.RB[:,1,CH,:]
    dve.wait_ge(n.lc_sh,1)
    dve.tensor_tensor(n.LCD[:,2:3],n.LCD[:,0:1],n.LCD[:,1:2],ALU.is_equal)
    dve.tensor_tensor(n.LCD[:,3:4],n.LCD[:,0:1],PSB[:,0:1],ALU.is_equal); dve.drain()
    dve.tensor_tensor(n.LCD[:,2:3],n.LCD[:,2:3],n.LCD[:,3:4],ALU.mult); dve.drain()
    dve.tensor_scalar(n.LCD[:,3:4],n.LCD[:,2:3],-1.0,BIG,ALU.add,ALU.mult); dve.drain()
    dve.tensor_copy(n.LCM[:,2,:],n.LCD[:,3:4].to_broadcast((P,20)))
    dve.tensor_copy(n.LCM[:,0,0:4],L[:,0:4])
    dve.tensor_copy(n.LCM[:,0,4:20].rearrange("p (h e) -> p h e",h=4),L[:,0:4].unsqueeze(2).to_broadcast((P,4,4)))
    dve.tensor_copy(n.LCM[:,1,:],L[:,4:24]).then_inc(n.lc_in,1)
    dve.memset(n.MCX[:,0:1],-BIG); dve.memset(n.SCX[:,0:1],0.0)
    dve.wait_ge(n.lc_tr,1)
    dve.tensor_copy(n.LCT[:,:,:],PSB[0:20,0:384].rearrange("p (a c) -> p a c",a=3)); dve.drain()
    lm,ls,pc=(n.LCT[:,i,:] for i in range(3))
    dve.tensor_tensor_scan(n.MCX[:,1:],pc,lm,-BIG,ALU.add,ALU.max); dve.drain()
    dve.tensor_tensor(n.LCE[:,0,:],n.MCX[:,0:P],pc,ALU.add)
    dve.tensor_tensor(n.LCE[:,1,:],lm,n.MCX[:,1:],ALU.subtract); dve.drain()
    dve.tensor_tensor(n.LCE[:,0,:],n.LCE[:,0,:],n.MCX[:,1:],ALU.subtract).then_inc(n.lc_e,1)
    dve.wait_ge(n.lc_ee,1)
    dve.tensor_tensor(n.LCE[:,1,:],n.LCE[:,1,:],ls,ALU.mult); dve.drain()
    dve.tensor_tensor_scan(n.SCX[:,1:],n.LCE[:,0,:],n.LCE[:,1,:],0.0,ALU.mult,ALU.add).then_inc(n.lc_o,1)
    dve.wait_ge(n.lc_t2,1)
    dve.tensor_copy(n.CTB[:,0:4],PSB[:,0:4]); dve.tensor_copy(n.CTB[:,4:24],PSB[:,20:40]).then_inc(n.lc_tab,1)
def carry_pe(pe,n,PSB,ident):
    pe.wait_ge(n.edges_done,1)
    pe.matmul(PSB[:,0:1],n.IDW[:,0:P],n.LCD[:,1:2],start=True,stop=True).then_inc(n.lc_sh,1)
    pe.wait_ge(n.lc_in,1)
    for i in range(3): last=pe.transpose(PSB[0:20,i*P:(i+1)*P],n.LCM[:,i,:],ident)
    last.then_inc(n.lc_tr,1)
    pe.wait_ge(n.lc_o,1)
    pe.transpose(PSB[:,0:20],n.MCX[:,0:P],ident[0:20,0:20])
    pe.transpose(PSB[:,20:40],n.SCX[:,0:P],ident[0:20,0:20]).then_inc(n.lc_t2,1)
def carry_act(act,n,d):
    act.wait_ge(n.lc_e,1)
    act.activation(n.LCE[:,:,:],n.LCE[:,:,:],ACT.Exp).then_inc(n.lc_ee,1)
    act.wait_ge(n.lc_tab,1)
    act.dma_start(d["CT"],n.CTB[:,:]).then_inc(n.lc_st,16)
def node_dve(dve,n,SA):
    o=[4096]
    def tmp(k):
        a=SA[:,o[0]:o[0]+NT*k]; o[0]+=NT*k
        return a.rearrange("p (t k) -> p t k",k=k)
    mE,mC,mS,M=tmp(4),tmp(4),tmp(4),tmp(4); DEN=tmp(4); MSG=tmp(16); T16=tmp(16); SC=tmp(4); MN=tmp(1); VR=tmp(1); I1=tmp(4); I2=tmp(4); M1=tmp(1); M2=tmp(1); FR=tmp(1); T1=tmp(1)
    dr=dve.drain
    b1=lambda a,k: a.to_broadcast((P,NT,k))
    h4=lambda a: a.rearrange("p t (h e) -> p t h e",h=4)
    be=lambda a: a.unsqueeze(3).to_broadcast((P,NT,4,4))
    dve.wait_ge(n.tbn_ld,16*4); dve.wait_ge(n.ad_ld,16)
    dve.tensor_tensor(mS,n.TBN[:,:,16:20],n.ADN[:,:,:],ALU.add)
    dve.tensor_scalar(n.VAL[:,:],n.VAL[:,:],-1.0,BIG,ALU.add,ALU.mult); dve.tensor_scalar(n.MUL[:,:],n.MUL[:,:],-1.0,BIG,ALU.add,ALU.mult); dr()
    dve.scalar_tensor_tensor(out=mS,in0=mS,scalar=0.2,in1=mS,op0=ALU.mult,op1=ALU.max)
    dve.wait_ge(n.re_g,16*NT)
    dve.tensor_tensor(mE,n.RE[:,:,0:4],n.VAL[:,:].unsqueeze(2).to_broadcast((P,NT,4)),ALU.add)
    dve.wait_ge(n.ce_g,16*NT)
    dve.tensor_tensor(mC,n.CE[:,:,0:4],n.MUL[:,:].unsqueeze(2).to_broadcast((P,NT,4)),ALU.add); dr()
    dve.tensor_tensor(M,mE,mC,ALU.max); dr()
    dve.tensor_tensor(M,M,mS,ALU.max); dr()
    for a in (mE,mC): dve.tensor_tensor(a,a,M,ALU.subtract)
    dve.tensor_tensor(mS,mS,M,ALU.subtract).then_inc(n.nd1,1)
    dve.wait_ge(n.nd1e,1)
    dve.tensor_tensor(DEN,n.RE[:,:,4:8],mE,ALU.mult)
    dve.tensor_tensor(M,n.CE[:,:,4:8],mC,ALU.mult)
    dve.tensor_tensor(h4(MSG),h4(n.RE[:,:,8:24]),be(mE),ALU.mult)
    dve.tensor_tensor(h4(T16),h4(n.CE[:,:,8:24]),be(mC),ALU.mult); dr()
    dve.tensor_tensor(DEN,DEN,M,ALU.add); dve.tensor_tensor(MSG,MSG,T16,ALU.add); dr()
    dve.tensor_tensor(DEN,DEN,mS,ALU.add); dve.tensor_tensor(h4(T16),h4(n.TBN[:,:,0:16]),be(mS),ALU.mult); dr()
    dve.tensor_tensor(MSG,MSG,T16,ALU.add); dve.tensor_scalar(DEN,DEN,1e-16,None,ALU.add); dr()
    dve.reciprocal(DEN,DEN); dr()
    dve.tensor_tensor(h4(MSG),h4(MSG),be(DEN),ALU.mult); dr()
    bc=lambda a: a[:,:].unsqueeze(1).to_broadcast((P,NT,16))
    dve.tensor_tensor(MSG,MSG,bc(n.BG),ALU.add); dr()
    dve.tensor_reduce(MN,MSG,AX.X,ALU.add); dr()
    dve.tensor_scalar(MN,MN,1.0/16,None,ALU.mult); dr()
    dve.tensor_tensor(MSG,MSG,b1(MN,16),ALU.subtract); dr()
    dve.tensor_tensor(T16,MSG,MSG,ALU.mult); dr()
    dve.tensor_reduce(VR,T16,AX.X,ALU.add); dr()
    dve.tensor_scalar(VR,VR,1.0/16,1e-5,ALU.mult,ALU.add).then_inc(n.nd2,1)
    dve.wait_ge(n.nd2e,1)
    dve.reciprocal(VR,VR); dr()
    dve.tensor_tensor(MSG,MSG,b1(VR,16),ALU.mult); dr()
    dve.tensor_tensor(MSG,MSG,bc(n.GM),ALU.mult); dr()
    dve.tensor_tensor(MSG,MSG,bc(n.BT),ALU.add); dr()
    dve.tensor_reduce(SC,MSG.rearrange("p t (h e) -> p t e h",h=4),AX.X,ALU.add); dr()
    dve.tensor_scalar(SC,SC,0.25,None,ALU.mult); dr()
    def first(mx,ind):
        dve.tensor_reduce(mx,SC,AX.X,ALU.max); dr()
        dve.tensor_tensor(ind,SC,b1(mx,4),ALU.is_equal)
        dve.memset(FR,1.0); dr()
        for e in range(4):
            dve.tensor_tensor(ind[:,:,e:e+1],ind[:,:,e:e+1],FR,ALU.mult); dr()
            dve.tensor_tensor(FR,FR,ind[:,:,e:e+1],ALU.subtract); dr()
    first(M1,I1)
    dve.tensor_scalar(T16[:,:,0:4],I1,-3e38,None,ALU.mult); dr()
    dve.tensor_tensor(SC,SC,T16[:,:,0:4],ALU.add); dr()
    first(M2,I2)
    dve.tensor_tensor(T1,M2,M1,ALU.subtract).then_inc(n.nd3,1)
    dve.wait_ge(n.nd3e,1)
    dve.tensor_scalar(M1,T1,1.0,None,ALU.add); dr()
    dve.reciprocal(M1,M1); dr()
    dve.tensor_tensor(M2,T1,M1,ALU.mult); dr()
    dve.tensor_tensor(I1,I1,b1(M1,4),ALU.mult); dve.tensor_tensor(I2,I2,b1(M2,4),ALU.mult); dr()
    dve.tensor_tensor(n.G4[:,:,:],I1,I2,ALU.add).then_inc(n.g_rdy,1)
    dr()
def node_act(act,n,SA):
    o=4096
    act.wait_ge(n.nd1,1)
    act.activation(SA[:,o:o+NT*12],SA[:,o:o+NT*12],ACT.Exp).then_inc(n.nd1e,1)
    act.wait_ge(n.nd2,1)
    vr=o+NT*(4*5+32+4+1)
    act.activation(SA[:,vr:vr+NT],SA[:,vr:vr+NT],ACT.Sqrt).then_inc(n.nd2e,1)
    t1=vr+NT*(1+8+3)
    act.wait_ge(n.nd3,1)
    act.activation(SA[:,t1:t1+NT],SA[:,t1:t1+NT],ACT.Exp).then_inc(n.nd3e,1)
NCK=NODES//512
def moe_sync(sp,n,d,tick):
    sp.wait_ge(n.edges_done,1)
    for dst,k in ((n.WM1,"W1"),(n.WM2,"W2"),(n.B1M,"b1mT"),(n.B2M,"b2m")):
        src=d[k]
        if k=="W1": src=src.rearrange("e c h -> c e h")
        if k=="W2": src=src.rearrange("e (f p) o -> p (e f) o",p=P)
        if k=="b2m": src=src.rearrange("e c -> (e c)").rearrange("(a n) -> a n",a=1)
        sp.dma_start(dst,src).then_inc(n.moe_w,16)
    x3=d["X3"].rearrange("(t p) c -> p t c",p=P)
    sp.wait_ge(n.g_rdy,1)
    def load(i):
        for s in range(2):
            j=i*2+s
            if not (isinstance(i,int) and i==0): sp.wait_ge(n.moe_out[s],i*16); sp.sem_inc(tick,1)
            sp.dma_start(n.TNC[:,s,:],d["TNT"][:,bass.ds(j*512,512)]).then_inc(n.moe_in[s],16)
            sp.dma_start(n.X3C[:,s],x3[:,bass.ds(j*4,4),:]).then_inc(n.moe_in[s],16)
    load(0)
    with sp.Fori(1,NCK//2) as i: load(i)
def moe_pe(pe,n,PSB,ones):
    pe.wait_ge(n.moe_w,64)
    with pe.Fori(0,NCK//2) as i:
        for s in range(2):
            j=i*2+s
            pe.wait_ge(n.moe_in[s],i*32+32)
            for m in range(8):
                (pe.wait_ge(n.moe_ge,j*8+(m-3)) if m>=4 else None)
                pe.matmul(PSB[:,(m%4)*512:(m%4+1)*512],n.WM1[:,m//2,(m%2)*P:(m%2+1)*P],n.TNC[:,s,:],start=True,stop=True).then_inc(n.moe_h,1)
            for t in range(4):
                if t==0: pe.wait_ge(n.moe_ge,j*8+8); pe.wait_ge(n.moe_dv,j*4+1)
                o=PSB[:,(4+t)*512:(5+t)*512]
                pe.matmul(o,ones[0:1,:],n.B2M,start=True,stop=False,skip_group_check=True)
                for m in range(8):
                    last=pe.matmul(PSB[:,(4+t)*512+(m//2)*P:(4+t)*512+(m//2+1)*P],n.HM2[:,s,m,P*t:P*(t+1)],n.WM2[:,m,:],start=False,stop=(m==7),skip_group_check=True)
                last.then_inc(n.moe_ys[s],1)
def moe_act(act,n,PSB):
    act.wait_ge(n.moe_w,64)
    with act.Fori(0,NCK//2) as i:
        for s in range(2):
            j=i*2+s
            for m in range(8):
                act.wait_ge(n.moe_h,j*8+(m+1))
                if m==0: act.wait_ge(n.moe_ys[s],i*4+1)
                act.activation(n.HM2[:,s,m,:],PSB[:,(m%4)*512:(m%4+1)*512],ACT.Gelu,bias=n.B1M[:,m:m+1]).then_inc(n.moe_ge,1)
def moe_pool(pool,n,out,tick):
    o=out.rearrange("(t p) c -> p t c",p=P)
    with pool.Fori(0,NCK//2) as i:
        for s in range(2):
            j=i*2+s
            pool.wait_ge(n.moe_dv,j*4+5); pool.sem_inc(tick,1)
            pool.dma_start(o[:,bass.ds(j*4,4),:],n.X3C[:,s]).then_inc(n.moe_out[s],16)
    for s in range(2): pool.wait_ge(n.moe_out[s],NCK//2*16)
def moe_dve(dve,n,PSB):
    with dve.Fori(0,NCK//2) as i:
        for s in range(2):
            j=i*2+s
            for t in range(4):
                dve.wait_ge(n.moe_ys[s],i*4+(t+2))
                for e in range(4):
                    x=n.X3C[:,s,t,:]
                    last=dve.scalar_tensor_tensor(out=x,in0=PSB[:,(4+t)*512+e*P:(4+t)*512+(e+1)*P],scalar=n.G4[:,bass.ds(j*4+t,1),e],in1=x,op0=ALU.mult,op1=ALU.add)
                    if e<3: dve.drain()
                last.then_inc(n.moe_dv,1)

EDGES=524288; SEGS=8; STEPS=COLS//SEGS; INVALID=NODES; DIG=128
NI=STEPS//4; ROUNDS=NI//2; BEFORE=3

def declare_sort(nc,ctx):
    class N: pass
    m=N()
    def sb(name,shape,dt=f32):
        t=ctx.enter_context(nc.sbuf_tensor(name,shape,dt)); return t
    def sem(name):
        s=ctx.enter_context(nc.semaphore(name)); return s
    m.SA=sb("SA_",[P,5*COLS])[:,:]; m.SI=m.SA.bitcast(i32)
    m.S=[m.SA[:,i*COLS:(i+1)*COLS] for i in range(5)]; m.SJ=[m.SI[:,i*COLS:(i+1)*COLS] for i in range(5)]
    m.SB=sb("SB_",[P,5120])[:,:]
    SBb=m.SB.bitcast(bf16)
    oh=lambda i: SBb[:,i*2048:(i+1)*2048].rearrange("p (u s v) -> p u s v",u=2,s=SEGS)
    m.OHL,m.OHH,m.junk=oh(0),oh(1),oh(2)
    m.Tc=m.SB[:,3072:4096].rearrange("p (s v) -> p s v",s=SEGS); m.INI=m.SB[:,4096:5120].rearrange("p (s v) -> p s v",s=SEGS)
    m.ident,m.ltri,m.ones,m.iotaf,m.tot,m.TT,m.cnt=[sb(t,[P,P]) for t in ("ident","ltri","ones","iotaf","tot","TT","cnt")]
    m.identb=sb("identb",[P,P],bf16); m.iotab=sb("iotab",[P,P],bf16); m.zb=sb("zb",[P,512],bf16); m.big=sb("big",[P,SEGS,4]); m.fill=sb("fill",[P,512],i32); m.zero=sb("zero",[P,512])
    m.VF=sb("VF",[P,2]); m.VI=sb("VI",[P,2],i32); m.KV=sb("KV",[P,2,4]); m.QI=sb("QI",[P,32],i32); m.QR=sb("QR",[P,32]); m.QT=sb("QTm",[P,32])
    m.v_rdy,m.oh_rank,m.rank_done=[sem(s) for s in ("v_rdy","oh_rank","rank_done")]
    m.IX=[sb(f"IX{i}",[P,32],i32) for i in range(2)]; m.PY=[sb(f"PY{i}",[P,32],i32) for i in range(2)]
    m.c_load, m.e_load, m.fill_rdy, m.fill_done, m.const_rdy, m.oh_rdy = [sem(s) for s in ("c_load", "e_load", "fill_rdy", "fill_done", "const_rdy", "oh_rdy",)]
    m.oh_free, m.hist_done, m.tt_rdy, m.lt_done, m.ini_rdy, m.accA = [sem(s) for s in ("oh_free", "hist_done", "tt_rdy", "lt_done", "ini_rdy", "accA",)]
    m.accB, m.exA, m.exB, m.pos_rdy, m.re_load, m.tick_sp = [sem(s) for s in ("accB", "exA", "exB", "pos_rdy", "re_load", "tick_sp",)]
    m.tick_pool, m.o_sem = [sem(s) for s in ("tick_pool", "o_sem",)]
    m.staged=[sem(f"staged{i}") for i in range(2)]; m.scat=[[sem(f"scat{r}{i}") for i in range(2)] for r in range(2)]
    return m

BLOCKS=32
def blocks(eng,m):
    eng.wait_ge(m.v_rdy,1)
    return eng.value_load(m.VI[0:1,0:1],min_val=1,max_val=BLOCKS)
def divide(dve,x,K,qi,r,t):
    dve.tensor_scalar(qi,x,K[:,2:3],None,ALU.mult); dve.drain()
    dve.tensor_copy(r,qi); dve.drain()
    dve.scalar_tensor_tensor(out=t,in0=r,scalar=K[:,1:2],in1=x,op0=ALU.mult,op1=ALU.add); dve.drain()
    dve.scalar_tensor_tensor(out=r,in0=t,scalar=0.0,in1=r,op0=ALU.is_lt,op1=ALU.subtract); dve.drain()
    dve.scalar_tensor_tensor(out=r,in0=t,scalar=K[:,0:1],in1=r,op0=ALU.is_ge,op1=ALU.subtract); dve.drain()
def block_count_dve(dve,m):
    f,i=m.VF[:,:],m.VI[:,:]
    dve.tensor_scalar(i[:,1:2],m.tot[:,P-1:P],16383.0,None,ALU.add); dve.drain()
    dve.tensor_scalar(i[:,1:2],i[:,1:2],14,None,ALU.logical_shift_right); dve.drain()
    dve.tensor_copy(f[:,1:2],i[:,1:2]); dve.drain()
    dve.tensor_scalar(f[:,0:1],f[:,1:2],1.0,None,ALU.max); dve.drain()
    for a,(w,full) in enumerate(((16.0,STEPS),(128.0,COLS))):
        dve.tensor_scalar(m.KV[:,a,0:1],f[:,0:1],w,None,ALU.mult)
        dve.tensor_scalar(m.KV[:,a,1:2],f[:,0:1],-w,None,ALU.mult)
        dve.tensor_scalar(m.KV[:,a,3:4],f[:,0:1],-w,float(full),ALU.mult,ALU.add)
    dve.drain()
    for a in range(2): dve.reciprocal(m.KV[:,a,2:3],m.KV[:,a,0:1])
    dve.tensor_copy(i[:,0:1],f[:,0:1]).then_inc(m.v_rdy,1)
    dve.drain()

def sort_sync_loads(sp,m,d):
    for t,src in ((m.ident,"ident"),(m.ltri,"ltri"),(m.iotaf,"iota")):
        sp.dma_start(t[:,:],d[src]).then_inc(m.c_load,16)
    sp.dma_start(m.SJ[4],d["edges"][0].rearrange("(p c) -> p c",p=P)).then_inc(m.e_load,16)
    sp.dma_start(m.SJ[1],d["edges"][1].rearrange("(p c) -> p c",p=P)).then_inc(m.e_load,16)
def sort_sync_fill(sp,m,d):
    sp.wait_ge(m.fill_rdy,2)
    for A in ("A1","A2"):
        a=d[A].rearrange("(q p c) o -> q p (c o)",p=P,c=512)
        for q in range(EDGES//(P*512)): sp.dma_start(a[q],m.fill[:,:]).then_inc(m.fill_done,16)
    a=d["AEXP"].rearrange("(p c) k -> p (c k)",p=P)
    for q in range(32): sp.dma_start(a[:,512*q:512*(q+1)],m.zero[:,:]).then_inc(m.fill_done,16)
FILLS=16*(2*EDGES//(P*512)+32)
def sort_sync(sp,m,d,r,V):
    if r==1:
        for s in range(2): sp.wait_ge(m.scat[0][s],512*ROUNDS)
        sp.dma_start(m.SJ[0],d["A1"].rearrange("(p c) o -> p (c o)",p=P)).then_inc(m.re_load,16)
    pk=m.SJ[0].rearrange("p (s k) -> p s k",s=SEGS); ps=m.SJ[1].rearrange("p (s k) -> p s k",s=SEGS)
    def stage(i):
        for s in range(2):
            g=i*2+s
            sp.wait_ge(m.pos_rdy,g+(r*NI+1)); sp.sem_inc(m.tick_sp,1)
            if not (isinstance(i,int) and i==0): sp.wait_ge(m.scat[r][s],i*512); sp.sem_inc(m.tick_sp,1)
            sp.dma_start(m.IX[s][:,:],ps[:,:,bass.ds(g*4,4)]).then_inc(m.staged[s],16)
            sp.dma_start(m.PY[s][:,:],pk[:,:,bass.ds(g*4,4)]).then_inc(m.staged[s],16)
    stage(0)
    with sp.Fori(1,ROUNDS) as i:
        if r==0: stage(i)
        else:
            with sp.If(i<V*2): stage(i)
def sort_pool(pool,m,d,r,V):
    if r==0: pool.wait_ge(m.fill_done,FILLS)
    A=d[("A1","A2")[r]]
    def scatter(i):
        for s in range(2):
            pool.wait_ge(m.staged[s],i*32+(r*ROUNDS*32+32)); pool.sem_inc(m.tick_pool,1)
            for c in range(32):
                pool.indirect_dma_start(out=A,out_offset=IOA(ap=m.IX[s][:,c:c+1],axis=0),in_=m.PY[s][:,c:c+1],in_offset=None,bounds_check=EDGES-1,oob_is_err=False).then_inc(m.scat[r][s],16)
    with pool.Fori(0,ROUNDS) as i:
        if r==0: scatter(i)
        else:
            with pool.If(i<V*2): scatter(i)
def sort_dve_prep(dve,m):
    S,SJ=m.S,m.SJ
    dve.memset(m.ones[:,:],1.0); dve.memset(m.zb[:,:],0.0)
    dve.wait_ge(m.c_load,48)
    dve.tensor_copy(m.identb[:,:],m.ident[:,:])
    dve.tensor_copy(m.iotab[:,:],m.iotaf[:,:]).then_inc(m.const_rdy,1)
    dve.wait_ge(m.e_load,32)
    dve.tensor_scalar(S[3],SJ[1],float(INVALID),None,ALU.min)
    dve.tensor_scalar(SJ[2],SJ[4],float(NODES-1),None,ALU.min); dve.drain()
    dve.tensor_copy(SJ[1],S[3])
    dve.tensor_scalar(SJ[0],SJ[2],15,None,ALU.logical_shift_left); dve.drain()
    dve.tensor_tensor(SJ[0],SJ[0],SJ[1],ALU.bitwise_or)
    dve.tensor_scalar(SJ[4],SJ[1],127,None,ALU.bitwise_and); dve.drain()
    dve.tensor_copy(S[2],SJ[4]); dve.drain()
    dve.tensor_scalar(S[4],S[3],float(INVALID),1000.0,ALU.is_ge,ALU.mult); dve.drain()
    dve.tensor_tensor(S[2],S[2],S[4],ALU.add); dve.drain()
    dve.tensor_scalar(SJ[4],SJ[1],7,None,ALU.logical_shift_right); dve.drain()
    dve.tensor_copy(S[3],SJ[4]); dve.drain()
def sort_dve(dve,m,PS,r,V=None):
    S,SJ=m.S,m.SJ
    if r==1:
        dve.wait_ge(m.re_load,16); dve.wait_ge(m.rank_done,1)
        for s in range(2): dve.wait_ge(m.staged[s],32*ROUNDS)
        dve.tensor_scalar(SJ[4],SJ[0],32767,7,ALU.bitwise_and,ALU.logical_shift_right); dve.drain()
        dve.tensor_copy(S[2],SJ[4]); dve.drain()
    def count(i):
        for u in range(2):
            k=i*2+u
            dve.wait_ge(m.oh_free,k+(1+r*STEPS))
            for s in range(SEGS):
                last=dve.tensor_scalar(m.OHL[:,u,s,:],m.iotab[:,:],S[2][:,bass.ds(k+s*STEPS,1)],None,ALU.is_equal)
                if r==0: last=dve.tensor_scalar(m.OHH[:,u,s,:],m.iotab[:,:],S[3][:,bass.ds(k+s*STEPS,1)],None,ALU.is_equal)
            last.then_inc(m.oh_rdy,1)
    with dve.Fori(0,STEPS//2) as i:
        if r==0: count(i)
        else:
            with dve.If(i<V*8): count(i)
    dve.wait_ge(m.hist_done,r+1)
    for b in range(2): dve.tensor_copy(m.Tc[:,4*b:4*b+4,:],PS[b].rearrange("p (s v) -> p s v",s=4))
    if r==0: dve.tensor_copy(m.cnt[:,:],PS[2][:,0:P])
    dve.drain()
    dve.tensor_reduce(m.TT[:,:],m.Tc.rearrange("p s v -> p v s"),AX.X,ALU.add).then_inc(m.tt_rdy,1)
    dve.wait_ge(m.lt_done,r+1)
    dve.tensor_tensor_scan(m.tot[:,:],m.ones[:,:],PS[3][:,P:2*P],0.0,ALU.mult,ALU.add); dve.drain()
    if r==0: block_count_dve(dve,m)
    dve.tensor_tensor(m.tot[:,:],m.tot[:,:],PS[3][:,P:2*P],ALU.subtract); dve.drain()
    dve.tensor_tensor(m.INI[:,0,:],m.tot[:,:],PS[3][:,0:P],ALU.add)
    for s in range(1,SEGS):
        dve.drain()
        last=dve.tensor_tensor(m.INI[:,s,:],m.INI[:,s-1,:],m.Tc[:,s-1,:],ALU.add)
    last.then_inc(m.ini_rdy,1)
    def rank(i):
        for u in range(4):
            k=i*4+u
            dve.wait_ge(m.accA,k+(1+r*(STEPS+1))); dve.wait_ge(m.accB,k+(1+r*(STEPS+1)))
            for s in range(SEGS):
                last=dve.tensor_scalar(m.OHL[:,u%2,s,:],m.iotab[:,:],S[2][:,bass.ds(k+s*STEPS,1)],None,ALU.is_equal)
            last.then_inc(m.oh_rank,1)
            for b in range(2):
                dve.wait_ge((m.accA,m.accB)[b],k+(2+r*(STEPS+1)))
                for s in range(4*b,4*b+4):
                    last=dve.scalar_tensor_tensor(out=m.junk[:,u%2,s,:],in0=m.iotab[:,:],scalar=S[2][:,bass.ds(k+s*STEPS,1)],in1=PS[b][:,(s%4)*DIG:(s%4+1)*DIG],op0=ALU.is_equal,op1=ALU.mult,accum_out=S[4][:,bass.ds(k+s*STEPS,1)])
                last.then_inc((m.exA,m.exB)[b],1)
        v=lambda t: t.rearrange("p (s k) -> p s k",s=SEGS)[:,:,bass.ds(i*4,4)]
        w=lambda t: t[:,:].rearrange("p (s k) -> p s k",s=SEGS)
        dve.tensor_scalar(m.big[:,:,:],v(S[2]),float(DIG),OUT_OF_RANGE,ALU.is_ge,ALU.mult)
        dve.drain()
        K=m.KV[:,r,:]
        divide(dve,v(S[4]),K,w(m.QI),w(m.QR),w(m.QT))
        dve.scalar_tensor_tensor(out=w(m.QT),in0=w(m.QR),scalar=K[:,3:4],in1=v(S[4]),op0=ALU.mult,op1=ALU.add); dve.drain()
        dve.tensor_tensor(v(SJ[1]),w(m.QT),m.big[:,:,:],ALU.add).then_inc(m.pos_rdy,1)
    with dve.Fori(0,NI) as i:
        if r==0: rank(i)
        else:
            with dve.If(i<V*4): rank(i)
def sort_pe(pe,m,PS,r,V=None):
    if r==0: pe.wait_ge(m.const_rdy,1); pe.sem_inc(m.oh_free,2)
    if r==1: pe.wait_ge(m.pos_rdy,NI)
    for b in range(3): pe.matmul(PS[b],m.zb[:,0:P],m.zb[:,:],start=True,stop=True)
    def count(i):
        for u in range(2):
            k=i*2+u
            pe.wait_ge(m.oh_rdy,k+(1+r*STEPS))
            if r==0:
                for s in range(SEGS): pe.matmul(PS[2][:,0:P],m.OHL[:,u,s,:],m.OHH[:,u,s,:],start=False,stop=True,skip_group_check=True)
            for b in range(2): last=pe.matmul(PS[b],m.identb[:,:],m.OHL[:,u,4*b:4*b+4,:],start=False,stop=True,skip_group_check=True)
            last.then_inc(m.oh_free,1)
    with pe.Fori(0,STEPS//2) as i:
        if r==0: count(i)
        else:
            with pe.If(i<V*8): count(i)
    for b in range(3): last=pe.matmul(PS[b],m.zb[:,0:P],m.zb[:,:],start=False,stop=True,skip_group_check=True)
    last.then_inc(m.hist_done,1)
    pe.wait_ge(m.tt_rdy,r+1)
    pe.matmul(PS[3][:,0:P],m.ltri[:,:],m.TT[:,:],start=True,stop=True)
    pe.matmul(PS[3][:,P:2*P],m.ones[:,:],m.TT[:,:],start=True,stop=True).then_inc(m.lt_done,1)
    pe.wait_ge(m.ini_rdy,r+1)
    for b in range(2): pe.matmul(PS[b],m.ident[:,:],m.INI[:,4*b:4*b+4,:],start=True,stop=True).then_inc((m.accA,m.accB)[b],1)
    def rank(i):
        for u in range(2):
            k=i*2+u
            pe.wait_ge(m.oh_rank,k+(1+r*STEPS))
            for b in range(2):
                pe.wait_ge((m.exA,m.exB)[b],k+(1+r*STEPS))
                pe.matmul(PS[b],m.identb[:,:],m.OHL[:,u,4*b:4*b+4,:],start=False,stop=True,skip_group_check=True).then_inc((m.accA,m.accB)[b],1)
    with pe.Fori(0,STEPS//2) as i:
        if r==0: rank(i)
        else:
            with pe.If(i<V*8): rank(i)
    pe.drain().then_inc(m.rank_done,1)

def build(nc,d,out):
    ctx=ExitStack()
    with ctx:
        m=declare_sort(nc,ctx)
        n=declare_dense(nc,ctx,m.SA,m.SB); n.UM=m.ltri[:,:]
        declare_nodes(nc,ctx,n,m.SA)
        for k,sh,dt in (("A1",(EDGES,1),i32),("A2",(EDGES,1),i32),("AEXP",(EDGES,4),f32),("R",(EDGES,24),f32),("CT",(P,24),f32),
                        ("T",(NODES,20),f32),("ADT",(NODES,4),f32),("TNT",(P,NODES),f32),("X3",(NODES,P),f32)):
            d[k]=nc.dram_tensor("s_"+k,sh,dt).ap()
        PSB=ctx.enter_context(nc.psum_tensor("PSB",[P,4096],f32))[:,:]
        PS=[PSB[:,512*i:512*(i+1)] for i in range(8)]
        ident=m.ident[:,:]; ones=m.ones
        block=ctx.enter_context(nc.Block())

        @block.sync
        def _(sp):
            sort_sync_loads(sp,m,d)
            sync_weights(sp,n,d)
            sort_sync_fill(sp,m,d)
            sort_sync(sp,m,d,0,None)
            V=blocks(sp,m)
            edges_sync_fill(sp,m,n,d,V)
            sort_sync(sp,m,d,1,V)
            for s in range(2): sp.wait_ge(m.scat[1][s],V*1024)
            sp.wait_ge(n.bar_dve,SE*IMGS)
            edges_sync(sp,n,d,m.SA,m.tick_sp,d["A2"],V)
            moe_sync(sp,n,d,m.tick_sp)

        @block.gpsimd
        def _(pool):
            for q in n.rbs: pool.sem_inc(q,1)
            pool.memset(m.fill[:,:],INVALID).then_inc(m.fill_rdy,1)
            pool.memset(m.zero[:,:],0.0).then_inc(m.fill_rdy,1)
            sort_pool(pool,m,d,0,None)
            V=blocks(pool,m)
            sort_pool(pool,m,d,1,V)
            edges_pool(pool,n,d,m.tick_pool,V)
            moe_pool(pool,n,out,m.tick_pool)

        @block.vector
        def _(dve):
            for q in (m.accA,m.accB,*n.rst): dve.sem_inc(q,1)
            sort_dve_prep(dve,m)
            dve_prep(dve,n)
            dve.memset(n.IDW[:,0:1],0.0); dve.tensor_copy(n.IDW[:,1:P+1],ident)
            sort_dve(dve,m,PS,0)
            V=blocks(dve,m)
            dve.wait_ge(m.rank_done,1)
            dve.drain().then_inc(n.sorted_,1)
            def image(b):
                l0conv_dve(dve,n,PSB,b)
                l0ffn_dve(dve,n,PSB,b,ident)
                l1conv_dve(dve,n,PSB,b)
                gat_dve(dve,n,PSB,b)
            with dve.Fori(0,BEFORE) as b: image(b)
            pos_dve(dve,n,PSB,ones[:,:],m.cnt[:,:],m)
            sort_dve(dve,m,PS,1,V)
            dve.wait_ge(m.rank_done,2)
            dve.drain().then_inc(n.sorted_,1)
            for b in range(BEFORE,IMGS): image(b)
            edges_prep_dve(dve,n,m.SA,V)
            edges_dve(dve,n,m.SA,V)
            carry_dve(dve,n,PSB)
            node_dve(dve,n,m.SA)
            moe_dve(dve,n,PSB)

        @block.scalar
        def _(act):
            for q in (n.s_pj,*n.moe_ys): act.sem_inc(q,1)
            act.wait_ge(n.sorted_,1)
            def image(b):
                l0conv_act(act,n,PSB,b,d)
                l0ffn_act(act,n,PSB,b)
                l1conv_act(act,n,PSB,b)
                gat_act(act,n,PSB,b,d)
            with act.Fori(0,BEFORE) as b: image(b)
            act.wait_ge(n.sorted_,2)
            for b in range(BEFORE,IMGS): image(b)
            edges_act(act,n,d,blocks(act,m))
            carry_act(act,n,d)
            node_act(act,n,m.SA)
            moe_act(act,n,PSB)

        @block.tensor
        def _(pe):
            for q in (n.s_xa,n.s_pta,n.s_cqc,n.s_sb,n.s_cxa,n.s_atc,n.moe_dv): pe.sem_inc(q,1)
            sort_pe(pe,m,PS,0)
            pe.wait_ge(n.sorted_,1)
            def image(b):
                l0conv_pe(pe,n,PSB,ident,b)
                l0ffn_pe(pe,n,PSB,ident,ones,b)
                l1conv_pe(pe,n,PSB,ident,ones,b)
                gat_pe(pe,n,PSB,ident,b)
            with pe.Fori(0,BEFORE) as b: image(b)
            pos_pe(pe,n,PSB,m.ltri[:,:],ones[:,:],m.cnt[:,:])
            pe.wait_ge(n.np_rdy,1)
            sort_pe(pe,m,PS,1,blocks(pe,m))
            pe.wait_ge(n.sorted_,2)
            for b in range(BEFORE,IMGS): image(b)
            carry_pe(pe,n,PSB,ident)
            moe_pe(pe,n,PSB,ones)


def shape_constants(np):
    p=np.arange(P); f=np.float32; k=np.arange(144)
    expand=np.zeros((72,9,P),f)
    for t in range(9):
        for h in range(8): expand[t*8+h,t,16*h:16*h+16]=1
    return dict(ident=np.eye(P,dtype=f), ltri=(p[:,None]<p[None,:]).astype(f), iota=np.tile(p.astype(f),(P,1)),
      PAR=((p[:,None]//16)%2==np.arange(2)[None,:]).astype(f), LM=(p[None,:]<p[:,None]).astype(f),
      INDH=((k[None,:]//12)==(p[:,None]%16)).astype(f), INDW=((k[None,:]%12)==(p[:,None]%16)).astype(f),
      HONE=((p[:,None]//16)==np.arange(8)[None,:]).astype(f), EXPN=expand)

def kernel(**inputs):
    import numpy as np
    import concourse.bacc as bacc
    from concourse.bass_utils import run_bass_kernel_spmd as run

    a=lambda k: np.asarray(inputs[k])
    arrays=dict(x=a("x").reshape(NODES,P),w_q=a("L0_conv_w_q"),w_kv=a("L0_conv_w_kv"),w_out=a("L0_conv_w_out"),
        pos_emb_h=a("L0_conv_pos_emb_h"),pos_emb_w=a("L0_conv_pos_emb_w"),wr=a("L0_ffn_wr"),br=a("L0_ffn_br"),
        w1=a("L0_ffn_w1"),w2=a("L0_ffn_w2"),b2=a("L0_ffn_b2"),b1T=a("L0_ffn_b1").reshape(4,P).T,
        WqkvT=a("L1_conv_Wqkv").T,WprojT=a("L1_conv_Wproj").T,bproj=a("L1_conv_bproj"),
        W_gat=a("L1_ffn_W_gat"),att_src=a("L1_ffn_att_src"),att_dst=a("L1_ffn_att_dst"),b_gat=a("L1_ffn_b_gat"),
        gamma=a("L1_ffn_ln_gamma"),beta=a("L1_ffn_ln_beta"),W1=a("L1_ffn_W1"),W2=a("L1_ffn_W2"),
        b1mT=a("L1_ffn_b1").reshape(8,P).T,b2m=a("L1_ffn_b2"),edges=a("L1_ffn_edge_index"))
    arrays.update(shape_constants(np))
    nc=bacc.Bacc("TRN2",target_bir_lowering=False,num_devices=1)
    feed,d={},{}
    for k,v in arrays.items():
        v=np.ascontiguousarray(v)
        feed["in_"+k]=v
        d[k]=nc.dram_tensor("in_"+k,v.shape,mybir.dt.from_np(v.dtype),kind="ExternalInput").ap()
    out=nc.dram_tensor("out_0",(NODES,P),f32,kind="ExternalOutput").ap()
    build(nc,d,out)
    r=run(nc,[feed],core_ids=[0])
    return np.asarray(r.results[0]["out_0"]).reshape(4,64,64,P)
```

```python
import concourse.bass as bass
from concourse import mybir
from contextlib import ExitStack

f32=mybir.dt.float32; i32=mybir.dt.int32; bf16=mybir.dt.bfloat16
ACT=mybir.ActivationFunctionType; ALU=mybir.AluOpType; AX=mybir.AxisListType
P=128; IMGS=4; IMGTOK=4096; TILES=32; C=128

def declare_dense(nc, ctx, SA, SB):
    class N: pass
    n=N()
    def sb(name,shape,dt=f32):
        t=ctx.enter_context(nc.sbuf_tensor(name,shape,dt)); return t
    def sem(name):
        s=ctx.enter_context(nc.semaphore(name)); return s
    n.X=SA[:,8192:12288].rearrange("p (t c) -> p t c",c=C)
    n.HTL=SA[:,12288:16384].rearrange("p (a m c) -> p a m c",a=2,m=4)
    n.XN=SA[:,16384:17408].rearrange("p (a t c) -> p a t c",a=2,t=4)
    n.ZQ=SA[:,17408:18432].rearrange("p (w s q) -> p w s q",w=8,s=2)
    n.Y=SA[:,16384:20480].rearrange("p (t c) -> p t c",c=C)
    n.KPAD=SB[:,0:4900]
    n.XPAD=sb("XPAD",[P,68*68]); n.VPAD=sb("VPAD",[P,70*70])
    V=n.VPAD
    n.KW=V[:,816:1632]; n.XV=V[:,1632:2784].rearrange("p (w k) -> p w k",w=8)
    n.PTS=V[0:72,2784:3808].rearrange("p (a q) -> p a q",a=8); n.VS=V[0:72,3808:4320].rearrange("p (s a q) -> p s a q",s=2,a=2); n.AOT=V[:,4320:4832]
    n.TB=V[:,0:640].rearrange("p (t k) -> p t k",k=20); n.ADB=V[:,640:768].rearrange("p (t k) -> p t k",k=4); n.HM=V[:,768:1280].rearrange("p (t k) -> p t k",k=16)
    n.ST=sb("ST",[P,TILES,6]); n.MV=sb("MV",[P,TILES,2]); n.RSTD=sb("RSTD",[P,TILES]); n.NMR=sb("NMR",[P,TILES]); n.RS1=sb("RS1",[P,TILES])
    n.QT=sb("QT",[P,512]); n.PRX=sb("PRX",[P,1152]); n.AOM=sb("AOM",[P,2,64])
    n.PR_=n.PRX[:,:].rearrange("p (s j k) -> p s j k",s=2,j=4)
    n.LG=n.PRX[:,0:288].rearrange("p (t k) -> p t k",t=4); n.AT=n.PRX[0:72,288:800]
    n.MX=sb("MX",[P,2,4]); n.SM=sb("SM",[P,2,4]); n.RSM=sb("RSM",[P,2,4])
    n.WQ=sb("WQ",[P,P]); n.WK=sb("WK",[P,P]); n.WV=sb("WV",[P,P]); n.WO=sb("WO",[P,P]); n.EH=sb("EH",[P,8,P]); n.EW=sb("EW",[P,8,P])
    n.W1=sb("W1",[P,512]); n.W2=sb("W2",[P,4,P]); n.B1=sb("B1",[P,4]); n.B2R=sb("B2R",[1,P]); n.WR=sb("WR",[P,1]); n.WRB=sb("WRB",[P,P]); n.BR=sb("BR",[P,1])
    n.WQKV=sb("WQKV",[P,384]); n.WP=sb("WP",[P,P]); n.BPR=sb("BPR",[1,4,P]); n.WG=sb("WG",[P,16]); n.AS=sb("AS",[P,16]); n.AD=sb("AD",[P,16])
    n.PAR=sb("PAR",[P,2]); n.PAR4=sb("PAR4",[P,2]); n.LM=sb("LM",[P,P]); n.INDH=sb("INDH",[P,144]); n.INDW=sb("INDW",[P,144]); n.EXPN=sb("EXPN",[72,9,P]); n.HONE=sb("HONE",[P,8])
    n.WCOL=sb("WCOL",[P,TILES]); n.RK=sb("RK",[P,4,TILES]); n.RANK=sb("RANK",[P,TILES]); n.GS=sb("GS",[P,TILES])
    n.PRD=n.HTL[:,0,:,:]
    n.PR2=n.HTL[:,1,:,:]
    n.ACC=n.HTL[:,1,3,:]
    n.LMX=sb("LMX",[P,4,8])
    n.tick_dve, n.tick_pe, n.s_xv, n.w_load, n.x_load, n.wprep = [sem(s) for s in ("tick_dve", "tick_pe", "s_xv", "w_load", "x_load", "wprep",)]
    n.bar_pe, n.bar_act, n.bar_dve, n.ln_st, n.ln_sd, n.ln_xn = [sem(s) for s in ("bar_pe", "bar_act", "bar_dve", "ln_st", "ln_sd", "ln_xn",)]
    n.ln_tr, n.ln_cp, n.s_k, n.s_kc, n.s_q = [sem(s) for s in ("ln_tr", "ln_cp", "s_k", "s_kc", "s_q",)]
    n.s_qc, n.s_zq, n.s_ph, n.s_pw, n.s_zh, n.s_zw = [sem(s) for s in ("s_qc", "s_zq", "s_ph", "s_pw", "s_zh", "s_zw",)]
    n.s_qk, n.s_mx, n.s_exp, n.s_nrm, n.s_tr, n.s_pta = [sem(s) for s in ("s_qk", "s_mx", "s_exp", "s_nrm", "s_tr", "s_pta",)]
    n.s_ptd, n.s_v, n.s_vc, n.s_pv, n.s_ao, n.s_pj = [sem(s) for s in ("s_ptd", "s_v", "s_vc", "s_pv", "s_ao", "s_pj",)]
    n.s_xa, n.s_w, n.s_wc, n.s_h, n.s_ge, n.s_y = [sem(s) for s in ("s_xa", "s_w", "s_wc", "s_h", "s_ge", "s_y",)]
    n.s_ya, n.s_pz, n.s_kv, n.s_kvc, n.s_vvc, n.s_cq = [sem(s) for s in ("s_ya", "s_pz", "s_kv", "s_kvc", "s_vvc", "s_cq",)]
    n.s_cqc, n.s_pr, n.s_lg, n.s_sb, n.s_ex, n.s_nm = [sem(s) for s in ("s_cqc", "s_pr", "s_lg", "s_sb", "s_ex", "s_nm",)]
    n.s_at, n.s_atc, n.s_ep, n.s_p2, n.s_pp, n.s_cxa = [sem(s) for s in ("s_at", "s_atc", "s_ep", "s_p2", "s_pp", "s_cxa",)]
    n.s_gt, n.s_tb, n.x3_st, n.tn_st, n.t_st, n.sorted_ = [sem(s) for s in ("s_gt", "s_tb", "x3_st", "tn_st", "t_st", "sorted_",)]
    n.s_acc, n.s_ws = [sem(s) for s in ("s_acc", "s_ws",)]
    n.INDHB=sb("INDHB",[P,144],bf16); n.INDWB=sb("INDWB",[P,144],bf16)
    B=SB.bitcast(bf16)
    n.ZB=[[B[:,(3*a+i)*1024:(3*a+i+1)*1024].rearrange("p (w s q) -> p w s q",w=8,s=2) for i in range(3)] for a in range(2)]
    n.HB=[[B[:,6144+(3*a+i)*512:6144+(3*a+i+1)*512] for i in range(3)] for a in range(2)]
    n.REST=[SA[:,18432+1024*a:18944+1024*a] for a in range(2)]
    n.bar=dict(pe=n.bar_pe,act=n.bar_act,dve=n.bar_dve)
    return n

def sync_weights(sp, n, d):
    k=0
    def ld(dst,src):
        nonlocal k
        sp.dma_start(dst,src).then_inc(n.w_load,16); k+=16
    ld(n.WQ[:,:],d["w_q"]); 
    kv=d["w_kv"].rearrange("c (n t e) -> c n t e",n=8,t=2)
    ld(n.WK[:,:].rearrange("c (n e) -> c n e",n=8),kv[:,:,0,:]); ld(n.WV[:,:].rearrange("c (n e) -> c n e",n=8),kv[:,:,1,:])
    ld(n.WO[:,:],d["w_out"])
    ld(n.W1[:,:],d["w1"]); ld(n.W2[:,:,:],d["w2"].rearrange("(m p) o -> p m o",p=P)); 
    ld(n.B1[:,:],d["b1T"]); ld(n.B2R[:,:],d["b2"].rearrange("(a n) -> a n",a=1))
    ld(n.WR[:,:],d["wr"]); ld(n.BR[:,:],d["br"].rearrange("(a n) -> a n",a=1).to_broadcast((P,1)))
    ld(n.WQKV[:,:],d["WqkvT"]); ld(n.WP[:,:],d["WprojT"])
    for i in range(4): ld(n.BPR[:,i,:],d["bproj"].rearrange("(a n) -> a n",a=1))
    ld(n.WG[:,:],d["W_gat"]); ld(n.AS[:,:],d["att_src"].rearrange("h e -> (h e)").rearrange("(a n) -> a n",a=1).to_broadcast((P,16))); ld(n.AD[:,:],d["att_dst"].rearrange("h e -> (h e)").rearrange("(a n) -> a n",a=1).to_broadcast((P,16)))
    for t,nm in ((n.PAR,"PAR"),(n.LM,"LM"),(n.INDH,"INDH"),(n.INDW,"INDW"),(n.HONE,"HONE")): ld(t[:,:],d[nm])
    ld(n.EXPN[:,:,:],d["EXPN"])
    sp.wait_ge(n.wprep,1)
    for h in range(8):
        for t,nm in ((n.EH,"pos_emb_h"),(n.EW,"pos_emb_w")):
            for q in range(8):
                ld(t[16*h:16*h+16,q,16*h:16*h+12],d[nm][:,11-q:23-q])
    n.NW=k

def dve_prep(dve,n):
    dve.memset(n.EH[:,:,:],0.0); dve.memset(n.EW[:,:,:],0.0).then_inc(n.wprep,1)
    dve.wait_ge(n.w_load,n.NW)
    dve.tensor_scalar(n.PAR4[:,:],n.PAR[:,:],0.25,None,ALU.mult)
    dve.tensor_copy(n.INDHB[:,:],n.INDH[:,:]); dve.tensor_copy(n.INDWB[:,:],n.INDW[:,:])
    dve.tensor_copy(n.WRB[:,:],n.WR[:,:].to_broadcast((P,P))).then_inc(n.wprep,1)

SE=4
def barrier(eng, n, me, b, st):
    eng.drain().then_inc(n.bar[me],1)
    for o in ("pe","act","dve"):
        if o!=me: eng.wait_ge(n.bar[o],b*SE+(st+1))

class Ln:
    @staticmethod
    def dve(dve,n,L,eps):
        for t in range(TILES): dve.bn_stats(n.ST[:,t,:],n.X[:,t,:])
        dve.drain()
        for t in range(TILES): dve.bn_aggr(n.MV[:,t,:],n.ST[:,t,:])
        dve.drain()
        dve.tensor_scalar(n.RSTD[:,:],n.MV[:,:,1],eps,None,ALU.add).then_inc(n.ln_st,1)
        dve.wait_ge(n.ln_sd,L+1)
        dve.reciprocal(n.RSTD[:,:],n.RSTD[:,:])
        dve.drain()
        dve.tensor_tensor(n.NMR[:,:],n.MV[:,:,0],n.RSTD[:,:],ALU.mult)
        dve.drain()
        dve.tensor_scalar(n.NMR[:,:],n.NMR[:,:],-1.0,None,ALU.mult)
        dve.drain()
        for g in range(8):
            if g>=2: dve.wait_ge(n.ln_tr,L*8+(g-1))
            for i in range(4):
                t=4*g+i
                last=dve.tensor_scalar(n.XN[:,g%2,i,:],n.X[:,t,:],n.RSTD[:,t:t+1],n.NMR[:,t:t+1],ALU.mult,ALU.add)
            last.then_inc(n.ln_xn,1)
    @staticmethod
    def pe(pe,n,PSB,ident,L):
        for g in range(8):
            pe.wait_ge(n.ln_xn,L*8+(g+1))
            if g>=2: pe.wait_ge(n.ln_cp,L*8+(g-1))
            for i in range(4):
                last=pe.transpose(PSB[:,(6+g%2)*512+i*P:(6+g%2)*512+(i+1)*P],n.XN[:,g%2,i,:],ident)
            last.then_inc(n.ln_tr,1)
    @staticmethod
    def act(act,n,PSB,L,padded):
        act.wait_ge(n.ln_st,L+1)
        act.activation(n.RSTD[:,:],n.RSTD[:,:],ACT.Sqrt).then_inc(n.ln_sd,1)
        for g in range(8):
            act.wait_ge(n.ln_tr,L*8+(g+1))
            src=PSB[:,(6+g%2)*512:(7+g%2)*512]
            if padded:
                dst=n.XPAD[:,:].rearrange("c (y x) -> c y x",y=68)[:,2+8*g:10+8*g,2:66]
                src=src.rearrange("c (y x) -> c y x",y=8)
            else: dst=n.XPAD[:,g*512:(g+1)*512]
            act.activation(dst,src,ACT.Copy).then_inc(n.ln_cp,1)

def l0conv_dve(dve,n,PSB,b):
    dve.wait_ge(n.x_load,b*64+64)
    xp=n.XPAD[:,:].rearrange("c (y x) -> c y x",y=68)
    dve.memset(xp[:,0:2,:],0.0); dve.memset(xp[:,66:68,:],0.0); dve.memset(xp[:,2:66,0:2],0.0); dve.memset(xp[:,2:66,66:68],0.0).then_inc(n.s_pz,1)
    Ln.dve(dve,n,b*4,1e-6)
    with dve.Fori(0,8) as hh:
        st=b*8+hh
        def norm(w):
            dve.wait_ge(n.s_exp,st*8+(w+1))
            dve.reciprocal(n.RSM[:,w%2,:],n.SM[:,w%2,:])
            dve.drain()
            dve.tensor_tensor(n.PR_[:,w%2,:,:],n.PR_[:,w%2,:,:],n.RSM[:,w%2,:].unsqueeze(2).to_broadcast((P,4,144)),ALU.mult).then_inc(n.s_nrm,1)
        def mx(w):
            dve.wait_ge(n.s_qk,st*8+(w+1))
            dve.tensor_reduce(n.MX[:,w%2,:],PSB[:,0:2048].rearrange("p (j x) -> p j x",j=4)[:,:,0:144],AX.X,ALU.max,negate=True).then_inc(n.s_mx,1)
        dve.wait_ge(n.s_qc,st+1)
        q=n.QT[:,:].rearrange("p (y w x) -> p w y x",y=8,w=8)
        for s in range(2):
            last=dve.tensor_scalar(n.ZQ[:,:,s,:].rearrange("p w (y x) -> p w y x",y=8),q,n.PAR4[:,s:s+1],None,ALU.mult)
        last.then_inc(n.s_zq,1)
        def split(a,bank):
            src=PSB[:,bank*512:(bank+1)*512]; h,r=n.HB[a],n.REST[a]
            dve.tensor_copy(h[0],src); dve.drain()
            dve.tensor_tensor(r,src,h[0],ALU.subtract); dve.drain()
            dve.tensor_copy(h[1],r); dve.drain()
            return dve.tensor_tensor(h[2],r,h[1],ALU.subtract)
        dve.wait_ge(n.s_pw,st+1)
        split(1,4).then_inc(n.s_ws,1)
        split(0,5); dve.drain()
        for i in range(3):
            q=n.HB[0][i].rearrange("p (y w x) -> p w y x",y=8,w=8)
            for s in range(2):
                last=dve.tensor_scalar(n.ZB[0][i][:,:,s,:].rearrange("p w (y x) -> p w y x",y=8),q,n.PAR[:,s:s+1],None,ALU.mult)
        last.then_inc(n.s_zh,1)
        mx(0)
        for w in range(8):
            norm(w)
            if w<7: mx(w+1)
            dve.wait_ge(n.s_tr,st*8+(w+1))
            dve.tensor_copy(n.PTS[:,4:8,:],PSB[0:72,5*512:6*512].rearrange("p (a q) -> p a q",a=4)).then_inc(n.s_ptd,1)
            dve.wait_ge(n.s_pv,st*8+(w+1))
            dve.tensor_scalar(n.AOM[:,w%2,:],PSB[:,7*512:7*512+64],n.PAR[:,0:1],None,ALU.mult)
            dve.drain()
            dve.scalar_tensor_tensor(out=n.AOT[:,:].rearrange("p (y x) -> p y x",y=8)[:,:,8*w:8*w+8],in0=PSB[:,7*512+64:7*512+128].rearrange("p (y x) -> p y x",y=8),scalar=n.PAR[:,1:2],in1=n.AOM[:,w%2,:].rearrange("p (y x) -> p y x",y=8),op0=ALU.mult,op1=ALU.add).then_inc(n.s_ao,1)
        dve.wait_ge(n.s_pj,st+1)
        xs=n.X[:,bass.ds(hh*4,4),:]
        dve.tensor_tensor(xs,xs,PSB[:,6*512:7*512].rearrange("p (t c) -> p t c",t=4),ALU.add).then_inc(n.s_xa,1)
    barrier(dve,n,"dve",b,0)

def windows(strip):
    return bass.AP(tensor=strip.tensor,offset=strip.offset,ap=[strip.ap[0],[8,8],[68,12],[1,12]])
def l0conv_act(act,n,PSB,b,d):
    for q in range(4):
        act.dma_start(n.X[:,8*q:8*q+8,:],d["x"].rearrange("(t p) c -> p t c",p=P)[:,bass.ds(b*TILES+8*q,8),:]).then_inc(n.x_load,16)
    act.wait_ge(n.s_pz,b+1)
    Ln.act(act,n,PSB,b*4,True)
    act.drain()
    with act.Fori(0,8) as hh:
        st=b*8+hh
        act.wait_ge(n.s_q,st+1)
        act.activation(n.QT[:,:],PSB[:,4*512:5*512],ACT.Copy).then_inc(n.s_qc,1)
        act.wait_ge(n.s_k,st+1)
        for i in range(2):
            last=act.activation(n.KW[:,408*i:408*(i+1)],PSB[:,(6+i)*512:(6+i)*512+408],ACT.Copy)
        last.then_inc(n.s_kc,1)
        act.activation(n.XV[:,:,:].rearrange("p w (y x) -> p w y x",y=12),windows(n.XPAD[:,bass.ds(hh*(8*68),12*68)]),ACT.Copy).then_inc(n.s_xv,1)
        act.wait_ge(n.s_ws,st+1)
        for i in range(3):
            q=n.HB[1][i].rearrange("p (x y w) -> p w y x",x=8,y=8)
            for s in range(2):
                last=act.activation(n.ZB[1][i][:,:,s,:].rearrange("p w (y x) -> p w y x",y=8),q,ACT.Copy,scale=n.PAR[:,s:s+1])
        last.then_inc(n.s_zw,1)
        def ex(w):
            act.wait_ge(n.s_mx,st*8+(w+1))
            if w>=2: act.wait_ge(n.s_tr,st*8+(w-1))
            for j in range(4):
                last=act.activation(n.PR_[:,w%2,j,:],PSB[:,j*512:j*512+144],ACT.Exp,bias=n.MX[:,w%2,j:j+1],accum_out=n.SM[:,w%2,j:j+1])
            last.then_inc(n.s_exp,1)
        def vc(w):
            act.wait_ge(n.s_v,st*8+(w+1))
            act.activation(n.VS[:,w%2,:,:],PSB[0:72,6*512:6*512+256].rearrange("p (a q) -> p a q",a=2),ACT.Copy).then_inc(n.s_vc,1)
        ex(0); vc(0)
        for w in range(8):
            if w<7: ex(w+1)
            act.wait_ge(n.s_tr,st*8+(w+1))
            act.activation(n.PTS[:,0:4,:],PSB[0:72,4*512:5*512].rearrange("p (a q) -> p a q",a=4),ACT.Copy).then_inc(n.s_pta,1)
            if w<7: vc(w+1)
    barrier(act,n,"act",b,0)

def l0conv_pe(pe,n,PSB,ident,b):
    Ln.pe(pe,n,PSB,ident,b*4)
    pe.wait_ge(n.ln_cp,b*32+8); pe.sem_inc(n.tick_pe,1)
    with pe.Fori(0,8) as hh:
        st=b*8+hh
        kw=n.KW[:,:].rearrange("c (y x) -> c y x",y=12)
        pe.wait_ge(n.s_xa,st+1); pe.wait_ge(n.s_pta,st*8+1)
        xs=n.XPAD[:,bass.ds(hh*(8*68)+2*68,8*68)].rearrange("c (y x) -> c y x",y=8)[:,:,2:66]
        pe.matmul(PSB[:,4*512:5*512],n.WQ[:,:],xs,start=True,stop=True).then_inc(n.s_q,1)
        for i in range(2):
            last=pe.matmul(PSB[:,(6+i)*512:(6+i)*512+408],n.WK[:,:],n.XPAD[:,bass.ds(hh*(8*68)+408*i,408)],start=True,stop=True)
        last.then_inc(n.s_k,1)
        pe.wait_ge(n.s_qc,st+1)
        qt=n.QT[:,:].rearrange("c (y w x) -> c y w x",y=8,w=8)
        for y in range(8):
            last=pe.matmul(PSB[:,5*512+64*y:5*512+64*(y+1)],n.EH[:,y,:],n.QT[:,64*y:64*(y+1)],start=True,stop=True)
        last.then_inc(n.s_ph,1)
        for x in range(8):
            last=pe.matmul(PSB[:,4*512+64*x:4*512+64*(x+1)],n.EW[:,x,:],qt[:,:,:,x],start=True,stop=True)
        last.then_inc(n.s_pw,1)
        pe.wait_ge(n.s_xv,st+1); pe.wait_ge(n.s_kc,st+1); pe.wait_ge(n.s_zq,st+1); pe.wait_ge(n.s_zh,st+1); pe.wait_ge(n.s_zw,st+1)
        def S(w):
            if w>=1: pe.wait_ge(n.s_exp,st*8+w)
            for j in range(4):
                r=slice(32*j,32*j+32)
                z=lambda t: t[r,w,:,:].rearrange("p s q -> p (s q)")
                o=PSB[:,j*512:j*512+144]
                pe.matmul(o,z(n.ZQ),kw[r,:,8*w:8*w+12],start=True,stop=False)
                for i in range(3):
                    pe.matmul(o,z(n.ZB[0][i]),n.INDHB[r,:],start=False,stop=False)
                    last=pe.matmul(o,z(n.ZB[1][i]),n.INDWB[r,:],start=False,stop=(i==2))
            last.then_inc(n.s_qk,1)
        def V(w):
            if w>=1: pe.wait_ge(n.s_vc,st*8+w)
            for g in range(2):
                last=pe.matmul(PSB[0:72,6*512+g*P:6*512+(g+1)*P],n.XV[:,w,72*g:72*g+72],n.WV[:,:],start=True,stop=True)
            last.then_inc(n.s_v,1)
        S(0); V(0)
        for w in range(8):
            if w<7: S(w+1)
            pe.wait_ge(n.s_nrm,st*8+(w+1)); 
            if w>=1: pe.wait_ge(n.s_pta,st*8+(w+1)); pe.wait_ge(n.s_ptd,st*8+w)
            for j in range(4):
                for g in range(2):
                    o=(4+j//2)*512+((j%2)*2+g)*P
                    last=pe.transpose(PSB[0:72,o:o+P],n.PR_[:,w%2,j,72*g:72*g+72],ident)
            last.then_inc(n.s_tr,1)
            if w<7: V(w+1)
            pe.wait_ge(n.s_pta,st*8+(w+2)); pe.wait_ge(n.s_ptd,st*8+(w+1)); pe.wait_ge(n.s_vc,st*8+(w+1))
            if w>=1: pe.wait_ge(n.s_ao,st*8+w)
            for j in range(4):
                for g in range(2):
                    last=pe.matmul(PSB[32*j:32*j+32,7*512:7*512+P],n.VS[:,w%2,g,32*j:32*j+32],n.PTS[:,2*j+g,:],start=(g==0),stop=(g==1))
            last.then_inc(n.s_pv,1)
        pe.wait_ge(n.s_ao,st*8+8)
        for i in range(4):
            last=pe.matmul(PSB[:,6*512+P*i:6*512+P*(i+1)],n.AOT[:,P*i:P*(i+1)],n.WO[:,:],start=True,stop=True)
        last.then_inc(n.s_pj,1)
    barrier(pe,n,"pe",b,0)

KEEP=2047
def l0ffn_dve(dve,n,PSB,b,ident):
    Ln.dve(dve,n,b*4+1,1e-5)
    dve.tensor_scalar(n.RS1[:,:],n.RSTD[:,:],1.0,None,ALU.add)
    dve.memset(n.RK[:,:,:],0.0)
    dve.drain()
    for t in range(TILES):
        dve.tensor_scalar(n.X[:,t,:],n.X[:,t,:],n.RS1[:,t:t+1],n.NMR[:,t:t+1],ALU.mult,ALU.add)
    wrow=n.VPAD[:,0:IMGTOK]; junk=n.KPAD[:,0:IMGTOK]
    dve.wait_ge(n.s_wc,b*8+8)
    dve.tensor_tensor(junk.rearrange("p (t j) -> p t j",j=P),wrow.rearrange("p (t j) -> p t j",j=P),ident.unsqueeze(1).to_broadcast((P,TILES,P)),ALU.mult)
    dve.drain()
    dve.tensor_reduce(n.WCOL[:,:],junk.rearrange("p (t j) -> p t j",j=P),AX.X,ALU.add)
    dve.drain()
    for t in range(TILES):
        w=n.WCOL[:,t:t+1]
        if t: dve.tensor_scalar(junk[:,0:t*P],wrow[:,0:t*P],w,0.0,ALU.is_ge,ALU.add,accum_out=n.RK[:,0,t:t+1])
        if t<TILES-1: dve.tensor_scalar(junk[:,(t+1)*P:],wrow[:,(t+1)*P:],w,0.0,ALU.is_gt,ALU.add,accum_out=n.RK[:,1,t:t+1])
        blk=wrow[:,t*P:(t+1)*P]
        dve.scalar_tensor_tensor(out=junk[:,t*P:(t+1)*P],in0=blk,scalar=w,in1=n.LM[:,:],op0=ALU.is_ge,op1=ALU.mult,accum_out=n.RK[:,2,t:t+1])
        dve.drain()
        dve.scalar_tensor_tensor(out=junk[:,t*P:(t+1)*P],in0=blk,scalar=w,in1=n.UM,op0=ALU.is_gt,op1=ALU.mult,accum_out=n.RK[:,3,t:t+1])
        dve.drain()
    dve.tensor_reduce(n.RANK[:,:],n.RK[:,:,:].rearrange("p a t -> p t a"),AX.X,ALU.add)
    dve.drain()
    dve.scalar_tensor_tensor(out=n.GS[:,:],in0=n.RANK[:,:],scalar=float(KEEP),in1=n.WCOL[:,:],op0=ALU.is_lt,op1=ALU.mult)
    dve.drain()
    dve.wait_ge(n.s_ya,b*8+8)
    for t in range(TILES):
        dve.scalar_tensor_tensor(out=n.X[:,t,:],in0=n.Y[:,t,:],scalar=n.GS[:,t:t+1],in1=n.X[:,t,:],op0=ALU.mult,op1=ALU.add)
    barrier(dve,n,"dve",b,1)

def l0ffn_act(act,n,PSB,b):
    Ln.act(act,n,PSB,b*4+1,False)
    for g in range(8):
        act.wait_ge(n.s_w,b*8+(g+1))
        act.activation(n.VPAD[:,512*g:512*(g+1)],PSB[:,(g%2)*512:(g%2+1)*512],ACT.Identity,bias=n.BR[:,:]).then_inc(n.s_wc,1)
    def ycopy(g):
        act.wait_ge(n.s_y,b*8+(g+1))
        act.activation(n.Y[:,4*g:4*g+4,:],PSB[:,(6+g%2)*512:(7+g%2)*512].rearrange("p (t c) -> p t c",c=C),ACT.Copy).then_inc(n.s_ya,1)
    for g in range(8):
        for m in range(4):
            act.wait_ge(n.s_h,b*32+(4*g+m+1))
            if g>=2 and m==0: act.wait_ge(n.s_y,b*8+(g-1))
            act.activation(n.HTL[:,g%2,m,:],PSB[:,(2+m)*512:(3+m)*512],ACT.Gelu_apprx_tanh,bias=n.B1[:,m:m+1]).then_inc(n.s_ge,1)
        if g: ycopy(g-1)
    ycopy(7)
    barrier(act,n,"act",b,1)

def l0ffn_pe(pe,n,PSB,ident,ones,b):
    Ln.pe(pe,n,PSB,ident,b*4+1)
    pe.wait_ge(n.ln_cp,b*32+16)
    for g in range(8):
        if g>=2: pe.wait_ge(n.s_wc,b*8+(g-1))
        pe.matmul(PSB[:,(g%2)*512:(g%2+1)*512],n.WRB[:,:],n.XPAD[:,512*g:512*(g+1)],start=True,stop=True).then_inc(n.s_w,1)
    def H(g):
        for m in range(4):
            if g: pe.wait_ge(n.s_ge,b*32+(4*(g-1)+m+1))
            pe.matmul(PSB[:,(2+m)*512:(3+m)*512],n.W1[:,P*m:P*(m+1)],n.XPAD[:,512*g:512*(g+1)],start=True,stop=True).then_inc(n.s_h,1)
    H(0)
    for g in range(8):
        if g<7: H(g+1)
        pe.wait_ge(n.s_ge,b*32+(4*g+4))
        if g>=2: pe.wait_ge(n.s_ya,b*8+(g-1))
        for i in range(4):
            o=PSB[:,(6+g%2)*512+i*P:(6+g%2)*512+(i+1)*P]
            pe.matmul(o,ones[0:1,:],n.B2R[:,:],start=True,stop=False)
            for m in range(4):
                last=pe.matmul(o,n.HTL[:,g%2,m,i*P:(i+1)*P],n.W2[:,m,:],start=False,stop=(m==3))
        last.then_inc(n.s_y,1)
    barrier(pe,n,"pe",b,1)

def halves(n_,buf,g8,a,bb):
    out=[]
    for lo,dil in ((0,2),(64,3)):
        v=buf[lo:lo+64,:].rearrange("p (y x) -> p y x",y=70)
        out.append((lo,v[:,bass.ds(g8+(3+(a-1)*dil),8),3+(bb-1)*dil:3+(bb-1)*dil+64]))
    return out
def l1conv_dve(dve,n,PSB,b):
    dve.memset(n.KPAD[:,:],0.0); dve.memset(n.VPAD[:,:],0.0).then_inc(n.s_pz,1)
    Ln.dve(dve,n,b*4+2,1e-6)
    for g in range(8):
        dve.wait_ge(n.s_kv,b*8+(g+1))
        dve.tensor_copy(n.VPAD[:,:].rearrange("p (y x) -> p y x",y=70)[:,3+8*g:11+8*g,3:67],PSB[:,(2+g%2)*512:(3+g%2)*512].rearrange("p (y x) -> p y x",y=8)).then_inc(n.s_vvc,1)
    dve.drain()
    dve.wait_ge(n.s_kvc,b*8+8); dve.sem_inc(n.tick_dve,1)
    def product(g,c,k):
        if k==0: dve.wait_ge(n.s_cqc,c+2)
        if k>=3: dve.wait_ge(n.s_lg,c*9+(k-2))
        for lo,src in halves(n,n.KPAD,g*8,k//3,k%3):
            last=dve.tensor_tensor(n.PRD[lo:lo+64,k%3,:].rearrange("p (y x) -> p y x",y=8),n.QT[lo:lo+64,:].rearrange("p (y x) -> p y x",y=8),src,ALU.mult)
        last.then_inc(n.s_pr,1)
    def strip(g,c,more):
        dve.wait_ge(n.s_lg,c*9+9)
        lg=PSB[:,5*512:5*512+288]
        dve.tensor_reduce(n.LMX[:,:,:],lg.rearrange("p (t k h) -> p t h k",t=4,k=9),AX.X,ALU.max)
        dve.drain()
        for t in range(4):
            last=dve.tensor_tensor(n.LG[:,t,:].rearrange("p (k h) -> p k h",k=9),lg[:,72*t:72*(t+1)].rearrange("p (k h) -> p k h",k=9),n.LMX[:,t,:].unsqueeze(1).to_broadcast((P,9,8)),ALU.subtract)
        last.then_inc(n.s_sb,1)
        dve.wait_ge(n.s_ex,c+1)
        dve.tensor_reduce(n.LMX[:,:,:],n.LG[:,:,:].rearrange("p t (k h) -> p t h k",k=9),AX.X,ALU.add)
        dve.drain()
        dve.reciprocal(n.LMX[:,:,:],n.LMX[:,:,:])
        dve.drain()
        for t in range(4):
            v=n.LG[:,t,:].rearrange("p (k h) -> p k h",k=9)
            last=dve.tensor_tensor(v,v,n.LMX[:,t,:].unsqueeze(1).to_broadcast((P,9,8)),ALU.mult)
        last.then_inc(n.s_nm,1)
        for k in range(9):
            if more: product(g+1,c+1,k)
            dve.wait_ge(n.s_ep,c*9+(k+1))
            to=n.PR2[:,k%2,:] if k else n.ACC
            for lo,src in halves(n,n.VPAD,g*8,k//3,k%3):
                last=dve.tensor_tensor(to[lo:lo+64,:].rearrange("p (y x) -> p y x",y=8),PSB[lo:lo+64,(k%2)*512:(k%2+1)*512].rearrange("p (y x) -> p y x",y=8),src,ALU.mult)
            last.then_inc(n.s_p2,1)
            if k:
                dve.drain()
                last=dve.tensor_tensor(n.ACC,n.ACC,to,ALU.add)
                if k==8: last.then_inc(n.s_acc,1)
        dve.wait_ge(n.s_pp,c+1)
        xs=n.X[:,bass.ds(g*4,4),:]
        dve.tensor_tensor(xs,xs,PSB[:,7*512:8*512].rearrange("p (t c) -> p t c",t=4),ALU.add).then_inc(n.s_cxa,1)
    for k in range(9): product(0,b*8,k)
    with dve.Fori(0,7) as g: strip(g,b*8+g,True)
    strip(7,b*8+7,False)
    barrier(dve,n,"dve",b,2)

def l1conv_act(act,n,PSB,b):
    Ln.act(act,n,PSB,b*4+2,False)
    for g in range(8):
        act.wait_ge(n.s_kv,b*8+(g+1))
        act.activation(n.KPAD[:,:].rearrange("p (y x) -> p y x",y=70)[:,3+8*g:11+8*g,3:67],PSB[:,(g%2)*512:(g%2+1)*512].rearrange("p (y x) -> p y x",y=8),ACT.Copy).then_inc(n.s_kvc,1)
    def queries(c):
        act.wait_ge(n.s_cq,c+1)
        act.activation(n.QT[:,:],PSB[:,4*512:5*512],ACT.Copy).then_inc(n.s_cqc,1)
    def strip(c,more):
        act.wait_ge(n.s_sb,c+2)
        act.activation(n.LG[:,:,:],n.LG[:,:,:],ACT.Exp,scale=0.25).then_inc(n.s_ex,1)
        if more: queries(c+1)
        act.wait_ge(n.s_at,c+1)
        act.activation(n.AT[:,:],PSB[0:72,6*512:7*512],ACT.Copy).then_inc(n.s_atc,1)
    queries(b*8)
    with act.Fori(0,7) as g: strip(b*8+g,True)
    strip(b*8+7,False)
    barrier(act,n,"act",b,2)

def l1conv_pe(pe,n,PSB,ident,ones,b):
    Ln.pe(pe,n,PSB,ident,b*4+2)
    pe.wait_ge(n.ln_cp,b*32+24)
    for g in range(8):
        if g>=2: pe.wait_ge(n.s_kvc,b*8+(g-1)); pe.wait_ge(n.s_vvc,b*8+(g-1))
        x=n.XPAD[:,512*g:512*(g+1)]
        pe.matmul(PSB[:,(g%2)*512:(g%2+1)*512],n.WQKV[:,P:2*P],x,start=True,stop=True)
        pe.matmul(PSB[:,(2+g%2)*512:(3+g%2)*512],n.WQKV[:,2*P:3*P],x,start=True,stop=True).then_inc(n.s_kv,1)
    pe.wait_ge(n.s_kvc,b*8+8); pe.wait_ge(n.s_vvc,b*8+8); pe.sem_inc(n.tick_pe,1)
    def queries(g,c):
        pe.wait_ge(n.s_cqc,c+1); pe.sem_inc(n.tick_pe,1)
        pe.matmul(PSB[:,4*512:5*512],n.WQKV[:,0:P],n.XPAD[:,bass.ds(g*512,512)],start=True,stop=True).then_inc(n.s_cq,1)
    def logits(c,k):
        if k==0: pe.wait_ge(n.s_sb,c+1)
        pe.wait_ge(n.s_pr,c*9+(k+1))
        for t in range(4):
            o=5*512+72*t+8*k
            last=pe.matmul(PSB[:,o:o+8],n.PRD[:,k%3,P*t:P*(t+1)],n.HONE[:,:],start=True,stop=True)
        last.then_inc(n.s_lg,1)
    def strip(g,c,more):
        if more: queries(g+1,c+1)
        pe.wait_ge(n.s_cxa,c+1)
        pe.matmul(PSB[:,7*512:8*512],ones[0:1,:],n.BPR[:,:,:].rearrange("a t c -> a (t c)"),start=True,stop=False,skip_group_check=True)
        pe.wait_ge(n.s_nm,c+1); pe.wait_ge(n.s_atc,c+1)
        for t in range(4):
            last=pe.transpose(PSB[0:72,6*512+P*t:6*512+P*(t+1)],n.LG[:,t,:],ident)
        last.then_inc(n.s_at,1)
        pe.wait_ge(n.s_atc,c+2)
        def E(k):
            if k>=2: pe.wait_ge(n.s_p2,c*9+(k-1))
            pe.matmul(PSB[:,(k%2)*512:(k%2+1)*512],n.EXPN[:,k,:],n.AT[:,:],start=True,stop=True).then_inc(n.s_ep,1)
        E(0)
        for k in range(9):
            if k<8: E(k+1)
            if more: logits(c+1,k)
        pe.wait_ge(n.s_acc,c+1)
        for t in range(4):
            last=pe.matmul(PSB[:,7*512+P*t:7*512+P*(t+1)],n.ACC[:,P*t:P*(t+1)],n.WP[:,:],start=False,stop=True,skip_group_check=True)
        last.then_inc(n.s_pp,1)
    queries(0,b*8)
    for k in range(9): logits(b*8,k)
    with pe.Fori(0,7) as g: strip(g,b*8+g,True)
    strip(7,b*8+7,False)
    barrier(pe,n,"pe",b,2)

def gat_dve(dve,n,PSB,b):
    Ln.dve(dve,n,b*4+3,1e-5)
    dve.wait_ge(n.s_gt,b+1)
    h=PSB[:,0:512].rearrange("p (t c) -> p t c",c=16)
    dve.tensor_copy(n.TB[:,:,0:16],h)
    for a,(att,dst) in enumerate(((n.AS,n.TB[:,:,16:20]),(n.AD,n.ADB[:,:,:]))):
        dve.drain()
        dve.tensor_tensor(n.HM[:,:,:],h,att[:,:].unsqueeze(1).to_broadcast((P,TILES,16)),ALU.mult)
        dve.drain()
        last=dve.tensor_reduce(dst,n.HM[:,:,:].rearrange("p t (h e) -> p t h e",h=4),AX.X,ALU.add)
    last.then_inc(n.s_tb,1)
    dve.drain()
    dve.wait_ge(n.x3_st,b*16+16); dve.wait_ge(n.tn_st,b*16+16); dve.wait_ge(n.t_st,b*32+32); dve.sem_inc(n.tick_dve,1)
    barrier(dve,n,"dve",b,3)
def gat_act(act,n,PSB,b,d):
    act.dma_start(d["X3"].rearrange("(t p) c -> p t c",p=P)[:,bass.ds(b*TILES,TILES),:],n.X[:,:,:]).then_inc(n.x3_st,16)
    Ln.act(act,n,PSB,b*4+3,False)
    act.drain()
    act.wait_ge(n.ln_cp,b*32+32)
    act.dma_start(d["TNT"][:,bass.ds(b*IMGTOK,IMGTOK)],n.XPAD[:,0:IMGTOK]).then_inc(n.tn_st,16)
    act.wait_ge(n.s_tb,b+1)
    act.dma_start(d["T"].rearrange("(t p) c -> p t c",p=P)[:,bass.ds(b*TILES,TILES),:],n.TB[:,:,:]).then_inc(n.t_st,16)
    act.dma_start(d["ADT"].rearrange("(t p) c -> p t c",p=P)[:,bass.ds(b*TILES,TILES),:],n.ADB[:,:,:]).then_inc(n.t_st,16)
    barrier(act,n,"act",b,3)
def gat_pe(pe,n,PSB,ident,b):
    Ln.pe(pe,n,PSB,ident,b*4+3)
    pe.wait_ge(n.ln_cp,b*32+32)
    for t in range(TILES):
        last=pe.matmul(PSB[:,16*t:16*t+16],n.XPAD[:,P*t:P*(t+1)],n.WG[:,:],start=True,stop=True)
    last.then_inc(n.s_gt,1)
    barrier(pe,n,"pe",b,3)

P=128; NODES=16384; NT=NODES//P; COLS=4096; CH=64; NCH=COLS//CH; BIG=1e30; OUT_OF_RANGE=float(2**20)
IOA=bass.IndirectOffsetOnAxis

def declare_nodes(nc,ctx,n,SA,m):
    def sem(name):
        s=ctx.enter_context(nc.semaphore(name)); return s
    def sb(name,shape,dt=f32):
        t=ctx.enter_context(nc.sbuf_tensor(name,shape,dt)); return t
    n.np_mm, n.np_rdy, n.ad_ld, n.ad_sc, n.d0_rdy, n.d0_g = [sem(s) for s in ("np_mm", "np_rdy", "ad_ld", "ad_sc", "d0_rdy", "d0_g",)]
    n.d0_st, n.a2_ld, n.keep_rdy, n.fw_rdy, n.fw_exp = [sem(s) for s in ("d0_st", "a2_ld", "keep_rdy", "fw_rdy", "fw_exp",)]
    n.lc_sh, n.lc_in, n.lc_tr, n.lc_e, n.lc_ee = [sem(s) for s in ("lc_sh", "lc_in", "lc_tr", "lc_e", "lc_ee",)]
    n.lc_o, n.lc_t2, n.lc_tab, n.lc_st, n.tbn_ld, n.re_g = [sem(s) for s in ("lc_o", "lc_t2", "lc_tab", "lc_st", "tbn_ld", "re_g",)]
    n.ce_g, n.nd1, n.nd1e, n.nd2, n.nd2e, n.nd3 = [sem(s) for s in ("ce_g", "nd1", "nd1e", "nd2", "nd2e", "nd3",)]
    n.nd3e, n.g_rdy, n.moe_w, n.moe_h, n.moe_ge = [sem(s) for s in ("nd3e", "g_rdy", "moe_w", "moe_h", "moe_ge",)]
    n.moe_dv, n.edges_done, n.r_fill, n.src_rdy, n.ad_ld2 = [sem(s) for s in ("moe_dv", "edges_done", "r_fill", "src_rdy", "ad_ld2",)]
    n.rbs=[sem(f"rbs{i}") for i in range(2)]; n.moe_ys=[sem(f"moe_ys{i}") for i in range(2)]
    n.gath=[sem(f"gath{i}") for i in range(2)]; n.gst=[sem(f"gst{i}") for i in range(2)]; n.adc=[sem(f"adc{i}") for i in range(2)]; n.rst=[sem(f"rst{i}") for i in range(2)]
    n.moe_in=[sem(f"moe_in{i}") for i in range(2)]; n.moe_out=[sem(f"moe_out{i}") for i in range(2)]
    n.SIX=sb("SIX",[P,NT],i32); n.EIX=sb("EIX",[P,NT],i32); n.PIX=sb("PIX",[P,NT],i32); n.VAL=sb("VAL",[P,NT]); n.MUL=sb("MUL",[P,NT]); n.NSF=sb("NSF",[P,NT]); n.NT1=sb("NT1",[P,NT]); n.NT2=sb("NT2",[P,NT],i32)
    n.END=sb("END",[P,NT]); n.QS=sb("QS",[P,NT]); n.QE=sb("QE",[P,NT])
    n.D0=sb("D0",[P,1],i32); n.AD0=sb("AD0",[P,4]); n.GIX=[sb(f"GIX{i}",[P,CH],i32) for i in range(2)]
    n.IDW=sb("IDW",[P,P+1]); n.LCM=sb("LCM",[P,3,20]); n.LCD=sb("LCD",[P,4]); n.LCT=sb("LCT",[20,3,P]); n.MCX=sb("MCX",[20,P+1]); n.SCX=sb("SCX",[20,P+1]); n.LCE=sb("LCE",[20,2,P]); n.CTB=sb("CTB",[P,24])
    n.G4=sb("G4",[P,NT,4]); n.BG=sb("BG",[P,16]); n.GM=sb("GM",[P,16]); n.BT=sb("BT",[P,16])
    A=n.HTL[:,:,:,:].rearrange("p a b c -> p (a b c)")
    n.G=A[:,0:2560].rearrange("p (s c k) -> p s c k",s=2,k=20)
    n.ADC=A[:,2560:3072].rearrange("p (s c k) -> p s c k",s=2,k=4)
    n.ADX=A[:,3072:3584].rearrange("p (s c k) -> p s c k",s=2,k=4)
    X=n.XPAD[:,:]
    n.RB=X[:,0:3120].rearrange("p (s c k) -> p s c k",s=2,k=24)
    n.EE=X[:,3120:3632].rearrange("p (s c k) -> p s c k",s=2,k=4)
    n.PEN=X[:,3632:3760].rearrange("p (s c) -> p s c",s=2)
    n.FW=n.KPAD[:,2048:3072].rearrange("p (s f c k) -> p s f c k",s=2,f=2,k=4)
    n.V=n.KPAD[:,0:2048].rearrange("p (s c k) -> p s c k",s=2,k=16)
    n.RE=n.VPAD[:,0:3072].rearrange("p (t k) -> p t k",k=24)
    n.CE=n.KPAD[:,0:3072].rearrange("p (t k) -> p t k",k=24)
    n.TBN=SA[:,0:2560].rearrange("p (t k) -> p t k",k=20)
    n.ADN=m.fill[:,:].bitcast(f32).rearrange("p (t k) -> p t k",k=4)
    n.HM2=SA[:,0:8192].rearrange("p (s m c) -> p s m c",s=2,m=8)
    n.TNC=X[:,0:1024].rearrange("p (s c) -> p s c",s=2)
    n.X3C=X[:,1024:2048].rearrange("p (s t c) -> p s t c",s=2,t=4)
    n.WM1=A[:,1024:2048].rearrange("p (e c) -> p e c",e=4)
    n.WM2=A[:,2048:3072].rearrange("p (m c) -> p m c",m=8)
    n.B1M=A[:,3072:3080]; n.B2M=A[0:1,3584:4096]

def pos_pe(pe,n,PSB,ltri,ones,cnt):
    pe.matmul(PSB[:,0:P],ltri,cnt,start=True,stop=True)
    pe.matmul(PSB[:,P:2*P],ones,cnt,start=True,stop=True).then_inc(n.np_mm,1)
def pos_dve(dve,n,PSB,ones,cnt,m):
    dve.wait_ge(n.np_mm,1)
    dve.tensor_tensor_scan(n.NSF[:,:],ones,PSB[:,P:2*P],0.0,ALU.mult,ALU.add); dve.drain()
    dve.tensor_tensor(n.NSF[:,:],n.NSF[:,:],PSB[:,P:2*P],ALU.subtract); dve.drain()
    dve.tensor_tensor(n.NSF[:,:],n.NSF[:,:],PSB[:,0:P],ALU.add)
    dve.tensor_scalar(n.VAL[:,:],cnt,0.0,None,ALU.is_gt); dve.drain()
    K=m.KV[:,1,:]
    dve.tensor_tensor(n.END[:,:],n.NSF[:,:],cnt,ALU.add); dve.drain()
    dve.tensor_scalar(n.END[:,:],n.END[:,:],-1.0,0.0,ALU.add,ALU.max); dve.drain()
    divide(dve,n.NSF[:,:],K,n.NT2[:,:],n.QS[:,:],n.NT1[:,:])
    divide(dve,n.END[:,:],K,n.NT2[:,:],n.QE[:,:],n.NT1[:,:])
    dve.tensor_copy(n.PIX[:,:],n.QE[:,:])
    dve.tensor_tensor(n.MUL[:,:],n.QS[:,:],n.QE[:,:],ALU.not_equal)
    dve.scalar_tensor_tensor(out=n.NSF[:,:],in0=n.QS[:,:],scalar=K[:,3:4],in1=n.NSF[:,:],op0=ALU.mult,op1=ALU.add)
    dve.scalar_tensor_tensor(out=n.EIX[:,:],in0=n.QE[:,:],scalar=K[:,3:4],in1=n.END[:,:],op0=ALU.mult,op1=ALU.add)
    dve.tensor_scalar(n.NT1[:,:],cnt,0.0,OUT_OF_RANGE,ALU.is_equal,ALU.mult); dve.drain()
    dve.tensor_tensor(n.SIX[:,:],n.NSF[:,:],n.NT1[:,:],ALU.add)
    dve.tensor_tensor(n.MUL[:,:],n.MUL[:,:],n.VAL[:,:],ALU.mult).then_inc(n.np_rdy,1)
    dve.drain()

def edges_prep_dve(dve,n,SA,V):
    I=SA.bitcast(i32)
    s=lambda t,i: t[:,i*4096:(i+1)*4096]
    dve.wait_ge(n.a2_ld,16)
    dve.tensor_scalar(s(I,1),s(I,0),15,None,ALU.logical_shift_right).then_inc(n.src_rdy,1)
    dve.tensor_scalar(s(I,4),s(I,0),32767,None,ALU.bitwise_and); dve.drain()
    dve.tensor_copy(s(SA,2),s(I,4)); dve.drain()
    d=s(SA,2); k=s(SA,4)
    dve.tensor_scalar(n.D0[:,:],d[:,0:1],float(NODES-1),None,ALU.min).then_inc(n.d0_rdy,1)
    dve.tensor_tensor(k[:,1:],d[:,1:],d[:,0:COLS-1],ALU.is_equal)
    dve.memset(k[:,0:1],0.0); dve.drain()
    dve.memset(n.ADX[:,1,:,:],0.0)
    dve.memset(n.RB[:,1,CH,0:4],-BIG); dve.memset(n.RB[:,1,CH,4:24],0.0)
    dve.drain()
    dve.tensor_copy(n.LCD[:,0:1],d[:,0:1]); dve.tensor_copy(n.LCD[:,1:2],SA[:,bass.ds(V*128+(2*4096-1),1)]).then_inc(n.keep_rdy,1)
    dve.drain()
def edges_dve(dve,n,SA,V):
    k_=SA[:,4*4096:5*4096]
    def chunks(i):
        for s in range(2):
            j=i*2+s
            G=n.G[:,s]; K=k_[:,bass.ds(j*CH,CH)]; RB=n.RB[:,s]; E=n.EE[:,s]; PEN=n.PEN[:,s,:]; FW=n.FW[:,s]
            dve.wait_ge(n.rst[s],i*16+1)
            dve.tensor_copy(RB[:,0,:],n.RB[:,1-s,CH,:])
            dve.tensor_scalar(PEN,K,-1.0,BIG,ALU.add,ALU.mult)
            dve.wait_ge(n.adc[s],i*16+16)
            for h in range(4):
                dve.tensor_tensor_scan(n.ADX[:,s,:,h],K,n.ADC[:,s,:,h],n.ADX[:,1-s,CH-1,h:h+1],ALU.mult,ALU.add)
            dve.drain()
            dve.wait_ge(n.gath[s],i*(CH*16)+CH*16)
            dve.tensor_tensor(E,G[:,:,16:20],n.ADX[:,s],ALU.add); dve.drain()
            dve.scalar_tensor_tensor(out=E,in0=E,scalar=0.2,in1=E,op0=ALU.mult,op1=ALU.max); dve.drain()
            for h in range(4):
                dve.tensor_tensor_scan(RB[:,1:CH+1,h],PEN,E[:,:,h],RB[:,0,h:h+1],ALU.add,ALU.max)
            dve.drain()
            dve.tensor_tensor(FW[:,0],RB[:,0:CH,0:4],PEN.unsqueeze(2).to_broadcast((P,CH,4)),ALU.add)
            dve.tensor_tensor(FW[:,1],E,RB[:,1:CH+1,0:4],ALU.subtract); dve.drain()
            dve.tensor_tensor(FW[:,0],FW[:,0],RB[:,1:CH+1,0:4],ALU.subtract).then_inc(n.fw_rdy,1)
            dve.wait_ge(n.fw_exp,j+1)
            dve.tensor_tensor(n.V[:,s].rearrange("p c (h e) -> p c h e",h=4),G[:,:,0:16].rearrange("p c (h e) -> p c h e",h=4),FW[:,1].unsqueeze(3).to_broadcast((P,CH,4,4)),ALU.mult)
            for h in range(4):
                last=dve.tensor_tensor_scan(RB[:,1:CH+1,4+h],FW[:,0,:,h],FW[:,1,:,h],RB[:,0,4+h:5+h],ALU.mult,ALU.add)
            dve.drain()
            for c in range(16):
                last=dve.tensor_tensor_scan(RB[:,1:CH+1,8+c],FW[:,0,:,c//4],n.V[:,s,:,c],RB[:,0,8+c:9+c],ALU.mult,ALU.add)
            last.then_inc(n.rbs[s],1)
            dve.drain()
    with dve.Fori(0,NCH//2) as i:
        with dve.If(i<V): chunks(i)
    dve.drain().then_inc(n.edges_done,1)
def edges_act(act,n,d,V):
    R=d["R"].rearrange("(p c) k -> p c k",p=P)
    def chunks(i):
        for s in range(2):
            j=i*2+s
            act.wait_ge(n.fw_rdy,j+1)
            act.activation(n.FW[:,s],n.FW[:,s],ACT.Exp).then_inc(n.fw_exp,1)
            act.wait_ge(n.rbs[s],i+2)
            act.dma_start(R[:,bass.ds(j*CH,CH),:],n.RB[:,s,1:CH+1,:]).then_inc(n.rst[s],16)
    with act.Fori(0,NCH//2) as i:
        with act.If(i<V): chunks(i)
def edges_pool(pool,n,d,tick,V):
    for t in range(NT):
        if t==0: pool.wait_ge(n.np_rdy,1); pool.wait_ge(n.ad_ld,16)
        if t==NT-NT//IMGS: pool.wait_ge(n.ad_ld2,16)
        pool.indirect_dma_start(out=d["AEXP"],out_offset=IOA(ap=n.SIX[:,t:t+1],axis=0),in_=n.ADN[:,t,:],in_offset=None,bounds_check=4096*128-1,oob_is_err=False).then_inc(n.ad_sc,16)
    pool.wait_ge(n.d0_rdy,1)
    pool.indirect_dma_start(out=n.AD0[:,:],out_offset=None,in_=d["ADT"],in_offset=IOA(ap=n.D0[:,:],axis=0)).then_inc(n.d0_g,16)
    def gather(i):
        for s in range(2):
            pool.wait_ge(n.gst[s],i*16+16); pool.sem_inc(tick,1)
            pool.wait_ge(n.rbs[s],i+1); pool.sem_inc(tick,1)
            for c in range(CH):
                pool.indirect_dma_start(out=n.G[:,s,c,:],out_offset=None,in_=d["T"],in_offset=IOA(ap=n.GIX[s][:,c:c+1],axis=0)).then_inc(n.gath[s],16)
    with pool.Fori(0,NCH//2) as i:
        with pool.If(i<V): gather(i)
    for s in range(2): pool.wait_ge(n.rst[s],V*16+1); pool.sem_inc(tick,1)
    pool.wait_ge(n.r_fill,BLOCKS*96)
    for t in range(NT):
        pool.indirect_dma_start(out=n.RE[:,t,:],out_offset=None,in_=d["R"],in_offset=IOA(ap=n.EIX[:,t:t+1],axis=0)).then_inc(n.re_g,16)
    pool.wait_ge(n.lc_st,16)
    for t in range(NT):
        pool.indirect_dma_start(out=n.CE[:,t,:],out_offset=None,in_=d["CT"],in_offset=IOA(ap=n.PIX[:,t:t+1],axis=0)).then_inc(n.ce_g,16)
def edges_sync_fill(sp,m,n,d,V):
    R=d["R"].rearrange("(p c) k -> p (c k)",p=P)
    with sp.Fori(0,BLOCKS) as i:
        with sp.If(V<=i):
            for q in range(6): sp.dma_start(R[:,bass.ds(i*3072+q*512,512)],m.zero[:,:]).then_inc(n.r_fill,16)
        with sp.If(i<V): sp.sem_inc(n.r_fill,96)
def edges_sync(sp,n,d,SA,tick,A2,V):
    I=SA.bitcast(i32)
    sp.dma_start(I[:,0:4096],A2.rearrange("(p c) o -> p (c o)",p=P)).then_inc(n.a2_ld,16)
    adt=d["ADT"].rearrange("(t p) c -> p t c",p=P); first=NT-NT//IMGS
    sp.wait_ge(n.bar_dve,SE*(IMGS-1))
    sp.dma_start(n.ADN[:,0:first],adt[:,0:first]).then_inc(n.ad_ld,16)
    sp.wait_ge(n.bar_dve,SE*IMGS)
    sp.dma_start(n.ADN[:,first:],adt[:,first:]).then_inc(n.ad_ld2,16)
    A=d["AEXP"].rearrange("(p c) k -> p c k",p=P)
    def sources(i,s):
        sp.dma_start(n.GIX[s][:,:],I[:,bass.ds((i*2+s)*CH+4096,CH)]).then_inc(n.gst[s],16)
    sp.wait_ge(n.src_rdy,1)
    for s in range(2): sources(0,s)
    sp.wait_ge(n.keep_rdy,1)
    sp.dma_start(n.TBN,d["T"].rearrange("(t p) c -> p t c",p=P)).then_inc(n.tbn_ld,16)
    for t,k in ((n.BG,"b_gat"),(n.GM,"gamma"),(n.BT,"beta")):
        sp.dma_start(t[:,:],d[k].rearrange("(a n) -> a n",a=1).to_broadcast((P,16))).then_inc(n.tbn_ld,16)
    sp.wait_ge(n.ad_sc,16*NT); sp.wait_ge(n.d0_g,16)
    sp.dma_start(A[:,0,:],n.AD0[:,:]).then_inc(n.d0_st,16)
    sp.wait_ge(n.d0_st,16)
    def stage(i):
        for s in range(2):
            j=i*2+s
            if not (isinstance(i,int) and i==0): sp.wait_ge(n.gath[s],i*(CH*16)); sp.sem_inc(tick,1); sources(i,s)
            sp.wait_ge(n.rbs[s],i+1); sp.sem_inc(tick,1)
            sp.dma_start(n.ADC[:,s],A[:,bass.ds(j*CH,CH),:]).then_inc(n.adc[s],16)
    stage(0)
    with sp.Fori(1,NCH//2) as i:
        with sp.If(i<V): stage(i)
def carry_dve(dve,n,PSB):
    L=n.RB[:,1,CH,:]
    dve.wait_ge(n.lc_sh,1)
    dve.tensor_tensor(n.LCD[:,2:3],n.LCD[:,0:1],n.LCD[:,1:2],ALU.is_equal)
    dve.tensor_tensor(n.LCD[:,3:4],n.LCD[:,0:1],PSB[:,0:1],ALU.is_equal); dve.drain()
    dve.tensor_tensor(n.LCD[:,2:3],n.LCD[:,2:3],n.LCD[:,3:4],ALU.mult); dve.drain()
    dve.tensor_scalar(n.LCD[:,3:4],n.LCD[:,2:3],-1.0,BIG,ALU.add,ALU.mult); dve.drain()
    dve.tensor_copy(n.LCM[:,2,:],n.LCD[:,3:4].to_broadcast((P,20)))
    dve.tensor_copy(n.LCM[:,0,0:4],L[:,0:4])
    dve.tensor_copy(n.LCM[:,0,4:20].rearrange("p (h e) -> p h e",h=4),L[:,0:4].unsqueeze(2).to_broadcast((P,4,4)))
    dve.tensor_copy(n.LCM[:,1,:],L[:,4:24]).then_inc(n.lc_in,1)
    dve.memset(n.MCX[:,0:1],-BIG); dve.memset(n.SCX[:,0:1],0.0)
    dve.wait_ge(n.lc_tr,1)
    dve.tensor_copy(n.LCT[:,:,:],PSB[0:20,0:384].rearrange("p (a c) -> p a c",a=3)); dve.drain()
    lm,ls,pc=(n.LCT[:,i,:] for i in range(3))
    dve.tensor_tensor_scan(n.MCX[:,1:],pc,lm,-BIG,ALU.add,ALU.max); dve.drain()
    dve.tensor_tensor(n.LCE[:,0,:],n.MCX[:,0:P],pc,ALU.add)
    dve.tensor_tensor(n.LCE[:,1,:],lm,n.MCX[:,1:],ALU.subtract); dve.drain()
    dve.tensor_tensor(n.LCE[:,0,:],n.LCE[:,0,:],n.MCX[:,1:],ALU.subtract).then_inc(n.lc_e,1)
    dve.wait_ge(n.lc_ee,1)
    dve.tensor_tensor(n.LCE[:,1,:],n.LCE[:,1,:],ls,ALU.mult); dve.drain()
    dve.tensor_tensor_scan(n.SCX[:,1:],n.LCE[:,0,:],n.LCE[:,1,:],0.0,ALU.mult,ALU.add).then_inc(n.lc_o,1)
    dve.wait_ge(n.lc_t2,1)
    dve.tensor_copy(n.CTB[:,0:4],PSB[:,0:4]); dve.tensor_copy(n.CTB[:,4:24],PSB[:,20:40]).then_inc(n.lc_tab,1)
def carry_pe(pe,n,PSB,ident):
    pe.wait_ge(n.edges_done,1)
    pe.matmul(PSB[:,0:1],n.IDW[:,0:P],n.LCD[:,1:2],start=True,stop=True).then_inc(n.lc_sh,1)
    pe.wait_ge(n.lc_in,1)
    for i in range(3): last=pe.transpose(PSB[0:20,i*P:(i+1)*P],n.LCM[:,i,:],ident)
    last.then_inc(n.lc_tr,1)
    pe.wait_ge(n.lc_o,1)
    pe.transpose(PSB[:,0:20],n.MCX[:,0:P],ident[0:20,0:20])
    pe.transpose(PSB[:,20:40],n.SCX[:,0:P],ident[0:20,0:20]).then_inc(n.lc_t2,1)
def carry_act(act,n,d):
    act.wait_ge(n.lc_e,1)
    act.activation(n.LCE[:,:,:],n.LCE[:,:,:],ACT.Exp).then_inc(n.lc_ee,1)
    act.wait_ge(n.lc_tab,1)
    act.dma_start(d["CT"],n.CTB[:,:]).then_inc(n.lc_st,16)
def node_dve(dve,n,SA):
    o=[4096]
    def tmp(k):
        a=SA[:,o[0]:o[0]+NT*k]; o[0]+=NT*k
        return a.rearrange("p (t k) -> p t k",k=k)
    mE,mC,mS,M=tmp(4),tmp(4),tmp(4),tmp(4); DEN=tmp(4); MSG=tmp(16); T16=tmp(16); SC=tmp(4); MN=tmp(1); VR=tmp(1); I1=tmp(4); I2=tmp(4); M1=tmp(1); M2=tmp(1); FR=tmp(1); T1=tmp(1)
    dr=dve.drain
    b1=lambda a,k: a.to_broadcast((P,NT,k))
    h4=lambda a: a.rearrange("p t (h e) -> p t h e",h=4)
    be=lambda a: a.unsqueeze(3).to_broadcast((P,NT,4,4))
    dve.wait_ge(n.tbn_ld,16*4); dve.wait_ge(n.ad_ld,16); dve.wait_ge(n.ad_ld2,16)
    dve.tensor_tensor(mS,n.TBN[:,:,16:20],n.ADN[:,:,:],ALU.add)
    dve.tensor_scalar(n.VAL[:,:],n.VAL[:,:],-1.0,BIG,ALU.add,ALU.mult); dve.tensor_scalar(n.MUL[:,:],n.MUL[:,:],-1.0,BIG,ALU.add,ALU.mult); dr()
    dve.scalar_tensor_tensor(out=mS,in0=mS,scalar=0.2,in1=mS,op0=ALU.mult,op1=ALU.max)
    dve.wait_ge(n.re_g,16*NT)
    dve.tensor_tensor(mE,n.RE[:,:,0:4],n.VAL[:,:].unsqueeze(2).to_broadcast((P,NT,4)),ALU.add)
    dve.wait_ge(n.ce_g,16*NT)
    dve.tensor_tensor(mC,n.CE[:,:,0:4],n.MUL[:,:].unsqueeze(2).to_broadcast((P,NT,4)),ALU.add); dr()
    dve.tensor_tensor(M,mE,mC,ALU.max); dr()
    dve.tensor_tensor(M,M,mS,ALU.max); dr()
    for a in (mE,mC): dve.tensor_tensor(a,a,M,ALU.subtract)
    dve.tensor_tensor(mS,mS,M,ALU.subtract).then_inc(n.nd1,1)
    dve.wait_ge(n.nd1e,1)
    dve.tensor_tensor(DEN,n.RE[:,:,4:8],mE,ALU.mult)
    dve.tensor_tensor(M,n.CE[:,:,4:8],mC,ALU.mult)
    dve.tensor_tensor(h4(MSG),h4(n.RE[:,:,8:24]),be(mE),ALU.mult)
    dve.tensor_tensor(h4(T16),h4(n.CE[:,:,8:24]),be(mC),ALU.mult); dr()
    dve.tensor_tensor(DEN,DEN,M,ALU.add); dve.tensor_tensor(MSG,MSG,T16,ALU.add); dr()
    dve.tensor_tensor(DEN,DEN,mS,ALU.add); dve.tensor_tensor(h4(T16),h4(n.TBN[:,:,0:16]),be(mS),ALU.mult); dr()
    dve.tensor_tensor(MSG,MSG,T16,ALU.add); dve.tensor_scalar(DEN,DEN,1e-16,None,ALU.add); dr()
    dve.reciprocal(DEN,DEN); dr()
    dve.tensor_tensor(h4(MSG),h4(MSG),be(DEN),ALU.mult); dr()
    bc=lambda a: a[:,:].unsqueeze(1).to_broadcast((P,NT,16))
    dve.tensor_tensor(MSG,MSG,bc(n.BG),ALU.add); dr()
    dve.tensor_reduce(MN,MSG,AX.X,ALU.add); dr()
    dve.tensor_scalar(MN,MN,1.0/16,None,ALU.mult); dr()
    dve.tensor_tensor(MSG,MSG,b1(MN,16),ALU.subtract); dr()
    dve.tensor_tensor(T16,MSG,MSG,ALU.mult); dr()
    dve.tensor_reduce(VR,T16,AX.X,ALU.add); dr()
    dve.tensor_scalar(VR,VR,1.0/16,1e-5,ALU.mult,ALU.add).then_inc(n.nd2,1)
    dve.wait_ge(n.nd2e,1)
    dve.reciprocal(VR,VR); dr()
    dve.tensor_tensor(MSG,MSG,b1(VR,16),ALU.mult); dr()
    dve.tensor_tensor(MSG,MSG,bc(n.GM),ALU.mult); dr()
    dve.tensor_tensor(MSG,MSG,bc(n.BT),ALU.add); dr()
    dve.tensor_reduce(SC,MSG.rearrange("p t (h e) -> p t e h",h=4),AX.X,ALU.add); dr()
    dve.tensor_scalar(SC,SC,0.25,None,ALU.mult); dr()
    def first(mx,ind):
        dve.tensor_reduce(mx,SC,AX.X,ALU.max); dr()
        dve.tensor_tensor(ind,SC,b1(mx,4),ALU.is_equal)
        dve.memset(FR,1.0); dr()
        for e in range(4):
            dve.tensor_tensor(ind[:,:,e:e+1],ind[:,:,e:e+1],FR,ALU.mult); dr()
            dve.tensor_tensor(FR,FR,ind[:,:,e:e+1],ALU.subtract); dr()
    first(M1,I1)
    dve.tensor_scalar(T16[:,:,0:4],I1,-3e38,None,ALU.mult); dr()
    dve.tensor_tensor(SC,SC,T16[:,:,0:4],ALU.add); dr()
    first(M2,I2)
    dve.tensor_tensor(T1,M2,M1,ALU.subtract).then_inc(n.nd3,1)
    dve.wait_ge(n.nd3e,1)
    dve.tensor_scalar(M1,T1,1.0,None,ALU.add); dr()
    dve.reciprocal(M1,M1); dr()
    dve.tensor_tensor(M2,T1,M1,ALU.mult); dr()
    dve.tensor_tensor(I1,I1,b1(M1,4),ALU.mult); dve.tensor_tensor(I2,I2,b1(M2,4),ALU.mult); dr()
    dve.tensor_tensor(n.G4[:,:,:],I1,I2,ALU.add).then_inc(n.g_rdy,1)
    dr()
def node_act(act,n,SA):
    o=4096
    act.wait_ge(n.nd1,1)
    act.activation(SA[:,o:o+NT*12],SA[:,o:o+NT*12],ACT.Exp).then_inc(n.nd1e,1)
    act.wait_ge(n.nd2,1)
    vr=o+NT*(4*5+32+4+1)
    act.activation(SA[:,vr:vr+NT],SA[:,vr:vr+NT],ACT.Sqrt).then_inc(n.nd2e,1)
    t1=vr+NT*(1+8+3)
    act.wait_ge(n.nd3,1)
    act.activation(SA[:,t1:t1+NT],SA[:,t1:t1+NT],ACT.Exp).then_inc(n.nd3e,1)
NCK=NODES//512
def moe_sync(sp,n,d,tick):
    sp.wait_ge(n.edges_done,1)
    for dst,k in ((n.WM1,"W1"),(n.WM2,"W2"),(n.B1M,"b1mT"),(n.B2M,"b2m")):
        src=d[k]
        if k=="W1": src=src.rearrange("e c h -> c e h")
        if k=="W2": src=src.rearrange("e (f p) o -> p (e f) o",p=P)
        if k=="b2m": src=src.rearrange("e c -> (e c)").rearrange("(a n) -> a n",a=1)
        sp.dma_start(dst,src).then_inc(n.moe_w,16)
    x3=d["X3"].rearrange("(t p) c -> p t c",p=P)
    sp.wait_ge(n.g_rdy,1)
    def load(i):
        for s in range(2):
            j=i*2+s
            if not (isinstance(i,int) and i==0): sp.wait_ge(n.moe_out[s],i*16); sp.sem_inc(tick,1)
            sp.dma_start(n.TNC[:,s,:],d["TNT"][:,bass.ds(j*512,512)]).then_inc(n.moe_in[s],16)
            sp.dma_start(n.X3C[:,s],x3[:,bass.ds(j*4,4),:]).then_inc(n.moe_in[s],16)
    load(0)
    with sp.Fori(1,NCK//2) as i: load(i)
def moe_pe(pe,n,PSB,ones):
    pe.wait_ge(n.moe_w,64)
    with pe.Fori(0,NCK//2) as i:
        for s in range(2):
            j=i*2+s
            pe.wait_ge(n.moe_in[s],i*32+32)
            for m in range(8):
                (pe.wait_ge(n.moe_ge,j*8+(m-3)) if m>=4 else None)
                pe.matmul(PSB[:,(m%4)*512:(m%4+1)*512],n.WM1[:,m//2,(m%2)*P:(m%2+1)*P],n.TNC[:,s,:],start=True,stop=True).then_inc(n.moe_h,1)
            for t in range(4):
                if t==0: pe.wait_ge(n.moe_ge,j*8+8); pe.wait_ge(n.moe_dv,j*4+1)
                o=PSB[:,(4+t)*512:(5+t)*512]
                pe.matmul(o,ones[0:1,:],n.B2M,start=True,stop=False,skip_group_check=True)
                for m in range(8):
                    last=pe.matmul(PSB[:,(4+t)*512+(m//2)*P:(4+t)*512+(m//2+1)*P],n.HM2[:,s,m,P*t:P*(t+1)],n.WM2[:,m,:],start=False,stop=(m==7),skip_group_check=True)
                last.then_inc(n.moe_ys[s],1)
def moe_act(act,n,PSB):
    act.wait_ge(n.moe_w,64)
    with act.Fori(0,NCK//2) as i:
        for s in range(2):
            j=i*2+s
            for m in range(8):
                act.wait_ge(n.moe_h,j*8+(m+1))
                if m==0: act.wait_ge(n.moe_ys[s],i*4+1)
                act.activation(n.HM2[:,s,m,:],PSB[:,(m%4)*512:(m%4+1)*512],ACT.Gelu,bias=n.B1M[:,m:m+1]).then_inc(n.moe_ge,1)
def moe_pool(pool,n,out,tick):
    o=out.rearrange("(t p) c -> p t c",p=P)
    with pool.Fori(0,NCK//2) as i:
        for s in range(2):
            j=i*2+s
            pool.wait_ge(n.moe_dv,j*4+5); pool.sem_inc(tick,1)
            pool.dma_start(o[:,bass.ds(j*4,4),:],n.X3C[:,s]).then_inc(n.moe_out[s],16)
    for s in range(2): pool.wait_ge(n.moe_out[s],NCK//2*16)
def moe_dve(dve,n,PSB):
    with dve.Fori(0,NCK//2) as i:
        for s in range(2):
            j=i*2+s
            for t in range(4):
                dve.wait_ge(n.moe_ys[s],i*4+(t+2))
                for e in range(4):
                    x=n.X3C[:,s,t,:]
                    last=dve.scalar_tensor_tensor(out=x,in0=PSB[:,(4+t)*512+e*P:(4+t)*512+(e+1)*P],scalar=n.G4[:,bass.ds(j*4+t,1),e],in1=x,op0=ALU.mult,op1=ALU.add)
                    if e<3: dve.drain()
                last.then_inc(n.moe_dv,1)

EDGES=524288; SEGS=8; STEPS=COLS//SEGS; INVALID=NODES; DIG=128
NI=STEPS//4; ROUNDS=NI//2; BEFORE=2

def declare_sort(nc,ctx):
    class N: pass
    m=N()
    def sb(name,shape,dt=f32):
        t=ctx.enter_context(nc.sbuf_tensor(name,shape,dt)); return t
    def sem(name):
        s=ctx.enter_context(nc.semaphore(name)); return s
    m.SA=sb("SA_",[P,5*COLS])[:,:]; m.SI=m.SA.bitcast(i32)
    m.S=[m.SA[:,i*COLS:(i+1)*COLS] for i in range(5)]; m.SJ=[m.SI[:,i*COLS:(i+1)*COLS] for i in range(5)]
    m.SB=sb("SB_",[P,5120])[:,:]
    SBb=m.SB.bitcast(bf16)
    oh=lambda i: SBb[:,i*2048:(i+1)*2048].rearrange("p (u s v) -> p u s v",u=2,s=SEGS)
    m.OHL,m.OHH,m.junk=oh(0),oh(1),oh(2)
    m.Tc=m.SB[:,3072:4096].rearrange("p (s v) -> p s v",s=SEGS); m.INI=m.SB[:,4096:5120].rearrange("p (s v) -> p s v",s=SEGS)
    m.ident,m.ltri,m.ones,m.iotaf,m.tot,m.TT,m.cnt=[sb(t,[P,P]) for t in ("ident","ltri","ones","iotaf","tot","TT","cnt")]
    m.identb=sb("identb",[P,P],bf16); m.iotab=sb("iotab",[P,P],bf16); m.zb=sb("zb",[P,512],bf16); m.big=sb("big",[P,SEGS,4]); m.fill=sb("fill",[P,512],i32); m.zero=sb("zero",[P,512])
    m.VF=sb("VF",[P,2]); m.VI=sb("VI",[P,2],i32); m.KV=sb("KV",[P,2,4]); m.QI=sb("QI",[P,32],i32); m.QR=sb("QR",[P,32]); m.QT=sb("QTm",[P,32])
    m.DGB=sb("DGB",[P,SEGS,8],bf16); m.DGF=sb("DGF",[P,SEGS,4]); m.RKT=sb("RKT",[P,SEGS,4]); m.NH=sb("NH",[P,SEGS,4])
    m.dig_rdy, m.ohh_rdy, m.cnt_mm = [sem(s) for s in ("dig_rdy", "ohh_rdy", "cnt_mm",)]
    m.v_rdy, m.oh_rank, m.rank_done = [sem(s) for s in ("v_rdy", "oh_rank", "rank_done",)]
    m.IX=[sb(f"IX{i}",[P,32],i32) for i in range(2)]; m.PY=[sb(f"PY{i}",[P,32],i32) for i in range(2)]
    m.c_load, m.e_load, m.fill_rdy, m.fill_done, m.const_rdy, m.oh_rdy = [sem(s) for s in ("c_load", "e_load", "fill_rdy", "fill_done", "const_rdy", "oh_rdy",)]
    m.oh_free, m.hist_done, m.tt_rdy, m.lt_done, m.ini_rdy, m.accA = [sem(s) for s in ("oh_free", "hist_done", "tt_rdy", "lt_done", "ini_rdy", "accA",)]
    m.accB, m.exA, m.exB, m.pos_rdy, m.re_load, m.tick_sp = [sem(s) for s in ("accB", "exA", "exB", "pos_rdy", "re_load", "tick_sp",)]
    m.tick_pool, = [sem(s) for s in ("tick_pool",)]
    m.staged=[sem(f"staged{i}") for i in range(2)]; m.scat=[[sem(f"scat{r}{i}") for i in range(2)] for r in range(2)]
    return m

BLOCKS=32
def blocks(eng,m):
    eng.wait_ge(m.v_rdy,1)
    return eng.value_load(m.VI[0:1,0:1],min_val=1,max_val=BLOCKS)
def divide(dve,x,K,qi,r,t):
    dve.tensor_scalar(qi,x,K[:,2:3],None,ALU.mult); dve.drain()
    dve.tensor_copy(r,qi); dve.drain()
    dve.scalar_tensor_tensor(out=t,in0=r,scalar=K[:,1:2],in1=x,op0=ALU.mult,op1=ALU.add); dve.drain()
    dve.scalar_tensor_tensor(out=r,in0=t,scalar=0.0,in1=r,op0=ALU.is_lt,op1=ALU.subtract); dve.drain()
    dve.scalar_tensor_tensor(out=r,in0=t,scalar=K[:,0:1],in1=r,op0=ALU.is_ge,op1=ALU.subtract); dve.drain()
def block_count_dve(dve,m):
    f,i=m.VF[:,:],m.VI[:,:]
    dve.tensor_scalar(i[:,1:2],m.tot[:,P-1:P],16383.0,None,ALU.add); dve.drain()
    dve.tensor_scalar(i[:,1:2],i[:,1:2],14,None,ALU.logical_shift_right); dve.drain()
    dve.tensor_copy(f[:,1:2],i[:,1:2]); dve.drain()
    dve.tensor_scalar(f[:,0:1],f[:,1:2],1.0,None,ALU.max); dve.drain()
    for a,(w,full) in enumerate(((16.0,STEPS),(128.0,COLS))):
        dve.tensor_scalar(m.KV[:,a,0:1],f[:,0:1],w,None,ALU.mult)
        dve.tensor_scalar(m.KV[:,a,1:2],f[:,0:1],-w,None,ALU.mult)
        dve.tensor_scalar(m.KV[:,a,3:4],f[:,0:1],-w,float(full),ALU.mult,ALU.add)
    dve.drain()
    for a in range(2): dve.reciprocal(m.KV[:,a,2:3],m.KV[:,a,0:1])
    dve.tensor_copy(i[:,0:1],f[:,0:1]).then_inc(m.v_rdy,1)
    dve.drain()

def sort_sync_loads(sp,m,d):
    for t,src in ((m.ident,"ident"),(m.ltri,"ltri"),(m.iotaf,"iota")):
        sp.dma_start(t[:,:],d[src]).then_inc(m.c_load,16)
    sp.dma_start(m.SJ[4],d["edges"][0].rearrange("(p c) -> p c",p=P)).then_inc(m.e_load,16)
    sp.dma_start(m.SJ[1],d["edges"][1].rearrange("(p c) -> p c",p=P)).then_inc(m.e_load,16)
def sort_sync_fill(sp,m,d):
    sp.wait_ge(m.fill_rdy,2)
    for A in ("A1","A2"):
        a=d[A].rearrange("(q p c) o -> q p (c o)",p=P,c=512)
        for q in range(EDGES//(P*512)): sp.dma_start(a[q],m.fill[:,:]).then_inc(m.fill_done,16)
    a=d["AEXP"].rearrange("(p c) k -> p (c k)",p=P)
    for q in range(32): sp.dma_start(a[:,512*q:512*(q+1)],m.zero[:,:]).then_inc(m.fill_done,16)
FILLS=16*(2*EDGES//(P*512)+32)
def sort_sync(sp,m,d,r,V):
    if r==1:
        for s in range(2): sp.wait_ge(m.scat[0][s],512*ROUNDS)
        sp.dma_start(m.SJ[0],d["A1"].rearrange("(p c) o -> p (c o)",p=P)).then_inc(m.re_load,16)
    pk=m.SJ[0].rearrange("p (s k) -> p s k",s=SEGS); ps=m.SJ[1].rearrange("p (s k) -> p s k",s=SEGS)
    def stage(i):
        for s in range(2):
            g=i*2+s
            sp.wait_ge(m.pos_rdy,g+(r*NI+1)); sp.sem_inc(m.tick_sp,1)
            if not (isinstance(i,int) and i==0): sp.wait_ge(m.scat[r][s],i*512); sp.sem_inc(m.tick_sp,1)
            sp.dma_start(m.IX[s][:,:],ps[:,:,bass.ds(g*4,4)]).then_inc(m.staged[s],16)
            sp.dma_start(m.PY[s][:,:],pk[:,:,bass.ds(g*4,4)]).then_inc(m.staged[s],16)
    stage(0)
    with sp.Fori(1,ROUNDS) as i:
        if r==0: stage(i)
        else:
            with sp.If(i<V*2): stage(i)
def sort_pool(pool,m,d,r,V):
    if r==0: pool.wait_ge(m.fill_done,FILLS)
    A=d[("A1","A2")[r]]
    def scatter(i):
        for s in range(2):
            pool.wait_ge(m.staged[s],i*32+(r*ROUNDS*32+32)); pool.sem_inc(m.tick_pool,1)
            for c in range(32):
                pool.indirect_dma_start(out=A,out_offset=IOA(ap=m.IX[s][:,c:c+1],axis=0),in_=m.PY[s][:,c:c+1],in_offset=None,bounds_check=EDGES-1,oob_is_err=False).then_inc(m.scat[r][s],16)
    with pool.Fori(0,ROUNDS) as i:
        if r==0: scatter(i)
        else:
            with pool.If(i<V*2): scatter(i)
def sort_dve_prep(dve,m):
    S,SJ=m.S,m.SJ
    dve.memset(m.ones[:,:],1.0); dve.memset(m.zb[:,:],0.0)
    dve.wait_ge(m.c_load,48)
    dve.tensor_copy(m.identb[:,:],m.ident[:,:])
    dve.tensor_copy(m.iotab[:,:],m.iotaf[:,:]).then_inc(m.const_rdy,1)
    dve.wait_ge(m.e_load,32)
    dve.tensor_scalar(S[3],SJ[1],float(INVALID),None,ALU.min)
    dve.tensor_scalar(SJ[2],SJ[4],float(NODES-1),None,ALU.min); dve.drain()
    dve.tensor_copy(SJ[1],S[3])
    dve.tensor_scalar(SJ[0],SJ[2],15,None,ALU.logical_shift_left); dve.drain()
    dve.tensor_tensor(SJ[0],SJ[0],SJ[1],ALU.bitwise_or)
    dve.tensor_scalar(SJ[4],SJ[1],127,None,ALU.bitwise_and); dve.drain()
    dve.tensor_copy(S[2],SJ[4]); dve.drain()
    dve.tensor_scalar(S[4],S[3],float(INVALID),1000.0,ALU.is_ge,ALU.mult); dve.drain()
    dve.tensor_tensor(S[2],S[2],S[4],ALU.add); dve.drain()
    dve.tensor_scalar(SJ[4],SJ[1],7,None,ALU.logical_shift_right); dve.drain()
    dve.tensor_copy(S[3],SJ[4]).then_inc(m.dig_rdy,1); dve.drain()
def sort_act(act,m,AB):
    v=lambda t,i: t.rearrange("p (s k) -> p s k",s=SEGS)[:,:,bass.ds(i*4,4)]
    act.wait_ge(m.dig_rdy,1)
    with act.Fori(0,NI) as i:
        act.activation(m.NH[:,:,:],v(m.S[3],i),ACT.Copy,scale=-1.0); act.drain()
        for u in range(4):
            k=i*4+u
            for s in range(SEGS): act.activation(AB[:,u%2,s,:],m.iotab[:,:],ACT.Abs,bias=m.NH[:,s,u:u+1])
            act.drain()
            act.wait_ge(m.cnt_mm,k+1)
            act.activation(m.OHH[:,u%2,:,:],AB[:,u%2],ACT.Relu,scale=-1.0,bias=m.ones[:,0:1]).then_inc(m.ohh_rdy,1)
def sort_dve(dve,m,PS,r,V=None):
    S,SJ=m.S,m.SJ
    if r==1:
        dve.wait_ge(m.re_load,16); dve.wait_ge(m.rank_done,1)
        for s in range(2): dve.wait_ge(m.staged[s],32*ROUNDS)
        dve.tensor_scalar(SJ[4],SJ[0],32767,7,ALU.bitwise_and,ALU.logical_shift_right); dve.drain()
        dve.tensor_copy(S[2],SJ[4]); dve.drain()
    iota8=m.iotab[:,:].unsqueeze(1).to_broadcast((P,SEGS,P))
    seg=lambda t,i,w: t.rearrange("p (s k) -> p s k",s=SEGS)[:,:,bass.ds(i*w,w)]
    def count(i):
        dve.drain(); dve.tensor_copy(m.DGB[:,:,:],seg(S[2],i,8)); dve.drain()
        for u in range(8):
            dve.wait_ge(m.oh_free,i*8+(u+1+r*STEPS))
            dve.tensor_tensor(m.OHL[:,u%2,:,:],iota8,m.DGB[:,:,u:u+1].to_broadcast((P,SEGS,P)),ALU.is_equal).then_inc(m.oh_rdy,1)
    with dve.Fori(0,STEPS//8) as i:
        if r==0: count(i)
        else:
            with dve.If(i<V*2): count(i)
    dve.wait_ge(m.hist_done,r+1)
    for b in range(2): dve.tensor_copy(m.Tc[:,4*b:4*b+4,:],PS[b].rearrange("p (s v) -> p s v",s=4))
    dve.drain()
    dve.tensor_reduce(m.TT[:,:],m.Tc.rearrange("p s v -> p v s"),AX.X,ALU.add).then_inc(m.tt_rdy,1)
    dve.wait_ge(m.lt_done,r+1)
    dve.tensor_tensor_scan(m.tot[:,:],m.ones[:,:],PS[3][:,P:2*P],0.0,ALU.mult,ALU.add); dve.drain()
    if r==0: block_count_dve(dve,m)
    dve.tensor_tensor(m.tot[:,:],m.tot[:,:],PS[3][:,P:2*P],ALU.subtract); dve.drain()
    dve.tensor_tensor(m.INI[:,0,:],m.tot[:,:],PS[3][:,0:P],ALU.add)
    for s in range(1,SEGS):
        dve.drain()
        last=dve.tensor_tensor(m.INI[:,s,:],m.INI[:,s-1,:],m.Tc[:,s-1,:],ALU.add)
    last.then_inc(m.ini_rdy,1)
    def rank(i):
        dve.tensor_copy(m.DGB[:,:,0:4],seg(S[2],i,4)); dve.tensor_copy(m.DGF[:,:,:],seg(S[2],i,4)); dve.drain()
        for u in range(4):
            k=i*4+u
            dve.wait_ge(m.accA,k+(1+r*(STEPS+1))); dve.wait_ge(m.accB,k+(1+r*(STEPS+1)))
            if r==0: dve.wait_ge(m.cnt_mm,k+1)
            dve.tensor_tensor(m.OHL[:,u%2,:,:],iota8,m.DGB[:,:,u:u+1].to_broadcast((P,SEGS,P)),ALU.is_equal).then_inc(m.oh_rank,1)
            for b in range(2):
                dve.wait_ge((m.accA,m.accB)[b],k+(2+r*(STEPS+1)))
                for s in range(4*b,4*b+4):
                    last=dve.scalar_tensor_tensor(out=m.junk[:,u%2,s,:],in0=m.iotab[:,:],scalar=m.DGF[:,s,u:u+1],in1=PS[b][:,(s%4)*DIG:(s%4+1)*DIG],op0=ALU.is_equal,op1=ALU.mult,accum_out=m.RKT[:,s,u:u+1])
                last.then_inc((m.exA,m.exB)[b],1)
        v=lambda t: t.rearrange("p (s k) -> p s k",s=SEGS)[:,:,bass.ds(i*4,4)]
        w=lambda t: t[:,:].rearrange("p (s k) -> p s k",s=SEGS)
        dve.tensor_scalar(m.big[:,:,:],m.DGF[:,:,:],float(DIG),OUT_OF_RANGE,ALU.is_ge,ALU.mult)
        dve.drain()
        K=m.KV[:,r,:]
        divide(dve,m.RKT[:,:,:],K,w(m.QI),w(m.QR),w(m.QT))
        dve.scalar_tensor_tensor(out=w(m.QT),in0=w(m.QR),scalar=K[:,3:4],in1=m.RKT[:,:,:],op0=ALU.mult,op1=ALU.add); dve.drain()
        dve.tensor_tensor(v(SJ[1]),w(m.QT),m.big[:,:,:],ALU.add).then_inc(m.pos_rdy,1)
    with dve.Fori(0,NI) as i:
        if r==0: rank(i)
        else:
            with dve.If(i<V*4): rank(i)
def sort_pe(pe,m,PS,r,V=None):
    if r==0: pe.wait_ge(m.const_rdy,1); pe.sem_inc(m.oh_free,2); pe.sem_inc(m.cnt_mm,2)
    if r==1: pe.wait_ge(m.pos_rdy,NI)
    for b in range(3): pe.matmul(PS[b],m.zb[:,0:P],m.zb[:,:],start=True,stop=True)
    def count(i):
        for u in range(2):
            k=i*2+u
            pe.wait_ge(m.oh_rdy,k+(1+r*STEPS))
            for b in range(2): last=pe.matmul(PS[b],m.identb[:,:],m.OHL[:,u,4*b:4*b+4,:],start=False,stop=True,skip_group_check=True)
            last.then_inc(m.oh_free,1)
    with pe.Fori(0,STEPS//2) as i:
        if r==0: count(i)
        else:
            with pe.If(i<V*8): count(i)
    for b in range(2): last=pe.matmul(PS[b],m.zb[:,0:P],m.zb[:,:],start=False,stop=True,skip_group_check=True)
    last.then_inc(m.hist_done,1)
    pe.wait_ge(m.tt_rdy,r+1)
    pe.matmul(PS[3][:,0:P],m.ltri[:,:],m.TT[:,:],start=True,stop=True)
    pe.matmul(PS[3][:,P:2*P],m.ones[:,:],m.TT[:,:],start=True,stop=True).then_inc(m.lt_done,1)
    pe.wait_ge(m.ini_rdy,r+1)
    for b in range(2): pe.matmul(PS[b],m.ident[:,:],m.INI[:,4*b:4*b+4,:],start=True,stop=True).then_inc((m.accA,m.accB)[b],1)
    def rank(i):
        for u in range(2):
            k=i*2+u
            pe.wait_ge(m.oh_rank,k+(1+r*STEPS))
            for b in range(2):
                pe.wait_ge((m.exA,m.exB)[b],k+(1+r*STEPS))
                pe.matmul(PS[b],m.identb[:,:],m.OHL[:,u,4*b:4*b+4,:],start=False,stop=True,skip_group_check=True).then_inc((m.accA,m.accB)[b],1)
            if r==0:
                pe.wait_ge(m.ohh_rdy,k+1)
                for s in range(SEGS): last=pe.matmul(PS[2][:,0:P],m.OHL[:,u,s,:],m.OHH[:,u,s,:],start=False,stop=True,skip_group_check=True)
                last.then_inc(m.cnt_mm,1)
    with pe.Fori(0,STEPS//2) as i:
        if r==0: rank(i)
        else:
            with pe.If(i<V*8): rank(i)
    pe.drain().then_inc(m.rank_done,1)

def build(nc,d,out):
    ctx=ExitStack()
    with ctx:
        m=declare_sort(nc,ctx)
        n=declare_dense(nc,ctx,m.SA,m.SB); n.UM=m.ltri[:,:]
        declare_nodes(nc,ctx,n,m.SA,m)
        for k,sh,dt in (("A1",(EDGES,1),i32),("A2",(EDGES,1),i32),("AEXP",(EDGES,4),f32),("R",(EDGES,24),f32),("CT",(P,24),f32),
                        ("T",(NODES,20),f32),("ADT",(NODES,4),f32),("TNT",(P,NODES),f32),("X3",(NODES,P),f32)):
            d[k]=nc.dram_tensor("s_"+k,sh,dt).ap()
        PSB=ctx.enter_context(nc.psum_tensor("PSB",[P,4096],f32))[:,:]
        PS=[PSB[:,512*i:512*(i+1)] for i in range(8)]
        ident=m.ident[:,:]; ones=m.ones
        block=ctx.enter_context(nc.Block())

        @block.sync
        def _(sp):
            sort_sync_loads(sp,m,d)
            sync_weights(sp,n,d)
            sort_sync_fill(sp,m,d)
            sort_sync(sp,m,d,0,None)
            V=blocks(sp,m)
            edges_sync_fill(sp,m,n,d,V)
            sort_sync(sp,m,d,1,V)
            for s in range(2): sp.wait_ge(m.scat[1][s],V*1024)
            edges_sync(sp,n,d,m.SA,m.tick_sp,d["A2"],V)
            moe_sync(sp,n,d,m.tick_sp)

        @block.gpsimd
        def _(pool):
            for q in n.rbs: pool.sem_inc(q,1)
            pool.memset(m.fill[:,:],INVALID).then_inc(m.fill_rdy,1)
            pool.memset(m.zero[:,:],0.0).then_inc(m.fill_rdy,1)
            sort_pool(pool,m,d,0,None)
            V=blocks(pool,m)
            sort_pool(pool,m,d,1,V)
            edges_pool(pool,n,d,m.tick_pool,V)
            moe_pool(pool,n,out,m.tick_pool)

        @block.vector
        def _(dve):
            for q in (m.accA,m.accB,*n.rst): dve.sem_inc(q,1)
            sort_dve_prep(dve,m)
            dve_prep(dve,n)
            dve.memset(n.IDW[:,0:1],0.0); dve.tensor_copy(n.IDW[:,1:P+1],ident)
            sort_dve(dve,m,PS,0)
            V=blocks(dve,m)
            dve.wait_ge(m.rank_done,1)
            dve.tensor_copy(m.cnt[:,:],PS[2][:,0:P])
            dve.drain().then_inc(n.sorted_,1)
            def image(b):
                l0conv_dve(dve,n,PSB,b)
                l0ffn_dve(dve,n,PSB,b,ident)
                l1conv_dve(dve,n,PSB,b)
                gat_dve(dve,n,PSB,b)
            with dve.Fori(0,BEFORE) as b: image(b)
            pos_dve(dve,n,PSB,ones[:,:],m.cnt[:,:],m)
            sort_dve(dve,m,PS,1,V)
            dve.wait_ge(m.rank_done,2)
            dve.drain().then_inc(n.sorted_,1)
            with dve.Fori(BEFORE,IMGS) as b: image(b)
            edges_prep_dve(dve,n,m.SA,V)
            edges_dve(dve,n,m.SA,V)
            carry_dve(dve,n,PSB)
            node_dve(dve,n,m.SA)
            moe_dve(dve,n,PSB)

        @block.scalar
        def _(act):
            for q in n.moe_ys: act.sem_inc(q,1)
            sort_act(act,m,n.XPAD[:,:].bitcast(bf16)[:,0:2048].rearrange("p (u s v) -> p u s v",u=2,s=SEGS))
            act.wait_ge(n.sorted_,1)
            def image(b):
                l0conv_act(act,n,PSB,b,d)
                l0ffn_act(act,n,PSB,b)
                l1conv_act(act,n,PSB,b)
                gat_act(act,n,PSB,b,d)
            with act.Fori(0,BEFORE) as b: image(b)
            act.wait_ge(n.sorted_,2)
            with act.Fori(BEFORE,IMGS) as b: image(b)
            edges_act(act,n,d,blocks(act,m))
            carry_act(act,n,d)
            node_act(act,n,m.SA)
            moe_act(act,n,PSB)

        @block.tensor
        def _(pe):
            for q in (n.s_xa,n.s_pta,n.s_cqc,n.s_sb,n.s_cxa,n.s_atc,n.moe_dv): pe.sem_inc(q,1)
            sort_pe(pe,m,PS,0)
            pe.wait_ge(n.sorted_,1)
            def image(b):
                l0conv_pe(pe,n,PSB,ident,b)
                l0ffn_pe(pe,n,PSB,ident,ones,b)
                l1conv_pe(pe,n,PSB,ident,ones,b)
                gat_pe(pe,n,PSB,ident,b)
            with pe.Fori(0,BEFORE) as b: image(b)
            pos_pe(pe,n,PSB,m.ltri[:,:],ones[:,:],m.cnt[:,:])
            pe.wait_ge(n.np_rdy,1)
            sort_pe(pe,m,PS,1,blocks(pe,m))
            pe.wait_ge(n.sorted_,2)
            with pe.Fori(BEFORE,IMGS) as b: image(b)
            carry_pe(pe,n,PSB,ident)
            moe_pe(pe,n,PSB,ones)


def shape_constants(np):
    p=np.arange(P); f=np.float32; k=np.arange(144)
    expand=np.zeros((72,9,P),f)
    for t in range(9):
        for h in range(8): expand[t*8+h,t,16*h:16*h+16]=1
    return dict(ident=np.eye(P,dtype=f), ltri=(p[:,None]<p[None,:]).astype(f), iota=np.tile(p.astype(f),(P,1)),
      PAR=((p[:,None]//16)%2==np.arange(2)[None,:]).astype(f), LM=(p[None,:]<p[:,None]).astype(f),
      INDH=((k[None,:]//12)==(p[:,None]%16)).astype(f), INDW=((k[None,:]%12)==(p[:,None]%16)).astype(f),
      HONE=((p[:,None]//16)==np.arange(8)[None,:]).astype(f), EXPN=expand)

def kernel(**inputs):
    import numpy as np
    import concourse.bacc as bacc
    from concourse.bass_utils import run_bass_kernel_spmd as run

    a=lambda k: np.asarray(inputs[k])
    arrays=dict(x=a("x").reshape(NODES,P),w_q=a("L0_conv_w_q"),w_kv=a("L0_conv_w_kv"),w_out=a("L0_conv_w_out"),
        pos_emb_h=a("L0_conv_pos_emb_h"),pos_emb_w=a("L0_conv_pos_emb_w"),wr=a("L0_ffn_wr"),br=a("L0_ffn_br"),
        w1=a("L0_ffn_w1"),w2=a("L0_ffn_w2"),b2=a("L0_ffn_b2"),b1T=a("L0_ffn_b1").reshape(4,P).T,
        WqkvT=a("L1_conv_Wqkv").T,WprojT=a("L1_conv_Wproj").T,bproj=a("L1_conv_bproj"),
        W_gat=a("L1_ffn_W_gat"),att_src=a("L1_ffn_att_src"),att_dst=a("L1_ffn_att_dst"),b_gat=a("L1_ffn_b_gat"),
        gamma=a("L1_ffn_ln_gamma"),beta=a("L1_ffn_ln_beta"),W1=a("L1_ffn_W1"),W2=a("L1_ffn_W2"),
        b1mT=a("L1_ffn_b1").reshape(8,P).T,b2m=a("L1_ffn_b2"),edges=a("L1_ffn_edge_index"))
    arrays.update(shape_constants(np))
    nc=bacc.Bacc("TRN2",target_bir_lowering=False,num_devices=1)
    feed,d={},{}
    for k,v in arrays.items():
        v=np.ascontiguousarray(v)
        feed["in_"+k]=v
        d[k]=nc.dram_tensor("in_"+k,v.shape,mybir.dt.from_np(v.dtype),kind="ExternalInput").ap()
    out=nc.dram_tensor("out_0",(NODES,P),f32,kind="ExternalOutput").ap()
    build(nc,d,out)
    r=run(nc,[feed],core_ids=[0])
    return np.asarray(r.results[0]["out_0"]).reshape(4,64,64,P)
```
